# Optimizing a Trainium2 kernel written in Bass

```python
import numpy as np
import jax
import jax.numpy as jnp

def _softmax(x, axis=-1):
    return jax.nn.softmax(x, axis=axis)

def _gelu(x):
    return jax.nn.gelu(x, approximate=True)

def _silu(x):
    return jax.nn.silu(x)

def _sigmoid(x):
    return jax.nn.sigmoid(x)

def _layernorm(x, axis=-1, eps=1e-05):
    m = jnp.mean(x, axis=axis, keepdims=True)
    v = jnp.var(x, axis=axis, keepdims=True)
    return (x - m) / jnp.sqrt(v + eps)

def _scatter_add(tgt, idx, src, axis=0):
    return tgt.at[idx].add(src)

def _segment_sum(src, seg, n):
    return jax.ops.segment_sum(src, seg, n)
kernel_name = 'mk_hybrid_d1_jaxref_r8_628751'

def setup_inputs(seed: int=0):
    np.random.seed(seed)
    _w = jnp.asarray

    def _L0_attn_a_setup():
        import jax, jax.numpy as jnp
        import numpy as np
        DIM = 128
        BATCH = 8
        SEQ = 256
        key = jax.random.key(seed)
        ks = jax.random.split(key, 10)
        s = 0.02
        return {'x': jax.random.normal(ks[0], (BATCH, SEQ, DIM), dtype=jnp.float32), 'Wq': jax.random.normal(ks[1], (DIM, DIM), dtype=jnp.float32) * s, 'bq': jnp.zeros((DIM,), jnp.float32), 'Wk': jax.random.normal(ks[2], (DIM, DIM), dtype=jnp.float32) * s, 'bk': jnp.zeros((DIM,), jnp.float32), 'Wv': jax.random.normal(ks[3], (DIM, DIM), dtype=jnp.float32) * s, 'bv': jnp.zeros((DIM,), jnp.float32), 'Wo': jax.random.normal(ks[4], (DIM, DIM), dtype=jnp.float32) * s, 'bo': jnp.zeros((DIM,), jnp.float32), 'decay_param': jnp.asarray(0.0, jnp.float32)}
    _L0_attn_a_in = _L0_attn_a_setup()

    def _L0_attn_b_setup():
        import jax, jax.numpy as jnp
        import numpy as np
        HIDDEN = 128
        HEADS = 16
        HEAD_DIM = HIDDEN // HEADS
        B, S = (4, 256)
        key = jax.random.key(seed)
        ks = jax.random.split(key, 10)
        scale = 1.0 / np.sqrt(HIDDEN)

        def lin(k):
            return jax.random.uniform(k, (HIDDEN, HIDDEN), jnp.float32, -scale, scale)
        return {'x': jax.random.normal(ks[0], (B, S, HIDDEN), jnp.float32), 'Wq': lin(ks[1]), 'bq': jnp.zeros((HIDDEN,), jnp.float32), 'Wk': lin(ks[2]), 'bk': jnp.zeros((HIDDEN,), jnp.float32), 'Wv': lin(ks[3]), 'bv': jnp.zeros((HIDDEN,), jnp.float32), 'Wo': lin(ks[4]), 'bo': jnp.zeros((HIDDEN,), jnp.float32), 'head_mask': jnp.ones((HEADS,), jnp.float32)}
    _L0_attn_b_in = _L0_attn_b_setup()

    def _L0_ffn_setup():
        import jax, jax.numpy as jnp
        import numpy as np
        E, D, F = (8, 128, 512)
        LN_EPS = 1e-05
        key = jax.random.key(seed)
        k = jax.random.split(key, 8)
        x = jax.random.normal(k[0], (4, 256, D), jnp.float32)
        centroids = jax.random.normal(k[1], (E, D), jnp.float32) * 0.1
        ln_g = jnp.ones((E, D), jnp.float32)
        ln_b = jnp.zeros((E, D), jnp.float32)
        w1 = jax.random.normal(k[2], (E, F, D), jnp.float32) * (1.0 / np.sqrt(D))
        b1 = jnp.zeros((E, F), jnp.float32)
        w2 = jax.random.normal(k[3], (E, D, F), jnp.float32) * (1.0 / np.sqrt(F))
        b2 = jnp.zeros((E, D), jnp.float32)
        return {'input_features': x, 'centroids': centroids, 'ln_g': ln_g, 'ln_b': ln_b, 'w1': w1, 'b1': b1, 'w2': w2, 'b2': b2}
    _L0_ffn_in = _L0_ffn_setup()
    _d = {'L0_attn_a_x': _L0_attn_a_in['x'], 'L0_attn_a_Wq': _L0_attn_a_in['Wq'], 'L0_attn_a_bq': _L0_attn_a_in['bq'], 'L0_attn_a_Wk': _L0_attn_a_in['Wk'], 'L0_attn_a_bk': _L0_attn_a_in['bk'], 'L0_attn_a_Wv': _L0_attn_a_in['Wv'], 'L0_attn_a_bv': _L0_attn_a_in['bv'], 'L0_attn_a_Wo': _L0_attn_a_in['Wo'], 'L0_attn_a_bo': _L0_attn_a_in['bo'], 'L0_attn_a_decay_param': _L0_attn_a_in['decay_param'], 'L0_attn_b_Wq': _L0_attn_b_in['Wq'], 'L0_attn_b_bq': _L0_attn_b_in['bq'], 'L0_attn_b_Wk': _L0_attn_b_in['Wk'], 'L0_attn_b_bk': _L0_attn_b_in['bk'], 'L0_attn_b_Wv': _L0_attn_b_in['Wv'], 'L0_attn_b_bv': _L0_attn_b_in['bv'], 'L0_attn_b_Wo': _L0_attn_b_in['Wo'], 'L0_attn_b_bo': _L0_attn_b_in['bo'], 'L0_attn_b_head_mask': _L0_attn_b_in['head_mask'], 'L0_ffn_centroids': _L0_ffn_in['centroids'], 'L0_ffn_ln_g': _L0_ffn_in['ln_g'], 'L0_ffn_ln_b': _L0_ffn_in['ln_b'], 'L0_ffn_w1': _L0_ffn_in['w1'], 'L0_ffn_b1': _L0_ffn_in['b1'], 'L0_ffn_w2': _L0_ffn_in['w2'], 'L0_ffn_b2': _L0_ffn_in['b2']}
    _x0 = _d['L0_attn_a_x']
    _d['L0_attn_a_x'] = jax.random.normal(jax.random.fold_in(jax.random.key(seed), 1), (8, 512, 128), dtype=_x0.dtype)
    del _x0
    return _d

def reference(L0_attn_a_x, L0_attn_a_Wq, L0_attn_a_bq, L0_attn_a_Wk, L0_attn_a_bk, L0_attn_a_Wv, L0_attn_a_bv, L0_attn_a_Wo, L0_attn_a_bo, L0_attn_a_decay_param, L0_attn_b_Wq, L0_attn_b_bq, L0_attn_b_Wk, L0_attn_b_bk, L0_attn_b_Wv, L0_attn_b_bv, L0_attn_b_Wo, L0_attn_b_bo, L0_attn_b_head_mask, L0_ffn_centroids, L0_ffn_ln_g, L0_ffn_ln_b, L0_ffn_w1, L0_ffn_b1, L0_ffn_w2, L0_ffn_b2):

    def _L0_attn_a_ref(x, Wq, bq, Wk, bk, Wv, bv, Wo, bo, decay_param):
        import jax, jax.numpy as jnp
        import numpy as np
        DIM = 128
        BATCH = 8
        SEQ = 256
        q = x @ Wq + bq
        k = jax.nn.elu(x @ Wk + bk) + 1.0
        v = x @ Wv + bv
        decay = jax.nn.sigmoid(decay_param)
        B, S, D = x.shape

        def step(mem, qkv):
            q_t, k_t, v_t = qkv
            read = jnp.einsum('bd,bde->be', q_t, mem)
            mem = decay * mem + k_t[:, :, None] * v_t[:, None, :]
            return (mem, read)
        mem0 = jnp.zeros((B, D, D), x.dtype)
        _, outs = jax.lax.scan(step, mem0, (q.transpose(1, 0, 2), k.transpose(1, 0, 2), v.transpose(1, 0, 2)))
        out = outs.transpose(1, 0, 2)
        return out @ Wo + bo

    def _L0_attn_b_ref(x, Wq, bq, Wk, bk, Wv, bv, Wo, bo, head_mask):
        import jax, jax.numpy as jnp
        import numpy as np
        HIDDEN = 128
        HEADS = 16
        HEAD_DIM = HIDDEN // HEADS
        B, S = (4, 256)
        b, s, _ = x.shape
        q = (x @ Wq.T + bq).reshape(b, s, HEADS, HEAD_DIM)
        k = (x @ Wk.T + bk).reshape(b, s, HEADS, HEAD_DIM)
        v = (x @ Wv.T + bv).reshape(b, s, HEADS, HEAD_DIM)
        attn = jnp.einsum('bqhd,bkhd->bhqk', q, k) / np.sqrt(HEAD_DIM).astype(np.float32)
        attn = jax.nn.softmax(attn, axis=-1)
        attn = attn * head_mask[None, :, None, None]
        out = jnp.einsum('bhqk,bkhd->bqhd', attn, v).reshape(b, s, HIDDEN)
        return out @ Wo.T + bo

    def _L0_ffn_ref(input_features, centroids, ln_g, ln_b, w1, b1, w2, b2):
        import jax, jax.numpy as jnp
        import numpy as np
        E, D, F = (8, 128, 512)
        LN_EPS = 1e-05
        x = input_features.reshape(-1, D)
        aff = jax.lax.stop_gradient(x) @ centroids.T
        assign = jnp.argmax(aff, axis=1)
        onehot = jax.nn.one_hot(assign, E, dtype=x.dtype)
        mu = jnp.mean(x, axis=-1, keepdims=True)
        var = jnp.mean((x - mu) ** 2, axis=-1, keepdims=True)
        xhat = (x - mu) * jax.lax.rsqrt(var + LN_EPS)
        xn = xhat[None, :, :] * ln_g[:, None, :] + ln_b[:, None, :]
        h = jax.nn.relu(jnp.einsum('etd,efd->etf', xn, w1) + b1[:, None, :])
        y = x[None, :, :] + jnp.einsum('etf,edf->etd', h, w2) + b2[:, None, :]
        alpha = jax.nn.sigmoid(x @ centroids.T)
        a = alpha.T[:, :, None]
        gated = a * y + (1.0 - a) * x[None, :, :]
        out = jnp.einsum('te,etd->td', onehot, gated)
        return out.reshape(input_features.shape)
    x = L0_attn_a_x
    x = x + _L0_attn_a_ref(_layernorm(x, axis=-1), L0_attn_a_Wq, L0_attn_a_bq, L0_attn_a_Wk, L0_attn_a_bk, L0_attn_a_Wv, L0_attn_a_bv, L0_attn_a_Wo, L0_attn_a_bo, L0_attn_a_decay_param)
    x = x + _L0_ffn_ref(_layernorm(x, axis=-1), L0_ffn_centroids, L0_ffn_ln_g, L0_ffn_ln_b, L0_ffn_w1, L0_ffn_b1, L0_ffn_w2, L0_ffn_b2)
    x = x + _L0_attn_b_ref(_layernorm(x, axis=-1), L0_attn_b_Wq, L0_attn_b_bq, L0_attn_b_Wk, L0_attn_b_bk, L0_attn_b_Wv, L0_attn_b_bv, L0_attn_b_Wo, L0_attn_b_bo, L0_attn_b_head_mask)
    x = x + _L0_ffn_ref(_layernorm(x, axis=-1), L0_ffn_centroids, L0_ffn_ln_g, L0_ffn_ln_b, L0_ffn_w1, L0_ffn_b1, L0_ffn_w2, L0_ffn_b2)
    return x

_drawn_inputs = setup_inputs


def setup_inputs(seed=0):
    import zlib

    import numpy as np

    out = dict(_drawn_inputs(seed))
    spreads = {'L0_attn_a_bq': (0.0, 0.1),
     'L0_attn_a_bk': (0.0, 0.1),
     'L0_attn_a_bv': (0.0, 0.1),
     'L0_attn_a_bo': (0.0, 0.1),
     'L0_attn_b_bq': (0.0, 0.8),
     'L0_attn_b_bk': (0.0, 0.8),
     'L0_attn_b_bv': (0.0, 0.1),
     'L0_attn_b_bo': (0.0, 0.1),
     'L0_ffn_ln_g': (1.0, 0.2),
     'L0_ffn_ln_b': (0.0, 0.1),
     'L0_ffn_b1': (0.0, 0.1),
     'L0_ffn_b2': (0.0, 0.1)}
    factors = {'L0_attn_b_Wq': 3.736, 'L0_attn_b_Wk': 3.45}
    for name, (base, spread) in spreads.items():
        noise = np.random.default_rng([zlib.crc32(name.encode()), seed]).standard_normal(out[name].shape)
        drawn = base * np.exp(spread * noise) if base else spread * noise
        out[name] = jnp.asarray(drawn.astype(out[name].dtype))
    for name, factor in factors.items():
        out[name] = (out[name] * factor).astype(out[name].dtype)
    return out
```

```python
import concourse.bass as bass
from concourse import mybir
from contextlib import ExitStack

F32 = mybir.dt.float32
F32R = mybir.dt.float32r
I32 = mybir.dt.int32
ALU = mybir.AluOpType
ACT = mybir.ActivationFunctionType
AX = mybir.AxisListType

D = 128
B, S = 8, 512
C = S // 128
NT = B * C
E, F = 8, 512
FC = F // 128
TILES = NT + E - 1
H, HD = 16, 8
G = 4
SETS = H // G
AUG = 32
EPS = 1e-5
SCALE = 1.0 / float(HD) ** 0.5


def ds(i, n):
    return bass.ds(i, n)


def wait(eng, sem, per, b):
    if isinstance(b, int) and b < 0:
        return
    eng.wait_ge(sem, per * (b + 1))


def at_least(eng, sem, value):
    if isinstance(value, int) and value <= 0:
        return
    eng.wait_ge(sem, value)


def apart(eng, sem, value, passed):
    if isinstance(value, int) and value <= 0:
        return
    eng.wait_ge(sem, value)
    eng.sem_inc(passed, 1)


class Round:

    def __init__(self, b, half, par):
        self.b, self.half, self.par = b, half, par

    def __add__(self, k):
        b = self.b + k
        return Round(b, self.half + (self.par + k) // 2, (self.par + k) % 2)

    def within(self, n):
        return not isinstance(self.b, int) or 0 <= self.b < n


def rounds(eng, first, loop_from, loop_to, last, body):
    def at(t):
        return Round(t, t // 2, t % 2)
    for t in range(first, loop_from):
        body(at(t))
    if loop_to > loop_from:
        turns = (loop_to - loop_from) // 2
        lo = loop_from // 2
        assert loop_from + 2 * turns == loop_to
        with eng.Fori(lo, lo + turns) as i:
            for h in range(2):
                k = loop_from % 2 + h
                body(Round(2 * i + k, i + k // 2, k % 2))
    for t in range(loop_to, last + 1):
        body(at(t))


def hybrid(nc, x_in, Wq_a, bq_a, Wk_a, bk_a, Wv_a, bv_a, Wo_a, bo_a, decay,
           Wq_b, bq_b, Wk_b, bk_b, Wv_b, bv_b, Wo_b, bo_b, head_mask,
           cent, ln_g, ln_b, w1, b1, w2, b2, consts, tile_ids, out, dbg=None, upto=99):
    ctx = ExitStack()
    with ctx:
        def sb(name, shape, dt=F32, c=ctx):
            return c.enter_context(nc.sbuf_tensor(name, shape, dt))

        early = ExitStack()
        held = []

        def sem(name):
            if held is None:
                return ctx.enter_context(nc.semaphore(name))
            held.append(early.enter_context(nc.semaphore(name)))
            return held[-1]

        PS = ctx.enter_context(nc.psum_tensor("PS", [128, 8, 512], F32))
        bank = [PS[:, i, :] for i in range(8)]
        quad = [b_.rearrange("p (c d) -> p c d", c=C) for b_ in bank]

        sorted_x = nc.dram_tensor("sorted_x", [TILES * 128, D], F32, kind="Internal").ap()
        sorted_y = nc.dram_tensor("sorted_y", [TILES * 128, D], F32, kind="Internal").ap()

        dve_passed, pool_passed, sp_passed = (ctx.enter_context(nc.semaphore(n))
                                              for n in ("dve_passed", "pool_passed", "sp_passed"))
        X = sb("X", [128, NT, D])
        XH = sb("XH", [128, NT, D])
        AFF = sb("AFF", [128, NT, E])
        POS = sb("POS", [128, NT], I32)
        ALPHA = sb("ALPHA", [128, NT])
        TE = sb("TE", [1, TILES], I32)
        NB1 = sb("NB1", [128, E, FC])
        C2 = sb("C2", [128, E, D])
        CON = sb("CON", [128, 1080])
        ID = CON[:, 0:128]
        LOW = CON[:, 128:256]
        IMP = CON[:, 256:385]
        IMP0 = CON[:, 385:514]
        CODE = CON[:, 514:522]
        RESET = CON[:, 522:778]
        STEPS = CON[:, 778:810]
        ROW39 = CON[:, 810:849]
        EPS1 = CON[:, 850:854]
        MHALF = CON[:, 854:858]
        ONES = sb("ONES", [128, 128])
        COL = sb("COL", [128, 61])
        LNG, LNB, B1T, CENT = COL[:, 1:9], COL[:, 9:17], COL[:, 17:49], COL[:, 49:57]
        MASKH, BQA, BKA, BQB, BKB = (COL[:, k:k + 1] for k in (0, 57, 58, 59, 60))
        WA = sb("WA", [128, 4, D])
        WB = sb("WB", [128, 4, D])
        REP = sb("REP", [128, 4, D])
        DEC = sb("DEC", [128, 129])
        DROW = sb("DROW", [128, 129])
        BVA, BOA, BVB, BOB = (REP[:, k, :] for k in range(4))

        weights = ExitStack()
        W1T = sb("W1T", [128, E, F], c=weights)
        W2T = sb("W2T", [128, E, FC, D], c=weights)
        w1_dram = nc.dram_tensor("w1_kept", [128, E * F], F32, kind="Internal").ap()
        w2_dram = nc.dram_tensor("w2_kept", [128, E * F], F32, kind="Internal").ap()

        with ExitStack() as c0:
            W1N = sb("W1N", [128, 2, FC, D], c=c0)
            W2N = sb("W2N", [128, 2, F], c=c0)
            W1U = sb("W1U", [128, 2, F], c=c0)
            B1E = sb("B1E", [128, E, FC], c=c0)
            B1R = sb("B1R", [128, 2, FC, D], c=c0)
            B2R = sb("B2R", [128, E, D], c=c0)
            SM = sb("SMALL", [61, D], c=c0)
            HM = sb("HM", [1, H], c=c0)
            u_mask, u_maskv = sem("u_mask"), sem("u_maskv")
            WBN = sb("WBN", [128, 4, D], c=c0)
            DT = sb("DT", [128, 4], c=c0)
            u_con, u_small, u_w, u_rep, u_b2 = (sem("u_" + n) for n in ("con", "small", "w", "rep", "b2"))
            u_w1n = [sem(f"u_w1n{i}") for i in range(2)]
            u_w2n = [sem(f"u_w2n{i}") for i in range(2)]
            u_col, u_colv, u_wbt, u_wbv = sem("u_col"), sem("u_colv"), sem("u_wbt"), sem("u_wbv")
            u_w1t, u_w1u, u_w1g, u_w2t, u_w2v = (sem("u_" + n) for n in ("w1t", "w1u", "w1g", "w2t", "w2v"))
            u_b1, u_b1e, u_b1r, u_c2, u_c2v = (sem("u_" + n) for n in ("b1", "b1e", "b1r", "c2", "c2v"))
            u_dec, u_e, u_ones, u_zero, u_xz = (sem("u_" + n) for n in ("dec", "e", "ones", "zero", "xz"))
            ZERO = sb("ZERO", [128, D], c=c0)
            block = c0.enter_context(nc.Block())

            @block.sync
            def _(sp):
                sp.dma_start(CON[:, :], consts).then_inc(u_con, 16)
                sp.dma_start(HM[:, :], head_mask[None, :]).then_inc(u_mask, 16)
                rows = [(ln_g, 1, 9), (ln_b, 9, 17), (b1.rearrange("e (c f) -> (e c) f", c=FC), 17, 49),
                        (cent, 49, 57), (bq_a[None, :], 57, 58), (bk_a[None, :], 58, 59),
                        ]
                for src, a, z in rows:
                    sp.dma_start(SM[a:z, :], src).then_inc(u_small, 16)
                with nc.allow_non_contiguous_dma(reason="256 numbers"):
                    for src, a in ((bq_b, 59), (bk_b, 60)):
                        sp.dma_start(SM[a:a + 1, :].rearrange("o (x s) -> o x s", s=SETS),
                                     src[None, :].rearrange("o (s x) -> o x s", s=SETS)).then_inc(u_small, 16)
                for k, w in enumerate((Wq_b, Wk_b, Wv_b, Wo_b)):
                    sp.dma_start(WBN[:, k, :], w).then_inc(u_w, 16)

                def load(r):
                    wait(sp, u_w1t, 1, r.b - 2)
                    sp.dma_start(W1N[:, r.par, :, :],
                                 w1[ds(r.b, 1), :, :].rearrange("e (c p) d -> p (e c) d", p=128)
                                 ).then_inc(u_w1n[r.par], 16)
                    wait(sp, u_w2t, 1, r.b - 2)
                    sp.dma_start(W2N[:, r.par, :],
                                 w2[ds(r.b, 1), :, :].rearrange("e d f -> (e d) f")).then_inc(u_w2n[r.par], 16)
                rounds(sp, 0, 2, 8, 7, load)
                sp.wait_ge(u_zero, 1)
                sp.dma_start(sorted_x.rearrange("(t p) d -> p t d", p=128),
                             ZERO[:, :][:, None, :].broadcast_to([128, TILES, D])).then_inc(u_xz, 16)
                sp.wait_ge(u_xz, 16)

            @block.scalar
            def _(act):
                for k, w in enumerate((Wq_a, Wk_a, Wv_a, Wo_a)):
                    act.dma_start(WA[:, k, :], w).then_inc(u_w, 16)
                for k, v in enumerate((bv_a, bo_a, bv_b, bo_b)):
                    act.dma_start(REP[:, k, :], v[None, :].broadcast_to([128, D])).then_inc(u_rep, 16)
                act.dma_start(B2R[:, :, :], b2[None, :, :].broadcast_to([128, E, D])).then_inc(u_b2, 16)
                act.dma_start(DT[:, 0:1], decay[None, :].broadcast_to([128, 1])).then_inc(u_rep, 16)
                act.wait_ge(u_rep, 80)
                nc.scalar.activation(DT[:, 1:2], DT[:, 0:1], ACT.Exp, scale=-1.0).then_inc(u_e, 1)
                act.wait_ge(u_wbt, 1)
                for k in range(2):
                    nc.scalar.copy(WB[:, k, :].rearrange("p (g d s) -> p g s d", g=G, s=SETS),
                                   quad[1][:, k, :].rearrange("p (s g d) -> p g s d", g=G, s=SETS))
                nc.scalar.copy(WB[:, 2, :], quad[1][:, 2, :]).then_inc(u_wbv, 1)
                act.wait_ge(u_colv, 1)
                nc.scalar.mul(WB[:, 3, :], quad[1][:, 3, :], MASKH).then_inc(u_wbv, 1)

                def take(r):
                    act.wait_ge(u_w1t, r.b + 1)
                    wait(act, u_b1, 1, r.b - 2)
                    wait(act, u_w1g, 1, r.b - 2)
                    nc.scalar.copy(W1U[:, r.par, :], bank[r.par][:, :]).then_inc(u_w1u, 1)
                    act.wait_ge(u_w2t, r.b + 1)
                    nc.scalar.copy(W2T[:, ds(r.b, 1), :, :].rearrange("p e c d -> p (e c) d"),
                                   quad[2 + r.par]).then_inc(u_w2v, 1)
                rounds(act, 0, 2, 8, 7, take)

            @block.gpsimd
            def _(pool):
                nc.gpsimd.memset(ONES[:, :], 1.0).then_inc(u_ones, 1)
                pool.wait_ge(u_mask, 16)
                nc.gpsimd.tensor_copy(SM[0:1, :].rearrange("o (h d) -> o h d", h=H),
                                      HM[:, :, None].broadcast_to([1, H, HD])).then_inc(u_maskv, 1)
                nc.gpsimd.memset(ZERO[:, :], 0.0).then_inc(u_zero, 1)

            @block.vector
            def _(dve):
                dve.wait_ge(u_col, 1)
                nc.vector.tensor_copy(COL[:, :], bank[0][:, 0:61]).then_inc(u_colv, 1)
                dve.wait_ge(u_e, 1)
                nc.vector.tensor_scalar_add(DT[:, 2:3], DT[:, 1:2], 1.0).then_inc(u_dec, 1)
                dve.wait_ge(u_dec, 1)
                nc.vector.reciprocal(DT[:, 3:4], DT[:, 2:3]).then_inc(u_dec, 1)
                dve.wait_ge(u_dec, 2)
                dve.wait_ge(u_con, 16)
                decays = DT[:, 3:4].broadcast_to([128, 129])
                nc.vector.tensor_tensor_scan(DEC[:, :], decays, IMP, 0.0, ALU.mult, ALU.add)
                nc.vector.tensor_tensor_scan(DROW[:, :], decays, IMP0, 0.0, ALU.mult, ALU.add).then_inc(u_dec, 1)
                dve.wait_ge(u_b2, 16)

                def fold(r):
                    dve.wait_ge(u_w1u, r.b + 1)
                    dve.wait_ge(u_colv, 1)
                    nc.vector.tensor_scalar(W1T[:, ds(r.b, 1), :].rearrange("p e f -> p (e f)"),
                                            W1U[:, r.par, :], LNG[:, ds(r.b, 1)], None,
                                            ALU.mult).then_inc(u_w1g, 1)
                    dve.wait_ge(u_b1, r.b + 1)
                    b1e = B1E[:, ds(r.b, 1), :].rearrange("p e c -> p (e c)")
                    nc.vector.tensor_tensor(b1e, bank[4 + r.par][:, 0:FC], B1T[:, ds(FC * r.b, FC)],
                                            ALU.add).then_inc(u_b1e, 1)
                    dve.wait_ge(u_b1e, r.b + 1)
                    apart(dve, u_c2, r.b - 1, dve_passed)
                    nc.vector.tensor_copy(B1R[:, r.par, :, :],
                                          b1e[:, :, None].broadcast_to([128, FC, D])).then_inc(u_b1r, 1)
                    nc.vector.tensor_scalar(NB1[:, ds(r.b, 1), :].rearrange("p e c -> p (e c)"), b1e, -1.0, None,
                                            ALU.mult)
                    dve.wait_ge(u_c2, r.b + 1)
                    nc.vector.tensor_tensor(C2[:, ds(r.b, 1), :].rearrange("p e d -> p (e d)"),
                                            bank[6 + r.par][:, 0:D],
                                            B2R[:, ds(r.b, 1), :].rearrange("p e d -> p (e d)"),
                                            ALU.add).then_inc(u_c2v, 1)
                rounds(dve, 0, 2, 8, 7, fold)

            @block.tensor
            def _(pe):
                pe.wait_ge(u_con, 16)
                pe.wait_ge(u_small, 128)
                pe.wait_ge(u_maskv, 1)
                nc.tensor.transpose(bank[0][:, 0:61], SM[:, :], ID[0:61, 0:61]).then_inc(u_col, 1)
                pe.wait_ge(u_w, 128)
                for k in range(4):
                    m = nc.tensor.transpose(quad[1][:, k, :], WBN[:, k, :], ID)
                m.then_inc(u_wbt, 1)
                pe.wait_ge(u_colv, 1)
                pe.wait_ge(u_wbv, 2)
                pe.wait_ge(u_ones, 1)

                def turn(r):
                    pe.wait_ge(u_w1n[r.par], 16 * (r.half + 1))
                    wait(pe, u_w1u, 1, r.b - 2)
                    for k in range(FC):
                        m = nc.tensor.transpose(bank[r.par][:, 128 * k:128 * k + 128], W1N[:, r.par, k, :], ID)
                    m.then_inc(u_w1t, 1)
                    pe.wait_ge(u_w2n[r.par], 16 * (r.half + 1))
                    wait(pe, u_w2v, 1, r.b - 2)
                    for k in range(FC):
                        m = nc.tensor.transpose(quad[2 + r.par][:, k, :],
                                                W2N[:, r.par, 128 * k:128 * k + 128], ID)
                    m.then_inc(u_w2t, 1)
                    pe.wait_ge(u_w1u, r.b + 1)
                    wait(pe, u_b1e, 1, r.b - 2)
                    for k in range(FC):
                        m = nc.tensor.matmul(bank[4 + r.par][:, k:k + 1], W1U[:, r.par, 128 * k:128 * k + 128],
                                             LNB[:, ds(r.b, 1)], start=True, stop=True)
                    m.then_inc(u_b1, 1)
                    pe.wait_ge(u_b1r, r.b + 1)
                    pe.wait_ge(u_w2v, r.b + 1)
                    wait(pe, u_c2v, 1, r.b - 2)
                    for k in range(FC):
                        m = nc.tensor.matmul(bank[6 + r.par][:, 0:D], B1R[:, r.par, k, :],
                                             W2T[:, ds(r.b, 1), k, :].rearrange("p e d -> p (e d)"),
                                             start=(k == 0), stop=(k == FC - 1))
                    m.then_inc(u_c2, 1)
                rounds(pe, 0, 2, 8, 7, turn)

        with ExitStack() as c1:
            st = [sb(f"a_st{i}", [128, C, 6], c=c1) for i in range(2)]
            mv = [sb(f"a_mv{i}", [128, C, 2], c=c1) for i in range(2)]
            st1 = [sb(f"a_st1{i}", [128, C, 6], c=c1) for i in range(2)]
            mv1 = [sb(f"a_mv1{i}", [128, C, 2], c=c1) for i in range(2)]
            tmp = [sb(f"a_tmp{i}", [128, 8, C], c=c1) for i in range(2)]
            U = [sb(f"a_U{i}", [128, C, D], c=c1) for i in range(2)]
            UT = [sb(f"a_UT{i}", [128, S], c=c1) for i in range(2)]
            QT = [sb(f"a_QT{i}", [128, S], c=c1) for i in range(2)]
            QD = [sb(f"a_QD{i}", [128, C, 128], c=c1) for i in range(2)]
            KE = [sb(f"a_KE{i}", [128, S], c=c1) for i in range(2)]
            KR = [sb(f"a_KR{i}", [128, S], c=c1) for i in range(2)]
            KT = [sb(f"a_KT{i}", [128, S], c=c1) for i in range(2)]
            V = [sb(f"a_V{i}", [128, C, D], c=c1) for i in range(2)]
            KP = [sb(f"a_KP{i}", [128, C, D], c=c1) for i in range(2)]
            SM_ = [sb(f"a_SM{i}", [128, C, 128], c=c1) for i in range(2)]
            MEM = [sb(f"a_MEM{i}", [128, C - 1, D], c=c1) for i in range(2)]
            RT = [sb(f"a_RT{i}", [128, S], c=c1) for i in range(2)]
            U1 = [sb(f"a_U1{i}", [128, C, D], c=c1) for i in range(2)]
            U1T = [sb(f"a_U1T{i}", [128, S], c=c1) for i in range(2)]
            x_here = [sem(f"a_x_here{i}") for i in range(2)]
            (stats, aggr, veps, rstd, u_done, xbo, uT, uTv, q_mm, qv, qd, k_mm, ke, kr, kt, v_mm, vv,
             s_mm, sm, kT_mm, kp, U_mm, mem, r_mm, rtv, o_mm, x1, stats1, aggr1, chain1, rstd1, u1, base,
             u1T_mm, u1Tv, aff_mm, affv) = (sem("a_" + n) for n in (
                 "stats aggr veps rstd u xbo uT uTv q qv qd k ke kr kt v vv s sm kT kp U mem r rtv o x1 "
                 "stats1 aggr1 chain1 rstd1 u1 base u1T u1Tv aff affv").split())
            block = c1.enter_context(nc.Block())
            LO, HI, END = 3, 7, 9

            @block.sync
            def _(sp):
                def load(r):
                    wait(sp, x_here[r.par], 16, r.half - 1)
                    sp.dma_start(X[:, ds(C * r.b, C), :],
                                 x_in[ds(r.b, 1), :, :].rearrange("o (c p) d -> p (o c) d", p=128)
                                 ).then_inc(x_here[r.par], 16)
                rounds(sp, 0, 2, 8, 7, load)

            @block.vector
            def _(dve):
                def xs(r, c):
                    return X[:, ds(C * r.b + c, 1), :].rearrange("p o d -> p (o d)")

                def input_stats(r):
                    apart(dve, x_here[r.par], 16 * (r.half + 1), dve_passed)
                    for c in range(C):
                        i = nc.vector.bn_stats(st[r.par][:, c, :], xs(r, c))
                    i.then_inc(stats, 1)
                    dve.wait_ge(stats, r.b + 1)
                    apart(dve, rstd, r.b - 1, dve_passed)
                    for c in range(C):
                        i = nc.vector.bn_aggr(mv[r.par][:, c, :], st[r.par][:, c, :])
                    i.then_inc(aggr, 1)

                def normalise(r):
                    dve.wait_ge(rstd, r.b + 1)
                    wait(dve, uT, 1, r.b - 2)
                    for c in range(C):
                        i = nc.vector.tensor_scalar(U[r.par][:, c, :], xs(r, c), mv[r.par][:, c, 0:1],
                                                    tmp[r.par][:, 0, c:c + 1], ALU.subtract, ALU.mult)
                    i.then_inc(u_done, 1)

                def residual(r):
                    dve.wait_ge(o_mm, r.b + 1)
                    dve.wait_ge(xbo, r.b + 1)
                    nc.vector.tensor_tensor(X[:, ds(C * r.b, C), :], quad[7], X[:, ds(C * r.b, C), :],
                                            ALU.add).then_inc(x1, 1)
                    apart(dve, x1, r.b + 1, dve_passed)
                    for c in range(C):
                        i = nc.vector.bn_stats(st1[r.par][:, c, :], xs(r, c))
                    i.then_inc(stats1, 1)
                    dve.wait_ge(stats1, r.b + 1)
                    apart(dve, rstd1, r.b, dve_passed)
                    for c in range(C):
                        i = nc.vector.bn_aggr(mv1[r.par][:, c, :], st1[r.par][:, c, :])
                    i.then_inc(aggr1, 1)

                def ffn_inputs(r):
                    dve.wait_ge(rstd1, r.b + 1)
                    wait(dve, u1T_mm, 1, r.b - 1)
                    wait(dve, base, 1, r.b - 1)
                    for c in range(C):
                        i = nc.vector.tensor_scalar(U1[r.par][:, c, :], xs(r, c), mv1[r.par][:, c, 0:1],
                                                    tmp[r.par][:, 2, c:c + 1], ALU.subtract, ALU.mult)
                        nc.vector.tensor_scalar(XH[:, ds(C * r.b + c, 1), :].rearrange("p o d -> p (o d)"),
                                                xs(r, c), mv1[r.par][:, c, 0:1],
                                                tmp[r.par][:, 7, c:c + 1], ALU.subtract, ALU.mult
                                                ).then_inc(u1, 1)

                def step(t):
                    if t.within(B):
                        normalise(t)
                    if (t + -2).within(B):
                        residual(t + -2)
                    if (t + -1).within(B):
                        r = t + -1
                        dve.wait_ge(s_mm, r.b + 1)
                        wait(dve, r_mm, 1, r.b - 2)
                        nc.vector.tensor_tensor(SM_[r.par][:, :, :], quad[4],
                                                DEC[:, None, 0:128].broadcast_to([128, C, 128]),
                                                ALU.mult).then_inc(sm, 1)
                        dve.wait_ge(U_mm, r.b + 1)
                        for c in range(C - 1):
                            if c == 0:
                                i = nc.vector.tensor_copy(MEM[r.par][:, 0, :], quad[6][:, 0, :])
                            else:
                                dve.wait_ge(mem, (C - 1) * r.b + c)
                                i = nc.vector.scalar_tensor_tensor(
                                    MEM[r.par][:, c, :], MEM[r.par][:, c - 1, :], DROW[:, 128:129],
                                    quad[6][:, c, :], ALU.mult, ALU.add)
                            i.then_inc(mem, 1)
                    if t.within(B):
                        r = t
                        dve.wait_ge(ke, r.b + 1)
                        dve.wait_ge(kr, r.b + 1)
                        wait(dve, kT_mm, 1, r.b - 2)
                        nc.vector.scalar_tensor_tensor(KT[r.par][:, :], KE[r.par][:, :], 1.0, KR[r.par][:, :],
                                                       ALU.min, ALU.add).then_inc(kt, 1)
                        dve.wait_ge(v_mm, r.b + 1)
                        nc.vector.tensor_tensor(V[r.par][:, :, :], quad[3],
                                                BVA[:, None, :].broadcast_to([128, C, D]), ALU.add).then_inc(vv, 1)
                    if (t + -2).within(B):
                        ffn_inputs(t + -2)
                    if (t + 1).within(B):
                        input_stats(t + 1)
                    if (t + -2).within(B):
                        r = t + -2
                        apart(dve, aff_mm, r.b + 1, dve_passed)
                        nc.vector.tensor_copy(AFF[:, ds(C * r.b, C), :],
                                              bank[7][:, 0:C * E].rearrange("p (c e) -> p c e", c=C)
                                              ).then_inc(affv, 1)
                input_stats(Round(0, 0, 0))
                rounds(dve, 0, LO, HI, END, step)

            @block.gpsimd
            def _(pool):
                def input_rstd(r):
                    pool.wait_ge(aggr, r.b + 1)
                    wait(pool, u_done, 1, r.b - 2)
                    nc.gpsimd.tensor_tensor(tmp[r.par][:, 1, :], mv[r.par][:, :, 1], EPS1, ALU.add).then_inc(veps, 1)
                    pool.wait_ge(veps, r.b + 1)
                    nc.gpsimd.tensor_tensor(tmp[r.par][:, 0, :], tmp[r.par][:, 1, :], MHALF,
                                            ALU.pow).then_inc(rstd, 1)

                def ffn_rstd(r):
                    tt, n = tmp[r.par], [0]
                    pool.wait_ge(aggr1, r.b + 1)
                    wait(pool, u1, C, r.b - 1)

                    def op(o, a, b_, f):
                        nc.gpsimd.tensor_tensor(o, a, b_, f).then_inc(chain1, 1)
                        n[0] += 1
                        pool.wait_ge(chain1, 6 * r.b + n[0])
                    op(tt[:, 3, :], mv1[r.par][:, :, 1], EPS1, ALU.add)
                    op(tt[:, 2, :], tt[:, 3, :], MHALF, ALU.pow)
                    op(tt[:, 4, :], mv1[r.par][:, :, 1], tt[:, 2, :], ALU.mult)
                    op(tt[:, 5, :], tt[:, 4, :], tt[:, 2, :], ALU.mult)
                    op(tt[:, 6, :], tt[:, 5, :], EPS1, ALU.add)
                    op(tt[:, 3, :], tt[:, 6, :], MHALF, ALU.pow)
                    nc.gpsimd.tensor_tensor(tt[:, 7, :], tt[:, 3, :], tt[:, 2, :], ALU.mult).then_inc(rstd1, 1)

                def step(t):
                    if (t + -2).within(B):
                        ffn_rstd(t + -2)
                    if t.within(B):
                        r = t
                        xb = X[:, ds(C * r.b, C), :]
                        pool.wait_ge(u_done, r.b + 1)
                        nc.gpsimd.tensor_tensor(xb, xb, BOA[:, None, :].broadcast_to([128, C, D]),
                                                ALU.add).then_inc(xbo, 1)
                        pool.wait_ge(qv, r.b + 1)
                        wait(pool, r_mm, 1, r.b - 2)
                        nc.gpsimd.tensor_tensor(QD[r.par][:, :, :],
                                                QT[r.par][:, :].rearrange("p (c t) -> p c t", c=C),
                                                DROW[:, None, 0:128].broadcast_to([128, C, 128]),
                                                ALU.mult).then_inc(qd, 1)
                    if (t + 1).within(B):
                        input_rstd(t + 1)
                    if (t + -2).within(B):
                        r = t + -2
                        xb = X[:, ds(C * r.b, C), :]
                        pool.wait_ge(u1, C * (r.b + 1))
                        nc.gpsimd.tensor_tensor(xb, xb, U1[r.par][:, :, :], ALU.add).then_inc(base, 1)
                input_rstd(Round(0, 0, 0))
                rounds(pool, 0, LO, HI, END, step)

            @block.scalar
            def _(act):
                def step(t):
                    if t.within(B):
                        r = t
                        act.wait_ge(uT, r.b + 1)
                        wait(act, v_mm, 1, r.b - 2)
                        nc.scalar.copy(UT[r.par][:, :], bank[0][:, :]).then_inc(uTv, 1)
                    if (t + -1).within(B):
                        r = t + -1
                        act.wait_ge(kT_mm, r.b + 1)
                        wait(act, U_mm, 1, r.b - 2)
                        nc.scalar.mul(KP[r.par][:, :, :], quad[3], DEC[:, 128:129]).then_inc(kp, 1)
                    if t.within(B):
                        r = t
                        act.wait_ge(q_mm, r.b + 1)
                        wait(act, s_mm, 1, r.b - 2)
                        wait(act, qd, 1, r.b - 2)
                        nc.scalar.activation(QT[r.par][:, :], bank[1][:, :], ACT.Identity, bias=BQA).then_inc(qv, 1)
                        act.wait_ge(k_mm, r.b + 1)
                        wait(act, kt, 1, r.b - 2)
                        nc.scalar.activation(KE[r.par][:, :], bank[2][:, :], ACT.Exp, bias=BKA).then_inc(ke, 1)
                        nc.scalar.activation(KR[r.par][:, :], bank[2][:, :], ACT.Relu, bias=BKA).then_inc(kr, 1)
                    if (t + -1).within(B):
                        r = t + -1
                        act.wait_ge(r_mm, r.b + 1)
                        wait(act, o_mm, 1, r.b - 2)
                        nc.scalar.copy(RT[r.par][:, :], bank[5][:, :]).then_inc(rtv, 1)
                    if (t + -2).within(B):
                        r = t + -2
                        act.wait_ge(u1T_mm, r.b + 1)
                        wait(act, aff_mm, 1, r.b - 1)
                        nc.scalar.copy(U1T[r.par][:, :], bank[0][:, :]).then_inc(u1Tv, 1)
                rounds(act, 0, LO, HI, END, step)

            @block.tensor
            def _(pe):
                def step(t):
                    f, m, z = t, t + -1, t + -2
                    if f.within(B):
                        pe.wait_ge(u_done, f.b + 1)
                        wait(pe, u1Tv, 1, f.b - 3)
                        if not isinstance(f.b, int) or f.b >= 1:
                            wait(pe, uTv, 1, f.b - 1)
                        for c in range(C):
                            i = nc.tensor.transpose(quad[0][:, c, :], U[f.par][:, c, :], ID)
                        i.then_inc(uT, 1)
                    if z.within(B):
                        pe.wait_ge(rtv, z.b + 1)
                        wait(pe, affv, 1, z.b - 1)
                        for c in range(C):
                            i = nc.tensor.matmul(quad[7][:, c, :], RT[z.par][:, 128 * c:128 * c + 128],
                                                 WA[:, 3, :], start=True, stop=True)
                        i.then_inc(o_mm, 1)
                    if m.within(B):
                        pe.wait_ge(qv, m.b + 1)
                        pe.wait_ge(kt, m.b + 1)
                        wait(pe, sm, 1, m.b - 1)
                        for c in range(C):
                            sl = slice(128 * c, 128 * c + 128)
                            i = nc.tensor.matmul(quad[4][:, c, :], KT[m.par][:, sl], QT[m.par][:, sl],
                                                 start=True, stop=True)
                        i.then_inc(s_mm, 1)
                        pe.wait_ge(vv, m.b + 1)
                        for c in range(C):
                            i = nc.tensor.transpose(quad[3][:, c, :], KT[m.par][:, 128 * c:128 * c + 128], ID)
                        i.then_inc(kT_mm, 1)
                    if f.within(B):
                        pe.wait_ge(uTv, f.b + 1)
                        wait(pe, qv, 1, f.b - 1)
                        nc.tensor.matmul(bank[1][:, :], WA[:, 0, :], UT[f.par][:, :], start=True,
                                         stop=True).then_inc(q_mm, 1)
                        wait(pe, kr, 1, f.b - 1)
                        wait(pe, ke, 1, f.b - 1)
                        nc.tensor.matmul(bank[2][:, :], WA[:, 1, :], UT[f.par][:, :], start=True,
                                         stop=True).then_inc(k_mm, 1)
                    if m.within(B):
                        pe.wait_ge(kp, m.b + 1)
                        wait(pe, mem, C - 1, m.b - 1)
                        for c in range(C - 1):
                            i = nc.tensor.matmul(quad[6][:, c, :], KP[m.par][:, c, :], V[m.par][:, c, :],
                                                 start=True, stop=True)
                        i.then_inc(U_mm, 1)
                    if f.within(B):
                        wait(pe, kp, 1, f.b - 1)
                        for c in range(C):
                            i = nc.tensor.matmul(quad[3][:, c, :], UT[f.par][:, 128 * c:128 * c + 128],
                                                 WA[:, 2, :], start=True, stop=True)
                        i.then_inc(v_mm, 1)
                    if m.within(B):
                        pe.wait_ge(sm, m.b + 1)
                        pe.wait_ge(qd, m.b + 1)
                        wait(pe, rtv, 1, m.b - 1)
                        for c in range(C):
                            i = nc.tensor.matmul(quad[5][:, c, :], V[m.par][:, c, :], SM_[m.par][:, c, :],
                                                 start=True, stop=(c == 0))
                            if c:
                                pe.wait_ge(mem, (C - 1) * m.b + c)
                                i = nc.tensor.matmul(quad[5][:, c, :], MEM[m.par][:, c - 1, :],
                                                     QD[m.par][:, c, :], start=False, stop=True)
                        i.then_inc(r_mm, 1)
                    if z.within(B):
                        pe.wait_ge(u1, C * (z.b + 1))
                        if f.within(B):
                            pe.wait_ge(uTv, f.b + 1)
                        else:
                            wait(pe, u1Tv, 1, z.b - 1)
                        for c in range(C):
                            i = nc.tensor.transpose(quad[0][:, c, :], U1[z.par][:, c, :], ID)
                        i.then_inc(u1T_mm, 1)
                        pe.wait_ge(u1Tv, z.b + 1)
                        pe.wait_ge(x1, z.b + 1)
                        for c in range(C):
                            i = nc.tensor.matmul(bank[7][:, E * c:E * c + E], U1T[z.par][:, 128 * c:128 * c + 128],
                                                 CENT, start=True, stop=True)
                        i.then_inc(aff_mm, 1)
                rounds(pe, 0, LO, HI, END, step)

        if upto == 1:
            with ExitStack() as cd:
                dd = sem("dd")
                block = cd.enter_context(nc.Block())

                @block.sync
                def _(sp):
                    for k, t in enumerate((X[:, :, :], XH[:, :, :])):
                        sp.dma_start(dbg[k].rearrange("(t p) d -> p t d", p=128), t).then_inc(dd, 16)
                    sp.dma_start(dbg[2, :, 0:8].rearrange("(t p) d -> p t d", p=128), AFF[:, :, :]).then_inc(dd, 16)
                    sp.dma_start(dbg[2, 0:128, 8:72], W1T[:, 3, 0:64]).then_inc(dd, 16)
                    sp.dma_start(dbg[2, 128:256, 8:72], C2[:, 3, 0:64]).then_inc(dd, 16)
                    sp.dma_start(dbg[2, 256:384, 8:40], NB1[:, :, :].rearrange("p e c -> p (e c)")).then_inc(dd, 16)
                    sp.wait_ge(dd, 96)
            return
        def route(tag, W1T, W2T):
            with ExitStack() as c:
                w_kept = sem(f"r{tag}_w")
                AM = sb(f"AM{tag}", [128, NT], c=c)
                EX = sb(f"EX{tag}", [128, NT], c=c)
                EX1 = sb(f"EX1{tag}", [128, NT], c=c)
                EQ = sb(f"EQ{tag}", [128, NT, E], c=c)
                KEY = sb(f"KEY{tag}", [128, NT, E], c=c)
                KM = sb(f"KM{tag}", [128, NT], c=c)
                OH = sb(f"OH{tag}", [128, E, NT], c=c)
                INC = sb(f"INC{tag}", [128, E, NT], c=c)
                GT = sb(f"GT{tag}", [128, E, NT], c=c)
                N_T = sb(f"N_T{tag}", [128, E], c=c)
                CUM = sb(f"CUM{tag}", [128, E], c=c)
                STA = sb(f"STA{tag}", [128, E], c=c)
                WT = sb(f"WT{tag}", [128, 3, E, NT], c=c)
                SEL = sb(f"SEL{tag}", [128, E, NT], c=c)
                POSF = sb(f"POSF{tag}", [128, NT], c=c)
                CMP = sb(f"CMP{tag}", [1, TILES, E - 1], c=c)
                TEF = sb(f"TEF{tag}", [1, TILES], c=c)
                IDX = [sb(f"IDX{tag}{i}", [128, C], I32, c=c) for i in range(2)]
                XS = [sb(f"XS{tag}{i}", [128, C, D], c=c) for i in range(2)]
                amax, exd, onehot, counts, chain, pos = (sem(f"r{tag}_{n}") for n in
                                                         ("amax", "exd", "onehot", "counts", "chain", "pos"))
                idx_here, xs_here = sem(f"r{tag}_idx"), sem(f"r{tag}_xs")
                sent = [sem(f"r{tag}_sent{i}") for i in range(2)]
                block = c.enter_context(nc.Block())
                code = CODE[:, None, :].broadcast_to([128, NT, E])

                @block.vector
                def _(dve):
                    n = [0]

                    def link(i):
                        i.then_inc(chain, 1)
                        n[0] += 1
                        dve.wait_ge(chain, n[0])
                    nc.vector.tensor_reduce(AM[:, :], AFF[:, :, :], axis=AX.X, op=ALU.max).then_inc(amax, 1)
                    dve.wait_ge(amax, 1)
                    link(nc.vector.tensor_tensor(EQ[:, :, :], AFF[:, :, :],
                                                 AM[:, :, None].broadcast_to([128, NT, E]), ALU.is_equal))
                    link(nc.vector.tensor_tensor(KEY[:, :, :], EQ[:, :, :], code, ALU.mult))
                    link(nc.vector.tensor_reduce(KM[:, :], KEY[:, :, :], axis=AX.X, op=ALU.max))
                    nc.vector.tensor_tensor(OH[:, :, :], CODE[:, :, None].broadcast_to([128, E, NT]),
                                            KM[:, None, :].broadcast_to([128, E, NT]),
                                            ALU.is_equal).then_inc(onehot, 1)
                    dve.wait_ge(exd, 1)
                    link(nc.vector.tensor_scalar_add(EX1[:, :], EX[:, :], 1.0))
                    nc.vector.reciprocal(ALPHA[:, :], EX1[:, :])
                    dve.wait_ge(counts, 1)
                    rank = bank[0][:, 0:E * NT].rearrange("p (e t) -> p e t", e=E)
                    tot = bank[1][:, 0:E * NT].rearrange("p (e t) -> p e t", e=E)
                    link(nc.vector.tensor_tensor_scan(INC[:, :, :].rearrange("p e t -> p (e t)"), RESET,
                                                      bank[1][:, 0:E * NT], 0.0, ALU.mult, ALU.add))
                    link(nc.vector.tensor_tensor(WT[:, 0, :, :], INC[:, :, :], tot, ALU.subtract))
                    link(nc.vector.tensor_tensor(WT[:, 1, :, :], WT[:, 0, :, :], rank, ALU.add))
                    link(nc.vector.tensor_tensor(GT[:, :, :], INC[:, :, NT - 1:NT].broadcast_to([128, E, NT]),
                                                 STEPS[:, None, :].broadcast_to([128, E, NT]), ALU.is_gt))
                    link(nc.vector.tensor_reduce(N_T[:, :], GT[:, :, :], axis=AX.X, op=ALU.add))
                    link(nc.vector.tensor_tensor_scan(CUM[:, :], ONES[:, 0:E], N_T[:, :], 0.0, ALU.mult, ALU.add))
                    link(nc.vector.tensor_tensor(STA[:, :], CUM[:, :], N_T[:, :], ALU.subtract))
                    link(nc.vector.scalar_tensor_tensor(WT[:, 2, :, :], STA[:, :, None].broadcast_to([128, E, NT]),
                                                        128.0, WT[:, 1, :, :], ALU.mult, ALU.add))
                    link(nc.vector.tensor_tensor(SEL[:, :, :], WT[:, 2, :, :], OH[:, :, :], ALU.mult))
                    link(nc.vector.tensor_reduce(POSF[:, :], SEL[:, :, :].rearrange("p e t -> p t e"),
                                                 axis=AX.X, op=ALU.add))
                    nc.vector.tensor_copy(POS[:, :], POSF[:, :]).then_inc(pos, 1)
                    link(nc.vector.tensor_tensor(CMP[:, :, :], ROW39[0:1, :, None].broadcast_to([1, TILES, E - 1]),
                                                 CUM[0:1, None, 0:E - 1].broadcast_to([1, TILES, E - 1]),
                                                 ALU.is_ge))
                    link(nc.vector.tensor_reduce(TEF[:, :], CMP[:, :, :], axis=AX.X, op=ALU.add))
                    nc.vector.tensor_copy(TE[:, :], TEF[:, :])
                    dve.wait_ge(pos, 1)

                    def stage(r):
                        apart(dve, sent[r.par], 16 * C * r.half, dve_passed)
                        nc.vector.tensor_copy(IDX[r.par][:, :], POS[:, ds(C * r.b, C)]).then_inc(idx_here, 1)
                    rounds(dve, 0, 2, 8, 7, stage)

                @block.sync
                def _(sp):
                    for kept, w in ((w1_dram, W1T[:, :, :].rearrange("p e f -> p (e f)")),
                                    (w2_dram, W2T[:, :, :, :].rearrange("p e c d -> p (e c d)"))):
                        sp.dma_start(*((kept, w) if tag == 1 else (w, kept))).then_inc(w_kept, 16)
                    sp.wait_ge(w_kept, 32)

                @block.scalar
                def _(act):
                    act.wait_ge(amax, 1)
                    nc.scalar.activation(EX[:, :], AM[:, :], ACT.Exp, scale=-1.0).then_inc(exd, 1)

                    def stage(r):
                        at_least(act, sent[r.par], 16 * C * r.half)
                        nc.scalar.copy(XS[r.par][:, :, :], XH[:, ds(C * r.b, C), :]).then_inc(xs_here, 1)
                    rounds(act, 0, 2, 8, 7, stage)

                @block.tensor
                def _(pe):
                    pe.wait_ge(onehot, 1)
                    oh = OH[:, :, :].rearrange("p e t -> p (e t)")
                    nc.tensor.matmul(bank[0][:, 0:E * NT], LOW, oh, start=True, stop=True)
                    nc.tensor.matmul(bank[1][:, 0:E * NT], ONES[:, :], oh, start=True, stop=True).then_inc(counts, 1)

                @block.gpsimd
                def _(pool):
                    def send(r):
                        pool.wait_ge(idx_here, r.b + 1)
                        apart(pool, xs_here, r.b + 1, pool_passed)
                        for c_ in range(C):
                            nc.gpsimd.indirect_dma_start(
                                sorted_x, bass.IndirectOffsetOnAxis(ap=IDX[r.par][:, c_:c_ + 1], axis=0),
                                XS[r.par][:, c_, :], None).then_inc(sent[r.par], 16)
                    rounds(pool, 0, 2, 8, 7, send)
                    for i in range(2):
                        pool.wait_ge(sent[i], 16 * C * B // 2)

        NB = 3

        def experts(tag, W1T, W2T):
            with ExitStack() as c:
                XT_IN = [sb(f"f{tag}_x{i}", [128, D], c=c) for i in range(NB)]
                W1B = [sb(f"f{tag}_w{i}", [128, F], c=c) for i in range(NB)]
                XT = [sb(f"f{tag}_xt{i}", [128, 128], c=c) for i in range(NB)]
                HM = [sb(f"f{tag}_h{i}", [128, FC, 128], c=c) for i in range(NB)]
                Y = [sb(f"f{tag}_y{i}", [128, D], c=c) for i in range(NB)]
                x_in_ = [sem(f"f{tag}_xin{i}") for i in range(NB)]
                w_in = [sem(f"f{tag}_win{i}") for i in range(NB)]
                y_out = [sem(f"f{tag}_yout{i}") for i in range(NB)]
                xt_mm, xtv, h_mm, hv, y_mm, yv = (sem(f"f{tag}_" + n) for n in ("xt", "xtv", "h", "hv", "y", "yv"))
                XB, HB, YB = (0, 1, 0), (3, 4, 5), (2, 6, 7)
                block = c.enter_context(nc.Block())

                def tiles(eng, body, lag):
                    for t in range(2 * NB):
                        body(t, t // NB, t % NB)
                    with eng.Fori(2, TILES // NB) as i:
                        for k in range(NB):
                            body(NB * i + k, i, k)
                    for t in range(TILES, TILES + lag):
                        body(t, t // NB, t % NB)

                def back(t, use, k, lag):
                    if isinstance(t, int) and not 0 <= t - lag < TILES:
                        return None
                    return t - lag, use - (1 if k < lag else 0), (k - lag) % NB

                def expert(eng, t):
                    return eng.value_load(TE[0:1, ds(t, 1)], min_val=0, max_val=E - 1)

                @block.sync
                def _(sp):
                    def load(t, use, k):
                        at_least(sp, xt_mm, t - 2)
                        sp.dma_start(XT_IN[k][:, :], sorted_x[ds(128 * t, 128), :]).then_inc(x_in_[k], 16)
                        e = expert(sp, t)
                        at_least(sp, h_mm, t - 2)
                        sp.dma_start(W1B[k][:, :], W1T[:, ds(e, 1), :].rearrange("p e f -> p (e f)")
                                     ).then_inc(w_in[k], 16)
                    tiles(sp, load, 0)

                @block.gpsimd
                def _(pool):
                    def store(t, use, k):
                        pool.wait_ge(yv, t + 1)
                        nc.gpsimd.dma_start(sorted_y[ds(128 * t, 128), :], Y[k][:, :]).then_inc(y_out[k], 16)
                    tiles(pool, store, 0)
                    for k in range(NB):
                        pool.wait_ge(y_out[k], 16 * TILES // NB)

                @block.scalar
                def _(act):
                    def step(t, use, k):
                        act.wait_ge(xt_mm, t + 1)
                        at_least(act, h_mm, t - 2)
                        nc.scalar.copy(XT[k][:, :], bank[XB[k]][:, 0:128]).then_inc(xtv, 1)
                    tiles(act, step, 0)

                @block.vector
                def _(dve):
                    def step(t, use, k):
                        z = back(t, use, k, 0)
                        if z:
                            e = expert(dve, z[0])
                            dve.wait_ge(h_mm, z[0] + 1)
                            at_least(dve, y_mm, z[0] - 2)
                            nc.vector.tensor_tensor(
                                HM[k][:, :, :], quad[HB[k]],
                                NB1[:, ds(e, 1), :].rearrange("p e c -> p (e c)")[:, :, None]
                                .broadcast_to([128, FC, 128]), ALU.max).then_inc(hv, 1)
                        z = back(t, use, k, 1)
                        if z:
                            e = expert(dve, z[0])
                            dve.wait_ge(y_mm, z[0] + 1)
                            at_least(dve, y_out[z[2]], 16 * z[1])
                            nc.vector.tensor_tensor(Y[z[2]][:, :], bank[YB[z[2]]][:, 0:D],
                                                    C2[:, ds(e, 1), :].rearrange("p e d -> p (e d)"),
                                                    ALU.add).then_inc(yv, 1)
                    tiles(dve, step, 1)

                @block.tensor
                def _(pe):
                    def step(t, use, k):
                        z = back(t, use, k, 0)
                        if z:
                            pe.wait_ge(x_in_[k], 16 * (use + 1))
                            at_least(pe, xtv, t - (0, 2, 1)[k])
                            nc.tensor.transpose(bank[XB[k]][:, 0:128], XT_IN[k][:, :], ID).then_inc(xt_mm, 1)
                        z = back(t, use, k, 1)
                        if z:
                            j, u, kk = z
                            pe.wait_ge(w_in[kk], 16 * (u + 1))
                            pe.wait_ge(xtv, j + 1)
                            at_least(pe, hv, j - 2)
                            for f in range(FC):
                                m = nc.tensor.matmul(quad[HB[kk]][:, f, :], W1B[kk][:, 128 * f:128 * f + 128],
                                                     XT[kk][:, :], start=True, stop=True)
                            m.then_inc(h_mm, 1)
                        z = back(t, use, k, 2)
                        if z:
                            j, u, kk = z
                            e = expert(pe, j)
                            pe.wait_ge(hv, j + 1)
                            at_least(pe, yv, j - 2)
                            for f in range(FC):
                                m = nc.tensor.matmul(bank[YB[kk]][:, 0:D], HM[kk][:, f, :],
                                                     W2T[:, ds(e, 1), f, :].rearrange("p e d -> p (e d)"),
                                                     start=(f == 0), stop=(f == FC - 1))
                            m.then_inc(y_mm, 1)
                    tiles(pe, step, 2)

        def attention():
            with ExitStack() as c:
                def two(name, shape, dt=F32):
                    return [sb(f"b_{name}{i}", shape, dt, c=c) for i in range(2)]
                IDX = two("IDX", [128, C], I32)
                GA = [sb("b_GA", [128, C, D], c=c)] * 2
                st, mv, st3, mv3 = two("st", [128, C, 6]), two("mv", [128, C, 2]), two("st3", [128, C, 6]), \
                    two("mv3", [128, C, 2])
                tmp = two("tmp", [128, 8, C])
                U2, U2T = [sb("b_U2", [128, C, D], c=c)] * 2, [sb("b_U2T", [128, S], c=c)] * 2
                QF, KF = sb("b_QF", [128, S], c=c), sb("b_KF", [128, S], c=c)
                QHI, QLO = sb("b_QHI", [128, S], F32R, c=c), sb("b_QLO", [128, S], F32R, c=c)
                KHI, KLO = sb("b_KHI", [128, S], F32R, c=c), sb("b_KLO", [128, S], F32R, c=c)
                QS, KS = two("QS", [128, SETS, S], F32R), two("KS", [128, SETS, G, S], F32R)
                VA = two("VA", [128, C, H, AUG])
                NM = two("NM", [128, SETS, C, G])
                PARTS, STACK = 3 * G * HD, 3 * G * HD + G
                P = two("P", [128, G, S])
                OSB = two("OSB", [128, S])
                RC = two("RC", [128, C, G])
                AT, ATB = [sb("b_AT", [128, C, D], c=c)] * 2, [sb("b_ATB", [128, C, D], c=c)] * 2
                ATT, U3 = [sb("b_ATT", [128, S], c=c)] * 2, [sb("b_U3", [128, C, D], c=c)] * 2
                U3T = [sb("b_U3T", [128, S], c=c)] * 2
                (idx_here, x2, xbo, stats, aggr, veps, rstd, u2, u2T_mm, u2Tv, q_mm, qf, k_mm, kf, q_parts, k_parts,
                 q_stack, k_stack, v_mm, vv, mx_mm, mx, ones_in, s_mm, exps, av, o_v,
                 otr_mm, rc, otr_v, atb, att_mm, att_v, o_mm, x3, stats3, aggr3, chain3, rstd3, u3, base,
                 u3T_mm, u3Tv, aff_mm, affv) = (sem("b_" + n) for n in (
                     "idx x2 xbo stats aggr veps rstd u2 u2T u2Tv q qf k kf q_parts k_parts "
                     "q_stack k_stack v vv mx_mm mx ones_in s exps av o_v "
                     "otr rc otr_v atb att att_v o x3 stats3 aggr3 chain3 rstd3 u3 base "
                     "u3T u3Tv aff affv").split())
                mt_mm = sem("b_mt_mm")
                k_zero, k_zero1 = sem("b_k_zero"), sem("b_k_zero1")
                q_hi, k_hi, vones, va_zero = sem("b_q_hi"), sem("b_k_hi"), sem("b_vones"), sem("b_va_zero")
                mt_v = sem("b_mt_v")
                gath = [sem(f"b_gath{i}") for i in range(2)]
                O, MISC = bank[6], bank[7]
                MQ = quad[7]
                SLOTS = SETS * C
                misc = [("u2T", 1, 0), ("otr", -1, 3), ("mt", 0, 1), ("q", 1, 0), ("k", 1, 0), ("otr", 0, 0),
                        ("mt", 0, 2), ("att", -1, 0), ("wo", -1, 0), ("otr", 0, 1), ("mt", 0, 3), ("v", 1, 0),
                        ("u3T", -1, 0), ("otr", 0, 2), ("mt", 1, 0), ("aff", -1, 0)]
                taken = {"u2T": (u2Tv, 1), "otr": (otr_v, SETS), "mt": (mt_v, SETS), "q": (qf, 1), "k": (kf, 1),
                         "att": (att_v, 1), "wo": (x3, 1), "v": (vv, 1), "u3T": (u3Tv, 1), "aff": (affv, 1)}

                def misc_free(pe, t, k):
                    for back_ in range(1, 3 * SLOTS):
                        n = k - back_
                        r = t + n // SLOTS
                        what, ahead, s = misc[n % SLOTS]
                        r = r + ahead
                        if isinstance(r.b, int) and not 0 <= r.b < B:
                            continue
                        signal, per = taken[what]
                        at_least(pe, signal, per * r.b + s + 1)
                        return

                def m_slot(t, k):
                    return (t, 2 + k // C) if k < SLOTS // 2 else (t + 1, k // C - 2)
                FIRST, LO, HI, END = -2, 2, 6, 8
                block = c.enter_context(nc.Block())

                @block.sync
                def _(sp):
                    sp.wait_ge(k_zero, 1)
                    sp.wait_ge(k_zero1, 1)

                    def stack(r, what, parts, src_ready, done, per):
                        apart(sp, src_ready, r.b + 1, sp_passed)
                        apart(sp, done, 16 * per * r.b, sp_passed)
                        apart(sp, s_mm, 2 * SLOTS * (r.b - 1), sp_passed)
                        for n, part in enumerate(parts):
                            if what == "q":
                                sp.dma_start(QS[r.par][32 * n:32 * n + 32, :, :].bitcast(F32),
                                             part[:, :].bitcast(F32)).then_inc(done, 16)
                                continue
                            for g in range(G):
                                z = 32 * n + HD * g
                                sp.dma_start(KS[r.par][z:z + HD, :, g, :].bitcast(F32),
                                             part[32 * g:32 * g + 32, :].bitcast(F32)).then_inc(done, 16)

                    def step(t):
                        for k in range(SLOTS):
                            what, ahead, s = misc[k]
                            r = t + ahead
                            if not r.within(B):
                                continue
                            if what == "q":
                                stack(r, what, (QHI, QHI, QLO), q_parts, q_stack, 3)
                            if what == "k":
                                stack(r, what, (KHI, KLO, KHI), k_parts, k_stack, 3 * G)
                    rounds(sp, FIRST, LO, HI, END, step)

                @block.gpsimd
                def _(pool):
                    def gather(r):
                        wait(pool, x2, 1, r.b - 1)
                        apart(pool, idx_here, r.b + 1, pool_passed)
                        for c_ in range(C):
                            nc.gpsimd.indirect_dma_start(
                                GA[r.par][:, c_, :], None, sorted_y,
                                bass.IndirectOffsetOnAxis(ap=IDX[r.par][:, c_:c_ + 1], axis=0)
                            ).then_inc(gath[r.par], 16)

                    def rstd_in(r):
                        pool.wait_ge(aggr, r.b + 1)
                        wait(pool, u2, 1, r.b - 2)
                        nc.gpsimd.tensor_tensor(tmp[r.par][:, 1, :], mv[r.par][:, :, 1], EPS1, ALU.add).then_inc(veps, 1)
                        pool.wait_ge(veps, r.b + 1)
                        nc.gpsimd.tensor_tensor(tmp[r.par][:, 0, :], tmp[r.par][:, 1, :], MHALF,
                                                ALU.pow).then_inc(rstd, 1)

                    def rstd_out(r):
                        tt, n = tmp[r.par], [0]
                        pool.wait_ge(aggr3, r.b + 1)
                        wait(pool, u3, C, r.b - 1)

                        def op(o, a, b_, f):
                            nc.gpsimd.tensor_tensor(o, a, b_, f).then_inc(chain3, 1)
                            n[0] += 1
                            pool.wait_ge(chain3, 6 * r.b + n[0])
                        op(tt[:, 3, :], mv3[r.par][:, :, 1], EPS1, ALU.add)
                        op(tt[:, 2, :], tt[:, 3, :], MHALF, ALU.pow)
                        op(tt[:, 4, :], mv3[r.par][:, :, 1], tt[:, 2, :], ALU.mult)
                        op(tt[:, 5, :], tt[:, 4, :], tt[:, 2, :], ALU.mult)
                        op(tt[:, 6, :], tt[:, 5, :], EPS1, ALU.add)
                        op(tt[:, 3, :], tt[:, 6, :], MHALF, ALU.pow)
                        nc.gpsimd.tensor_tensor(tt[:, 7, :], tt[:, 3, :], tt[:, 2, :], ALU.mult).then_inc(rstd3, 1)

                    def parts(r, full, hi, lo, ready, stacked, per, first, done):
                        wait(pool, stacked, 16 * per, r.b - 1)
                        apart(pool, ready, r.b + 1, pool_passed)
                        nc.gpsimd.tensor_copy(hi[:, :], full[:, :]).then_inc(first, 1)
                        pool.wait_ge(first, r.b + 1)
                        nc.gpsimd.tensor_tensor(lo[:, :], full[:, :], hi[:, :].bitcast(F32),
                                                ALU.subtract).then_inc(done, 1)

                    def step(t):
                        for k in range(SLOTS):
                            if k == 0 and (t + 2).within(B):
                                gather(t + 2)
                            if k == 2 and (t + -1).within(B):
                                r = t + -1
                                pool.wait_ge(otr_v, SETS * (r.b + 1))
                                wait(pool, att_mm, 1, r.b - 1)
                                nc.gpsimd.tensor_tensor(ATB[r.par][:, :, :], AT[r.par][:, :, :],
                                                        BVB[:, None, :].broadcast_to([128, C, D]),
                                                        ALU.add).then_inc(atb, 1)
                            if k == 3 and (t + 1).within(B):
                                parts(t + 1, QF, QHI, QLO, qf, q_stack, 3, q_hi, q_parts)
                            if k == 4 and (t + 1).within(B):
                                parts(t + 1, KF, KHI, KLO, kf, k_stack, 3 * G, k_hi, k_parts)
                            if k == 6 and (t + 2).within(B):
                                rstd_in(t + 2)
                            if k == 9 and (t + -1).within(B):
                                rstd_out(t + -1)
                            if k == 12 and (t + 2).within(B):
                                r = t + 2
                                xb = X[:, ds(C * r.b, C), :]
                                pool.wait_ge(u2, r.b + 1)
                                nc.gpsimd.tensor_tensor(xb, xb, BOB[:, None, :].broadcast_to([128, C, D]),
                                                        ALU.add).then_inc(xbo, 1)
                            if k == 13 and (t + -1).within(B):
                                r = t + -1
                                xb = X[:, ds(C * r.b, C), :]
                                pool.wait_ge(u3, C * (r.b + 1))
                                nc.gpsimd.tensor_tensor(xb, xb, U3[r.par][:, :, :], ALU.add).then_inc(base, 1)
                    nc.gpsimd.memset(KS[1][0:PARTS, :, :, :].bitcast(F32), 0.0).then_inc(k_zero1, 1)
                    rounds(pool, FIRST, LO, HI, END, step)

                @block.vector
                def _(dve):
                    for p in range(2):
                        i = nc.vector.memset(VA[p][:, :, :, :], 0.0)
                    i.then_inc(va_zero, 1)
                    nc.vector.memset(KS[0][0:PARTS, :, :, :].bitcast(F32), 0.0).then_inc(k_zero, 1)

                    def xs(r, c_):
                        return X[:, ds(C * r.b + c_, 1), :].rearrange("p o d -> p (o d)")

                    def add_ffn(r):
                        dve.wait_ge(gath[r.par], 16 * C * (r.half + 1))
                        for c_ in range(C):
                            i = nc.vector.scalar_tensor_tensor(xs(r, c_), GA[r.par][:, c_, :],
                                                               ALPHA[:, ds(C * r.b + c_, 1)], xs(r, c_),
                                                               ALU.mult, ALU.add)
                        i.then_inc(x2, 1)
                        apart(dve, x2, r.b + 1, dve_passed)
                        for c_ in range(C):
                            i = nc.vector.bn_stats(st[r.par][:, c_, :], xs(r, c_))
                        i.then_inc(stats, 1)
                        dve.wait_ge(stats, r.b + 1)
                        apart(dve, rstd, r.b - 1, dve_passed)
                        for c_ in range(C):
                            i = nc.vector.bn_aggr(mv[r.par][:, c_, :], st[r.par][:, c_, :])
                        i.then_inc(aggr, 1)

                    def index(r):
                        apart(dve, gath[r.par], 16 * C * r.half, dve_passed)
                        nc.vector.tensor_copy(IDX[r.par][:, :], POS[:, ds(C * r.b, C)]).then_inc(idx_here, 1)

                    def step(t):
                        for k in range(SLOTS):
                            if k == 0 and (t + 2).within(B):
                                index(t + 2)
                            r, s = m_slot(t, k)
                            if r.within(B):
                                for g in range(G):
                                    n = SLOTS * G * r.b + C * G * s + G * (k % C) + g
                                    dve.wait_ge(mx_mm, n + 1)
                                    nc.vector.tensor_reduce(NM[r.par][:, s, k % C, g:g + 1], bank[4 + g % 2],
                                                            axis=AX.X, op=ALU.max, negate=True).then_inc(mx, 1)
                            what, ahead, s = misc[k]
                            r = t + ahead
                            if what == "otr" and r.within(B):
                                n = SETS * r.b + s
                                rows = MQ.rearrange("p c (g a) -> p c g a", g=G)
                                dve.wait_ge(otr_mm, n + 1)
                                nc.vector.reciprocal(RC[s % 2][:, :, :], rows[:, :, :, HD]).then_inc(rc, 1)
                                dve.wait_ge(rc, n + 1)
                                if s == 0:
                                    wait(dve, atb, 1, r.b - 1)
                                nc.vector.tensor_tensor(
                                    AT[r.par][:, :, 32 * s:32 * s + 32].rearrange("p c (g d) -> p c g d", g=G),
                                    rows[:, :, :, 0:HD], RC[s % 2][:, :, :, None].broadcast_to([128, C, G, HD]),
                                    ALU.mult).then_inc(otr_v, 1)
                            if what == "wo" and r.within(B):
                                dve.wait_ge(o_mm, r.b + 1)
                                dve.wait_ge(xbo, r.b + 1)
                                nc.vector.tensor_tensor(X[:, ds(C * r.b, C), :], MQ, X[:, ds(C * r.b, C), :],
                                                        ALU.add).then_inc(x3, 1)
                                apart(dve, x3, r.b + 1, dve_passed)
                                for c_ in range(C):
                                    i = nc.vector.bn_stats(st3[r.par][:, c_, :], xs(r, c_))
                                i.then_inc(stats3, 1)
                                dve.wait_ge(stats3, r.b + 1)
                                apart(dve, rstd3, r.b, dve_passed)
                                for c_ in range(C):
                                    i = nc.vector.bn_aggr(mv3[r.par][:, c_, :], st3[r.par][:, c_, :])
                                i.then_inc(aggr3, 1)
                            if k == 10 and (t + -1).within(B):
                                r = t + -1
                                dve.wait_ge(rstd3, r.b + 1)
                                wait(dve, u3T_mm, 1, r.b - 1)
                                wait(dve, base, 1, r.b - 1)
                                for c_ in range(C):
                                    nc.vector.tensor_scalar(U3[r.par][:, c_, :], xs(r, c_), mv3[r.par][:, c_, 0:1],
                                                            tmp[r.par][:, 2, c_:c_ + 1], ALU.subtract, ALU.mult)
                                    nc.vector.tensor_scalar(XH[:, ds(C * r.b + c_, 1), :].rearrange("p o d -> p (o d)"),
                                                            xs(r, c_), mv3[r.par][:, c_, 0:1],
                                                            tmp[r.par][:, 7, c_:c_ + 1], ALU.subtract, ALU.mult
                                                            ).then_inc(u3, 1)
                            if what == "aff" and r.within(B):
                                apart(dve, aff_mm, r.b + 1, dve_passed)
                                nc.vector.tensor_copy(AFF[:, ds(C * r.b, C), :],
                                                      MISC[:, 0:C * E].rearrange("p (c e) -> p c e", c=C)
                                                      ).then_inc(affv, 1)
                            if k == 4 and (t + 2).within(B):
                                add_ffn(t + 2)
                            if k == 8 and (t + 2).within(B):
                                r = t + 2
                                dve.wait_ge(rstd, r.b + 1)
                                wait(dve, u2T_mm, 1, r.b - 1)
                                for c_ in range(C):
                                    i = nc.vector.tensor_scalar(U2[r.par][:, c_, :], xs(r, c_),
                                                                mv[r.par][:, c_, 0:1], tmp[r.par][:, 0, c_:c_ + 1],
                                                                ALU.subtract, ALU.mult)
                                i.then_inc(u2, 1)

                    rounds(dve, FIRST, LO, HI, END, step)

                @block.scalar
                def _(act):
                    act.wait_ge(va_zero, 1)
                    for p in range(2):
                        i = nc.scalar.activation(VA[p][:, :, :, HD:HD + 1], VA[p][:, :, :, HD:HD + 1], ACT.Copy,
                                                 bias=1.0)
                    i.then_inc(vones, 1)
                    act.wait_ge(vones, 1)
                    for p in range(2):
                        nc.scalar.copy(KS[p][PARTS:STACK, :, :, :],
                                       ID[PARTS:STACK, None, PARTS:STACK, None].broadcast_to([G, SETS, G, S])
                                       ).then_inc(ones_in, 1)

                    def step(t):
                        for k in range(SLOTS):
                            if t.within(B):
                                r = t
                                for j in range(2):
                                    act.wait_ge(s_mm, 2 * SLOTS * r.b + 2 * k + j + 1)
                                    at_least(act, av, SLOTS * r.b + k - 1)
                                    nc.scalar.activation(P[k % 2][:, 2 * j:2 * j + 2, :], PS[:, 2 * j:2 * j + 2, :],
                                                         ACT.Exp, scale=SCALE).then_inc(exps, 1)
                            what, ahead, s = misc[k]
                            r = t + ahead
                            if r.within(B):
                                if what == "u2T":
                                    act.wait_ge(u2T_mm, r.b + 1)
                                    wait(act, v_mm, 1, r.b - 1)
                                    nc.scalar.copy(U2T[r.par][:, :], MISC).then_inc(u2Tv, 1)
                                if what == "mt":
                                    act.wait_ge(mt_mm, SETS * r.b + s + 1)
                                    at_least(act, s_mm, 2 * (SLOTS * (r.b - 2) + C * (s + 1)))
                                    nc.scalar.copy(QS[r.par][PARTS:STACK, s, :],
                                                   MISC[PARTS:STACK, :]).then_inc(mt_v, 1)
                                if what == "q":
                                    act.wait_ge(q_mm, r.b + 1)
                                    wait(act, q_parts, 1, r.b - 1)
                                    nc.scalar.activation(QF[:, :], MISC, ACT.Identity, bias=BQB).then_inc(qf, 1)
                                if what == "k":
                                    act.wait_ge(k_mm, r.b + 1)
                                    wait(act, k_parts, 1, r.b - 1)
                                    nc.scalar.activation(KF[:, :], MISC, ACT.Identity, bias=BKB).then_inc(kf, 1)
                                if what == "v":
                                    act.wait_ge(v_mm, r.b + 1)
                                    at_least(act, av, SLOTS * (r.b - 1))
                                    nc.scalar.copy(VA[r.par][:, :, :, 0:HD],
                                                   MQ.rearrange("p c (h d) -> p c h d", h=H)).then_inc(vv, 1)
                                if what == "att":
                                    act.wait_ge(att_mm, r.b + 1)
                                    wait(act, o_mm, 1, r.b - 1)
                                    nc.scalar.copy(ATT[r.par][:, :], MISC).then_inc(att_v, 1)
                                if what == "u3T":
                                    act.wait_ge(u3T_mm, r.b + 1)
                                    wait(act, aff_mm, 1, r.b - 1)
                                    nc.scalar.copy(U3T[r.par][:, :], MISC).then_inc(u3Tv, 1)
                            if k % C == 0:
                                r, s = (t, k // C - 1) if k else (t + -1, SETS - 1)
                                if r.within(B):
                                    n = SETS * r.b + s
                                    act.wait_ge(av, SLOTS * r.b + C * (s + 1))
                                    at_least(act, otr_mm, n - 1)
                                    nc.scalar.copy(OSB[s % 2][:, :], O).then_inc(o_v, 1)
                    rounds(act, FIRST, LO, HI, END, step)

                @block.tensor
                def _(pe):
                    pe.wait_ge(ones_in, 2)
                    pe.wait_ge(vones, 1)

                    def products(r, k):
                        s, c_ = k // C, k % C
                        if c_ == 0:
                            at_least(pe, o_v, SETS * r.b + s)
                            if k == 0:
                                pe.wait_ge(vv, r.b + 1)
                        pe.wait_ge(exps, 2 * (SLOTS * r.b + k + 1))
                        for g in range(G):
                            i = nc.tensor.matmul(O[32 * g:32 * g + 32, :], VA[r.par][:, c_, G * s + g, :],
                                                 P[k % 2][:, g, :], start=(c_ == 0), stop=(c_ == C - 1))
                        i.then_inc(av, 1)

                    def scores(t, k, j):
                        if not t.within(B):
                            return
                        s, c_ = k // C, k % C
                        if c_ == 0 and j == 0:
                            pe.wait_ge(mt_v, SETS * t.b + s + 1)
                        at_least(pe, exps, 2 * (SLOTS * t.b + k) + j - 1)
                        for g in (2 * j, 2 * j + 1):
                            i = nc.tensor.matmul(bank[g], KS[t.par][0:STACK, s, g, 128 * c_:128 * c_ + 128],
                                                 QS[t.par][0:STACK, s, :], start=True, stop=True)
                        i.then_inc(s_mm, 1)

                    def rowwise(t, k, g):
                        r, s = m_slot(t, k)
                        if not r.within(B):
                            return
                        if k == SLOTS // 2 and g == 0:
                            pe.wait_ge(q_stack, 16 * 3 * (r.b + 1))
                            pe.wait_ge(k_stack, 16 * 3 * G * (r.b + 1))
                        at_least(pe, mx, SLOTS * G * r.b + C * G * s + G * (k % C) + g - 1)
                        qt = 128 * (k % C)
                        nc.tensor.matmul(bank[4 + g % 2], QS[r.par][0:PARTS, s, qt:qt + 128],
                                         KS[r.par][0:PARTS, s, g, :], start=True, stop=True).then_inc(mx_mm, 1)

                    def spare(t, k):
                        what, ahead, s = misc[k]
                        r = t + ahead
                        if r.within(B):
                            misc_free(pe, t, k)
                            if what == "u2T":
                                pe.wait_ge(u2, r.b + 1)
                                for c_ in range(C):
                                    i = nc.tensor.transpose(MQ[:, c_, :], U2[r.par][:, c_, :], ID)
                                i.then_inc(u2T_mm, 1)
                            if what == "otr":
                                n = SETS * r.b + s
                                pe.wait_ge(o_v, n + 1)
                                for c_ in range(C):
                                    i = nc.tensor.transpose(MQ[:, c_, :], OSB[s % 2][:, 128 * c_:128 * c_ + 128], ID)
                                i.then_inc(otr_mm, 1)
                            if what == "mt":
                                pe.wait_ge(mx, SLOTS * G * r.b + C * G * (s + 1))
                                for c_ in range(C):
                                    i = nc.tensor.matmul(MQ[PARTS:STACK, c_, :], NM[r.par][:, s, c_, :], ID,
                                                         start=True, stop=True)
                                i.then_inc(mt_mm, 1)
                            if what in ("q", "k"):
                                pe.wait_ge(u2Tv, r.b + 1)
                                nc.tensor.matmul(MISC, WB[:, 0 if what == "q" else 1, :], U2T[r.par][:, :],
                                                 start=True, stop=True).then_inc(q_mm if what == "q" else k_mm, 1)
                            if what == "v":
                                for c_ in range(C):
                                    i = nc.tensor.matmul(MQ[:, c_, :], U2T[r.par][:, 128 * c_:128 * c_ + 128],
                                                         WB[:, 2, :], start=True, stop=True)
                                i.then_inc(v_mm, 1)
                            if what == "att":
                                pe.wait_ge(atb, r.b + 1)
                                for c_ in range(C):
                                    i = nc.tensor.transpose(MQ[:, c_, :], ATB[r.par][:, c_, :], ID)
                                i.then_inc(att_mm, 1)
                            if what == "wo":
                                pe.wait_ge(att_v, r.b + 1)
                                for c_ in range(C):
                                    i = nc.tensor.matmul(MQ[:, c_, :], ATT[r.par][:, 128 * c_:128 * c_ + 128],
                                                         WB[:, 3, :], start=True, stop=True)
                                i.then_inc(o_mm, 1)
                            if what == "u3T":
                                pe.wait_ge(u3, C * (r.b + 1))
                                for c_ in range(C):
                                    i = nc.tensor.transpose(MQ[:, c_, :], U3[r.par][:, c_, :], ID)
                                i.then_inc(u3T_mm, 1)
                            if what == "aff":
                                pe.wait_ge(u3Tv, r.b + 1)
                                for c_ in range(C):
                                    i = nc.tensor.matmul(MISC[:, E * c_:E * c_ + E],
                                                         U3T[r.par][:, 128 * c_:128 * c_ + 128], CENT,
                                                         start=True, stop=True)
                                i.then_inc(aff_mm, 1)

                    def step(t):
                        for k in range(SLOTS):
                            scores(t, k, 0)
                            rowwise(t, k, 0)
                            scores(t, k, 1)
                            rowwise(t, k, 1)
                            r, kk = (t, k - 1) if k else (t + -1, SLOTS - 1)
                            if r.within(B):
                                products(r, kk)
                            rowwise(t, k, 2)
                            spare(t, k)
                            rowwise(t, k, 3)
                    rounds(pe, FIRST, LO, HI, END, step)

        def finish():
            with ExitStack() as c:
                IDX = [sb(f"z_IDX{i}", [128, C], I32, c=c) for i in range(2)]
                GA = [sb(f"z_GA{i}", [128, C, D], c=c) for i in range(2)]
                idx_here, done = sem("z_idx"), sem("z_done")
                gath = [sem(f"z_gath{i}") for i in range(2)]
                stored = sem("z_stored")
                block = c.enter_context(nc.Block())

                @block.gpsimd
                def _(pool):
                    def gather(r):
                        wait(pool, done, 1, r.b - 2)
                        apart(pool, idx_here, r.b + 1, pool_passed)
                        for c_ in range(C):
                            nc.gpsimd.indirect_dma_start(
                                GA[r.par][:, c_, :], None, sorted_y,
                                bass.IndirectOffsetOnAxis(ap=IDX[r.par][:, c_:c_ + 1], axis=0)
                            ).then_inc(gath[r.par], 16)
                    rounds(pool, 0, 2, 8, 7, gather)

                @block.vector
                def _(dve):
                    def index(r):
                        apart(dve, gath[r.par], 16 * C * r.half, dve_passed)
                        nc.vector.tensor_copy(IDX[r.par][:, :], POS[:, ds(C * r.b, C)]).then_inc(idx_here, 1)

                    def add(r):
                        if (r + 1).within(B):
                            index(r + 1)
                        dve.wait_ge(gath[r.par], 16 * C * (r.half + 1))
                        for c_ in range(C):
                            xs = X[:, ds(C * r.b + c_, 1), :].rearrange("p o d -> p (o d)")
                            i = nc.vector.scalar_tensor_tensor(xs, GA[r.par][:, c_, :],
                                                               ALPHA[:, ds(C * r.b + c_, 1)], xs,
                                                               ALU.mult, ALU.add)
                        i.then_inc(done, 1)
                    index(Round(0, 0, 0))
                    rounds(dve, 0, 1, 7, 7, add)

                @block.sync
                def _(sp):
                    def store(r):
                        sp.wait_ge(done, r.b + 1)
                        sp.dma_start(out[ds(r.b, 1), :, :].rearrange("o (c p) d -> p (o c) d", p=128),
                                     X[:, ds(C * r.b, C), :]).then_inc(stored, 16)
                    rounds(sp, 0, 2, 8, 7, store)
                    sp.wait_ge(stored, 16 * B)

        def dump(n, parts):
            with ExitStack() as cd:
                dd = sem("dd")
                cd.enter_context(nc.allow_non_contiguous_dma(reason="debug"))
                block = cd.enter_context(nc.Block())

                @block.sync
                def _(sp):
                    for o, i in parts:
                        sp.dma_start(o, i).then_inc(dd, 16)
                    sp.wait_ge(dd, 16 * len(parts))
        with nc.Block() as block:
            @block.gpsimd
            def _(pool):
                for s in held:
                    pool.sem_clear(s)
        held = None
        early.close()
        route(1, W1T, W2T)
        if upto == 2:
            return dump(2, [(dbg[0], sorted_x[0:4096, :]), (dbg[1, :, 0:1].rearrange("(t p) o -> p (t o)", p=128), ALPHA[:, :]),
                            (dbg[1, 0:1, 64:103], TE[:, :].bitcast(F32)),
                            (dbg[2, :, 0:1].rearrange("(t p) o -> p (t o)", p=128), POS[:, :].bitcast(F32))])
        experts(1, W1T, W2T)
        weights.close()
        if upto == 3:
            return dump(3, [(dbg[0], sorted_y[0:4096, :]), (dbg[1, 0:896], sorted_y[4096:, :]),
                            (dbg[2, :, 0:1].rearrange("(t p) o -> p (t o)", p=128), POS[:, :].bitcast(F32))])
        attention()
        if upto == 4:
            return dump(4, [(dbg[k].rearrange("(t p) d -> p t d", p=128), t) for k, t in
                            enumerate((X[:, :, :], XH[:, :, :]))] +
                        [(dbg[2, :, 0:8].rearrange("(t p) d -> p t d", p=128), AFF[:, :, :])])
        W1T = sb("W1T2", [128, E, F])
        W2T = sb("W2T2", [128, E, FC, D])
        route(2, W1T, W2T)
        experts(2, W1T, W2T)
        finish()


_INS = ['L0_attn_a_x', 'L0_attn_a_Wq', 'L0_attn_a_bq', 'L0_attn_a_Wk', 'L0_attn_a_bk', 'L0_attn_a_Wv',
        'L0_attn_a_bv', 'L0_attn_a_Wo', 'L0_attn_a_bo', 'L0_attn_a_decay_param', 'L0_attn_b_Wq', 'L0_attn_b_bq',
        'L0_attn_b_Wk', 'L0_attn_b_bk', 'L0_attn_b_Wv', 'L0_attn_b_bv', 'L0_attn_b_Wo', 'L0_attn_b_bo',
        'L0_attn_b_head_mask', 'L0_ffn_centroids', 'L0_ffn_ln_g', 'L0_ffn_ln_b', 'L0_ffn_w1', 'L0_ffn_b1',
        'L0_ffn_w2', 'L0_ffn_b2']


def shape_constants(np):
    con = np.zeros((128, 1080), np.float32)
    con[:, 0:128] = np.eye(128)
    i = np.arange(128)
    con[:, 128:256] = i[:, None] < i[None, :]
    con[:, 256:385] = np.arange(129)[None, :] == i[:, None] + 1
    con[:, 385] = 1
    con[:, 514:522] = E - np.arange(E)
    reset = np.ones((E, NT), np.float32)
    reset[:, 0] = 0
    con[:, 522:778] = reset.reshape(-1)
    con[:, 778:810] = 128 * np.arange(NT)
    con[:, 810:849] = np.arange(TILES)
    con[:, 850:854] = EPS
    con[:, 854:858] = -0.5
    ids = np.tile(np.arange(TILES, dtype=np.float32), (1, 1))
    return con, ids


def kernel(**inputs):
    import numpy as _np
    import concourse.bacc as _bacc
    from concourse import mybir as _mybir
    from concourse.bass_utils import run_bass_kernel_spmd as _run

    nc = _bacc.Bacc("TRN2", target_bir_lowering=False, num_devices=1)
    arrays, args = {}, []
    con, ids = shape_constants(_np)
    named = [(n, _np.ascontiguousarray(inputs[n]).reshape(_np.shape(inputs[n]) or (1,))) for n in _INS] + [("consts", con), ("tile_ids", ids)]
    for name, a in named:
        arrays[f"in_{name}"] = a
        args.append(nc.dram_tensor(f"in_{name}", a.shape, _mybir.dt.from_np(a.dtype), kind="ExternalInput").ap())
    out = nc.dram_tensor("out", (B, S, D), F32, kind="ExternalOutput").ap()
    hybrid(nc, *args, out)
    r = _run(nc, [arrays], core_ids=[0])
    return r.results[0]["out"]
```

```python
import concourse.bass as bass
from concourse import mybir
from contextlib import ExitStack

F32 = mybir.dt.float32
F32R = mybir.dt.float32r
I32 = mybir.dt.int32
ALU = mybir.AluOpType
ACT = mybir.ActivationFunctionType
AX = mybir.AxisListType

D = 128
B, S = 8, 512
C = S // 128
NT = B * C
E, F = 8, 512
FC = F // 128
TILES = NT + E - 1
TOKENS = B * S
CAP = TOKENS + 128
SPARE = E * CAP
PADS = 2 * E - 1
ROW = D + 1
LINKS = 10
H, HD = 16, 8
G = 4
SETS = H // G
AUG = 32
EPS = 1e-5
SCALE = 1.0 / float(HD) ** 0.5


def ds(i, n):
    return bass.ds(i, n)


def wait(eng, sem, per, b):
    if isinstance(b, int) and b < 0:
        return
    eng.wait_ge(sem, per * (b + 1))


def at_least(eng, sem, value):
    if isinstance(value, int) and value <= 0:
        return
    eng.wait_ge(sem, value)


def apart(eng, sem, value, passed):
    if isinstance(value, int) and value <= 0:
        return
    eng.wait_ge(sem, value)
    eng.sem_inc(passed, 1)


class Round:

    def __init__(self, b, half, par):
        self.b, self.half, self.par = b, half, par

    def __add__(self, k):
        b = self.b + k
        return Round(b, self.half + (self.par + k) // 2, (self.par + k) % 2)

    def within(self, n):
        return not isinstance(self.b, int) or 0 <= self.b < n


def rounds(eng, first, loop_from, loop_to, last, body):
    def at(t):
        return Round(t, t // 2, t % 2)
    for t in range(first, loop_from):
        body(at(t))
    if loop_to > loop_from:
        turns = (loop_to - loop_from) // 2
        lo = loop_from // 2
        assert loop_from + 2 * turns == loop_to
        with eng.Fori(lo, lo + turns) as i:
            for h in range(2):
                k = loop_from % 2 + h
                body(Round(2 * i + k, i + k // 2, k % 2))
    for t in range(loop_to, last + 1):
        body(at(t))


def hybrid(nc, x_in, Wq_a, bq_a, Wk_a, bk_a, Wv_a, bv_a, Wo_a, bo_a, decay,
           Wq_b, bq_b, Wk_b, bk_b, Wv_b, bv_b, Wo_b, bo_b, head_mask,
           cent, ln_g, ln_b, w1, b1, w2, b2, consts, tile_ids, out, dbg=None, upto=99):
    ctx = ExitStack()
    with ctx:
        def sb(name, shape, dt=F32, c=ctx):
            return c.enter_context(nc.sbuf_tensor(name, shape, dt))

        early = ExitStack()
        held = []

        def sem(name):
            if held is None:
                return ctx.enter_context(nc.semaphore(name))
            held.append(early.enter_context(nc.semaphore(name)))
            return held[-1]

        soft = {n: ctx.enter_context(nc.semaphore(n)) for n in
                ("u_kept0 u_kept1 pa_sent0 pa_sent1 pb_sent0 pb_sent1 r1_padded r2_padded "
                 "f1_yout0 f1_yout1 f1_yout2 f2_yout0 f2_yout1 f2_yout2").split()}
        PS = ctx.enter_context(nc.psum_tensor("PS", [128, 8, 512], F32))
        bank = [PS[:, i, :] for i in range(8)]
        quad = [b_.rearrange("p (c d) -> p c d", c=C) for b_ in bank]

        sorted_x = nc.dram_tensor("sorted_x", [SPARE + 128 * (E - 1), ROW], F32, kind="Internal").ap()
        y_tok = nc.dram_tensor("y_tok", [TOKENS + 128 * PADS, D], F32, kind="Internal").ap()

        dve_passed, pool_passed, sp_passed = (ctx.enter_context(nc.semaphore(n))
                                              for n in ("dve_passed", "pool_passed", "sp_passed"))
        X = sb("X", [128, NT, D])
        AFF = sb("AFF", [128, NT, E])
        ALPHA = sb("ALPHA", [128, NT])
        TE = sb("TE", [1, TILES], I32)
        TROW = sb("TROW", [1, TILES], I32)
        IDS = sb("IDS", [128, TILES], I32)
        CARRY = sb("CARRY", [128, E])
        PADROW = sb("PADROW", [128, PADS, ROW])
        NB1 = sb("NB1", [128, E, FC])
        C2 = sb("C2", [128, E, D])
        CON = sb("CON", [128, 672])
        ID = CON[:, 0:128]
        LOW = CON[:, 128:256]
        IMP = CON[:, 256:385]
        IMP0 = CON[:, 385:514]
        CODE = CON[:, 514:522]
        STEPS = CON[:, 522:554]
        TOK = CON[:, 554:586]
        ROW39 = CON[:, 586:625]
        EPS1 = CON[:, 625:629]
        MHALF = CON[:, 629:633]
        REGION = CON[:, 633:641]
        JUMP = CON[:, 641:649]
        PART = CON[:, 649:657]
        PADID = CON[:, 657:657 + PADS]
        ONES = sb("ONES", [128, 128])
        COL = sb("COL", [128, 61])
        LNG, LNB, B1T, CENT = COL[:, 1:9], COL[:, 9:17], COL[:, 17:49], COL[:, 49:57]
        MASKH, BQA, BKA, BQB, BKB = (COL[:, k:k + 1] for k in (0, 57, 58, 59, 60))
        WA = sb("WA", [128, 4, D])
        WB = sb("WB", [128, 4, D])
        REP = sb("REP", [128, 4, D])
        DEC = sb("DEC", [128, 129])
        DROW = sb("DROW", [128, 129])
        BVA, BOA, BVB, BOB = (REP[:, k, :] for k in range(4))

        W2T = sb("W2T", [128, E, FC, D])
        w1_kept = nc.dram_tensor("w1_kept", [E, 128, F], F32, kind="Internal").ap()

        class Placing:

            def __init__(self, tag, c):
                t = "p" + tag + "_"
                self.AFFB = sb(t + "AFFB", [128, C, E], c=c)
                self.AM, self.KM, self.POSF = (sb(t + n, [128, C], c=c) for n in ("AM", "KM", "POSF"))
                self.EQ, self.KEY, self.OH, self.W, self.SEL = (sb(t + n, [128, C, E], c=c)
                                                                for n in ("EQ", "KEY", "OH", "W", "SEL"))
                self.IDX = [sb(f"{t}IDX{i}", [128, C], I32, c=c) for i in range(2)]
                self.XS = [sb(f"{t}XS{i}", [128, C, ROW], c=c) for i in range(2)]
                self.kept, self.link, self.ranked, self.ids = (sem(t + n) for n in ("kept", "link", "ranked", "ids"))
                self.sent = [soft[f"{t}sent{i}"] for i in range(2)]
                self.free = [sem(f"{t}free{i}") for i in range(2)]

            def start(self, pool):
                for f in self.free:
                    pool.sem_inc(f, 1)

            def wait_free(self, eng, r):
                eng.wait_ge(self.free[r.par], r.half + 1)

            def keep(self, act, r, affv):
                act.wait_ge(affv, r.b + 1)
                nc.scalar.copy(AFF[:, ds(C * r.b, C), :], self.AFFB[:, :, :]).then_inc(self.kept, 1)

            def number(self, act, r):
                self.wait_free(act, r)
                nc.scalar.copy(self.XS[r.par][:, :, D:ROW], TOK[:, ds(C * r.b, C)][:, :, None]).then_inc(self.ids, 1)

            def choose(self, dve, r, steps, affv=None):
                wide = [128, C, E]
                code = CODE[:, None, :].broadcast_to(wide)
                for n in steps:
                    if n == 0:
                        dve.wait_ge(affv, r.b + 1)
                        i = nc.vector.tensor_reduce(self.AM[:, :], self.AFFB[:, :, :], axis=AX.X, op=ALU.max)
                    else:
                        dve.wait_ge(self.link, LINKS * r.b + n)
                    if n == 1:
                        i = nc.vector.tensor_tensor(self.EQ[:, :, :], self.AFFB[:, :, :],
                                                    self.AM[:, :, None].broadcast_to(wide), ALU.is_equal)
                    if n == 2:
                        i = nc.vector.tensor_tensor(self.KEY[:, :, :], self.EQ[:, :, :], code, ALU.mult)
                    if n == 3:
                        i = nc.vector.tensor_reduce(self.KM[:, :], self.KEY[:, :, :], axis=AX.X, op=ALU.max)
                    if n == 4:
                        i = nc.vector.tensor_tensor(self.OH[:, :, :], code, self.KM[:, :, None].broadcast_to(wide),
                                                    ALU.is_equal)
                    i.then_inc(self.link, 1)

            def rank(self, pe, r, ranks):
                pe.wait_ge(self.link, LINKS * r.b + 5)
                oh = self.OH[:, :, :].rearrange("p c e -> p (c e)")
                nc.tensor.matmul(ranks[:, 0:C * E], LOW, oh, start=True, stop=False)
                for n in range(1, C):
                    nc.tensor.matmul(ranks[:, E * n:C * E], ONES[:, :], oh[:, 0:E * (C - n)],
                                     start=False, stop=(n == C - 1))
                for n in range(C):
                    i = nc.tensor.matmul(ranks[:, C * E:(C + 1) * E], ONES[:, :], oh[:, E * n:E * n + E],
                                         start=(n == 0), stop=(n == C - 1))
                i.then_inc(self.ranked, 1)

            def place(self, dve, r, ranks):
                dve.wait_ge(self.ranked, r.b + 1)
                dve.wait_ge(self.link, LINKS * r.b + 5)
                nc.vector.tensor_tensor(self.W[:, :, :], ranks[:, 0:C * E].rearrange("p (c e) -> p c e", c=C),
                                        CARRY[:, None, :].broadcast_to([128, C, E]), ALU.add).then_inc(self.link, 1)
                dve.wait_ge(self.link, LINKS * r.b + 6)
                nc.vector.tensor_tensor(self.SEL[:, :, :], self.W[:, :, :], self.OH[:, :, :],
                                        ALU.mult).then_inc(self.link, 1)
                nc.vector.tensor_tensor(CARRY[:, :], ranks[:, C * E:(C + 1) * E], CARRY[:, :],
                                        ALU.add).then_inc(self.link, 1)
                dve.wait_ge(self.link, LINKS * r.b + 7)
                nc.vector.tensor_reduce(self.POSF[:, :], self.SEL[:, :, :], axis=AX.X,
                                        op=ALU.add).then_inc(self.link, 1)
                dve.wait_ge(self.link, LINKS * r.b + 9)
                self.wait_free(dve, r)
                nc.vector.tensor_copy(self.IDX[r.par][:, :], self.POSF[:, :]).then_inc(self.link, 1)

            def send(self, pool, r):
                pool.wait_ge(self.link, LINKS * (r.b + 1))
                apart(pool, self.ids, r.b + 1, pool_passed)
                for c_ in range(C):
                    nc.gpsimd.indirect_dma_start(
                        sorted_x, bass.IndirectOffsetOnAxis(ap=self.IDX[r.par][:, c_:c_ + 1], axis=0),
                        self.XS[r.par][:, c_, :], None).then_inc(self.sent[r.par], 16)

            def release(self, pool, r):
                pool.wait_ge(self.sent[r.par], 16 * C * (r.half + 1))
                pool.sem_inc(self.free[r.par], 1)

        with ExitStack() as c0:
            W1N = sb("W1N", [128, 2, FC, D], c=c0)
            W2N = sb("W2N", [128, 2, F], c=c0)
            W1U = sb("W1U", [128, 2, F], c=c0)
            W1G = sb("W1G", [128, 2, F], c=c0)
            B1E = sb("B1E", [128, E, FC], c=c0)
            B1R = sb("B1R", [128, 2, FC, D], c=c0)
            B2R = sb("B2R", [128, E, D], c=c0)
            SM = sb("SMALL", [61, D], c=c0)
            HM = sb("HM", [1, H], c=c0)
            u_mask, u_maskv = sem("u_mask"), sem("u_maskv")
            WBN = sb("WBN", [128, 4, D], c=c0)
            DT = sb("DT", [128, 4], c=c0)
            u_con, u_small, u_w, u_rep, u_b2 = (sem("u_" + n) for n in ("con", "small", "w", "rep", "b2"))
            u_w1n = [sem(f"u_w1n{i}") for i in range(2)]
            u_w2n = [sem(f"u_w2n{i}") for i in range(2)]
            u_col, u_colv, u_wbt, u_wbv = sem("u_col"), sem("u_colv"), sem("u_wbt"), sem("u_wbv")
            u_w1t, u_w1u, u_w1g, u_w2t, u_w2v = (sem("u_" + n) for n in ("w1t", "w1u", "w1g", "w2t", "w2v"))
            u_b1, u_b1e, u_b1r, u_c2, u_c2v = (sem("u_" + n) for n in ("b1", "b1e", "b1r", "c2", "c2v"))
            u_dec, u_e, u_ones, u_zero, u_xz = (sem("u_" + n) for n in ("dec", "e", "ones", "zero", "xz"))
            u_kept, u_carry, u_pad = [soft[f"u_kept{i}"] for i in range(2)], sem("u_carry"), sem("u_pad")
            block = c0.enter_context(nc.Block())

            @block.sync
            def _(sp):
                sp.dma_start(CON[:, :], consts).then_inc(u_con, 16)
                sp.dma_start(HM[:, :], head_mask[None, :]).then_inc(u_mask, 16)
                rows = [(ln_g, 1, 9), (ln_b, 9, 17), (b1.rearrange("e (c f) -> (e c) f", c=FC), 17, 49),
                        (cent, 49, 57), (bq_a[None, :], 57, 58), (bk_a[None, :], 58, 59),
                        ]
                for src, a, z in rows:
                    sp.dma_start(SM[a:z, :], src).then_inc(u_small, 16)
                with nc.allow_non_contiguous_dma(reason="256 numbers"):
                    for src, a in ((bq_b, 59), (bk_b, 60)):
                        sp.dma_start(SM[a:a + 1, :].rearrange("o (x s) -> o x s", s=SETS),
                                     src[None, :].rearrange("o (s x) -> o x s", s=SETS)).then_inc(u_small, 16)
                for k, w in enumerate((Wq_b, Wk_b, Wv_b, Wo_b)):
                    sp.dma_start(WBN[:, k, :], w).then_inc(u_w, 16)

                def load(r):
                    wait(sp, u_w1t, 1, r.b - 2)
                    sp.dma_start(W1N[:, r.par, :, :],
                                 w1[ds(r.b, 1), :, :].rearrange("e (c p) d -> p (e c) d", p=128)
                                 ).then_inc(u_w1n[r.par], 16)
                    wait(sp, u_w2t, 1, r.b - 2)
                    sp.dma_start(W2N[:, r.par, :],
                                 w2[ds(r.b, 1), :, :].rearrange("e d f -> (e d) f")).then_inc(u_w2n[r.par], 16)
                rounds(sp, 0, 2, 8, 7, load)
                sp.wait_ge(u_pad, 1)
                sp.dma_start(sorted_x[SPARE:SPARE + 128 * (E - 1), :].rearrange("(n p) d -> p n d", p=128),
                             PADROW[:, E:PADS, :]).then_inc(u_xz, 16)
                sp.wait_ge(u_xz, 16)

            @block.scalar
            def _(act):
                for k, w in enumerate((Wq_a, Wk_a, Wv_a, Wo_a)):
                    act.dma_start(WA[:, k, :], w).then_inc(u_w, 16)
                for k, v in enumerate((bv_a, bo_a, bv_b, bo_b)):
                    act.dma_start(REP[:, k, :], v[None, :].broadcast_to([128, D])).then_inc(u_rep, 16)
                act.dma_start(B2R[:, :, :], b2[None, :, :].broadcast_to([128, E, D])).then_inc(u_b2, 16)
                act.dma_start(DT[:, 0:1], decay[None, :].broadcast_to([128, 1])).then_inc(u_rep, 16)
                act.wait_ge(u_rep, 80)
                nc.scalar.activation(DT[:, 1:2], DT[:, 0:1], ACT.Exp, scale=-1.0).then_inc(u_e, 1)
                act.wait_ge(u_wbt, 1)
                for k in range(2):
                    nc.scalar.copy(WB[:, k, :].rearrange("p (g d s) -> p g s d", g=G, s=SETS),
                                   quad[1][:, k, :].rearrange("p (s g d) -> p g s d", g=G, s=SETS))
                nc.scalar.copy(WB[:, 2, :], quad[1][:, 2, :]).then_inc(u_wbv, 1)
                act.wait_ge(u_colv, 1)
                nc.scalar.mul(WB[:, 3, :], quad[1][:, 3, :], MASKH).then_inc(u_wbv, 1)

                def take(r):
                    act.wait_ge(u_w1t, r.b + 1)
                    wait(act, u_b1, 1, r.b - 2)
                    wait(act, u_w1g, 1, r.b - 2)
                    nc.scalar.copy(W1U[:, r.par, :], bank[r.par][:, :]).then_inc(u_w1u, 1)
                    act.wait_ge(u_w2t, r.b + 1)
                    nc.scalar.copy(W2T[:, ds(r.b, 1), :, :].rearrange("p e c d -> p (e c) d"),
                                   quad[2 + r.par]).then_inc(u_w2v, 1)
                rounds(act, 0, 2, 8, 7, take)

            @block.gpsimd
            def _(pool):
                nc.gpsimd.memset(ONES[:, :], 1.0).then_inc(u_ones, 1)
                pool.wait_ge(u_mask, 16)
                nc.gpsimd.tensor_copy(SM[0:1, :].rearrange("o (h d) -> o h d", h=H),
                                      HM[:, :, None].broadcast_to([1, H, HD])).then_inc(u_maskv, 1)
                nc.gpsimd.memset(PADROW[:, :, 0:D], 0.0).then_inc(u_zero, 1)
                pool.wait_ge(u_con, 16)
                nc.gpsimd.tensor_copy(PADROW[:, :, D:ROW], PADID[:, :, None]).then_inc(u_pad, 1)
                nc.gpsimd.tensor_copy(CARRY[:, :], REGION).then_inc(u_carry, 1)

                def keep(r):
                    apart(pool, u_w1g, r.b + 1, pool_passed)
                    nc.gpsimd.dma_start(w1_kept[ds(r.b, 1), :, :].rearrange("e p f -> (e p) f"),
                                        W1G[:, r.par, :]).then_inc(u_kept[r.par], 16)
                rounds(pool, 0, 2, 8, 7, keep)
                for i in range(2):
                    pool.wait_ge(u_kept[i], 16 * E // 2)

            @block.vector
            def _(dve):
                dve.wait_ge(u_col, 1)
                nc.vector.tensor_copy(COL[:, :], bank[0][:, 0:61]).then_inc(u_colv, 1)
                dve.wait_ge(u_e, 1)
                nc.vector.tensor_scalar_add(DT[:, 2:3], DT[:, 1:2], 1.0).then_inc(u_dec, 1)
                dve.wait_ge(u_dec, 1)
                nc.vector.reciprocal(DT[:, 3:4], DT[:, 2:3]).then_inc(u_dec, 1)
                dve.wait_ge(u_dec, 2)
                dve.wait_ge(u_con, 16)
                decays = DT[:, 3:4].broadcast_to([128, 129])
                nc.vector.tensor_tensor_scan(DEC[:, :], decays, IMP, 0.0, ALU.mult, ALU.add)
                nc.vector.tensor_tensor_scan(DROW[:, :], decays, IMP0, 0.0, ALU.mult, ALU.add).then_inc(u_dec, 1)
                dve.wait_ge(u_b2, 16)

                def fold(r):
                    dve.wait_ge(u_w1u, r.b + 1)
                    dve.wait_ge(u_colv, 1)
                    at_least(dve, u_kept[r.par], 16 * r.half)
                    nc.vector.tensor_scalar(W1G[:, r.par, :],
                                            W1U[:, r.par, :], LNG[:, ds(r.b, 1)], None,
                                            ALU.mult).then_inc(u_w1g, 1)
                    dve.wait_ge(u_b1, r.b + 1)
                    b1e = B1E[:, ds(r.b, 1), :].rearrange("p e c -> p (e c)")
                    nc.vector.tensor_tensor(b1e, bank[4 + r.par][:, 0:FC], B1T[:, ds(FC * r.b, FC)],
                                            ALU.add).then_inc(u_b1e, 1)
                    dve.wait_ge(u_b1e, r.b + 1)
                    apart(dve, u_c2, r.b - 1, dve_passed)
                    nc.vector.tensor_copy(B1R[:, r.par, :, :],
                                          b1e[:, :, None].broadcast_to([128, FC, D])).then_inc(u_b1r, 1)
                    nc.vector.tensor_scalar(NB1[:, ds(r.b, 1), :].rearrange("p e c -> p (e c)"), b1e, -1.0, None,
                                            ALU.mult)
                    dve.wait_ge(u_c2, r.b + 1)
                    nc.vector.tensor_tensor(C2[:, ds(r.b, 1), :].rearrange("p e d -> p (e d)"),
                                            bank[6 + r.par][:, 0:D],
                                            B2R[:, ds(r.b, 1), :].rearrange("p e d -> p (e d)"),
                                            ALU.add).then_inc(u_c2v, 1)
                rounds(dve, 0, 2, 8, 7, fold)

            @block.tensor
            def _(pe):
                pe.wait_ge(u_con, 16)
                pe.wait_ge(u_small, 128)
                pe.wait_ge(u_maskv, 1)
                nc.tensor.transpose(bank[0][:, 0:61], SM[:, :], ID[0:61, 0:61]).then_inc(u_col, 1)
                pe.wait_ge(u_w, 128)
                for k in range(4):
                    m = nc.tensor.transpose(quad[1][:, k, :], WBN[:, k, :], ID)
                m.then_inc(u_wbt, 1)
                pe.wait_ge(u_colv, 1)
                pe.wait_ge(u_wbv, 2)
                pe.wait_ge(u_ones, 1)

                def turn(r):
                    pe.wait_ge(u_w1n[r.par], 16 * (r.half + 1))
                    wait(pe, u_w1u, 1, r.b - 2)
                    for k in range(FC):
                        m = nc.tensor.transpose(bank[r.par][:, 128 * k:128 * k + 128], W1N[:, r.par, k, :], ID)
                    m.then_inc(u_w1t, 1)
                    pe.wait_ge(u_w2n[r.par], 16 * (r.half + 1))
                    wait(pe, u_w2v, 1, r.b - 2)
                    for k in range(FC):
                        m = nc.tensor.transpose(quad[2 + r.par][:, k, :],
                                                W2N[:, r.par, 128 * k:128 * k + 128], ID)
                    m.then_inc(u_w2t, 1)
                    pe.wait_ge(u_w1u, r.b + 1)
                    wait(pe, u_b1e, 1, r.b - 2)
                    for k in range(FC):
                        m = nc.tensor.matmul(bank[4 + r.par][:, k:k + 1], W1U[:, r.par, 128 * k:128 * k + 128],
                                             LNB[:, ds(r.b, 1)], start=True, stop=True)
                    m.then_inc(u_b1, 1)
                    pe.wait_ge(u_b1r, r.b + 1)
                    pe.wait_ge(u_w2v, r.b + 1)
                    wait(pe, u_c2v, 1, r.b - 2)
                    for k in range(FC):
                        m = nc.tensor.matmul(bank[6 + r.par][:, 0:D], B1R[:, r.par, k, :],
                                             W2T[:, ds(r.b, 1), k, :].rearrange("p e d -> p (e d)"),
                                             start=(k == 0), stop=(k == FC - 1))
                    m.then_inc(u_c2, 1)
                rounds(pe, 0, 2, 8, 7, turn)

        with ExitStack() as c1:
            st = [sb(f"a_st{i}", [128, C, 6], c=c1) for i in range(2)]
            mv = [sb(f"a_mv{i}", [128, C, 2], c=c1) for i in range(2)]
            st1 = [sb(f"a_st1{i}", [128, C, 6], c=c1) for i in range(2)]
            mv1 = [sb(f"a_mv1{i}", [128, C, 2], c=c1) for i in range(2)]
            tmp = [sb(f"a_tmp{i}", [128, 8, C], c=c1) for i in range(2)]
            U = [sb(f"a_U{i}", [128, C, D], c=c1) for i in range(2)]
            UT = [sb(f"a_UT{i}", [128, S], c=c1) for i in range(2)]
            QT = [sb(f"a_QT{i}", [128, S], c=c1) for i in range(2)]
            QD = [sb(f"a_QD{i}", [128, C, 128], c=c1) for i in range(2)]
            KE = [sb(f"a_KE{i}", [128, S], c=c1) for i in range(2)]
            KR = [sb(f"a_KR{i}", [128, S], c=c1) for i in range(2)]
            KT = [sb(f"a_KT{i}", [128, S], c=c1) for i in range(2)]
            V = [sb(f"a_V{i}", [128, C, D], c=c1) for i in range(2)]
            KP = [sb(f"a_KP{i}", [128, C, D], c=c1) for i in range(2)]
            SM_ = [sb(f"a_SM{i}", [128, C, 128], c=c1) for i in range(2)]
            MEM = [sb(f"a_MEM{i}", [128, C - 1, D], c=c1) for i in range(2)]
            RT = [sb(f"a_RT{i}", [128, S], c=c1) for i in range(2)]
            U1 = [sb(f"a_U1{i}", [128, C, D], c=c1) for i in range(2)]
            U1T = [sb(f"a_U1T{i}", [128, S], c=c1) for i in range(2)]
            x_here = [sem(f"a_x_here{i}") for i in range(2)]
            (stats, aggr, veps, rstd, u_done, xbo, uT, uTv, q_mm, qv, qd, k_mm, ke, kr, kt, v_mm, vv,
             s_mm, sm, kT_mm, kp, U_mm, mem, r_mm, rtv, o_mm, x1, stats1, aggr1, chain1, rstd1, u1, base,
             u1T_mm, u1Tv, aff_mm, affv) = (sem("a_" + n) for n in (
                 "stats aggr veps rstd u xbo uT uTv q qv qd k ke kr kt v vv s sm kT kp U mem r rtv o x1 "
                 "stats1 aggr1 chain1 rstd1 u1 base u1T u1Tv aff affv").split())
            block = c1.enter_context(nc.Block())
            LO, HI, END = 3, 7, 10
            placing = Placing("a", c1)
            RANKS = bank[7][:, 0:(C + 1) * E]
            AFFP = bank[6][:, (C - 1) * D:(C - 1) * D + C * E]

            @block.sync
            def _(sp):
                def load(r):
                    wait(sp, x_here[r.par], 16, r.half - 1)
                    sp.dma_start(X[:, ds(C * r.b, C), :],
                                 x_in[ds(r.b, 1), :, :].rearrange("o (c p) d -> p (o c) d", p=128)
                                 ).then_inc(x_here[r.par], 16)
                rounds(sp, 0, 2, 8, 7, load)

            @block.vector
            def _(dve):
                def xs(r, c):
                    return X[:, ds(C * r.b + c, 1), :].rearrange("p o d -> p (o d)")

                def input_stats(r):
                    apart(dve, x_here[r.par], 16 * (r.half + 1), dve_passed)
                    for c in range(C):
                        i = nc.vector.bn_stats(st[r.par][:, c, :], xs(r, c))
                    i.then_inc(stats, 1)
                    dve.wait_ge(stats, r.b + 1)
                    apart(dve, rstd, r.b - 1, dve_passed)
                    for c in range(C):
                        i = nc.vector.bn_aggr(mv[r.par][:, c, :], st[r.par][:, c, :])
                    i.then_inc(aggr, 1)

                def normalise(r):
                    dve.wait_ge(rstd, r.b + 1)
                    wait(dve, uT, 1, r.b - 2)
                    for c in range(C):
                        i = nc.vector.tensor_scalar(U[r.par][:, c, :], xs(r, c), mv[r.par][:, c, 0:1],
                                                    tmp[r.par][:, 0, c:c + 1], ALU.subtract, ALU.mult)
                    i.then_inc(u_done, 1)

                def residual(r):
                    dve.wait_ge(o_mm, r.b + 1)
                    dve.wait_ge(xbo, r.b + 1)
                    nc.vector.tensor_tensor(X[:, ds(C * r.b, C), :], quad[7], X[:, ds(C * r.b, C), :],
                                            ALU.add).then_inc(x1, 1)
                    apart(dve, x1, r.b + 1, dve_passed)
                    for c in range(C):
                        i = nc.vector.bn_stats(st1[r.par][:, c, :], xs(r, c))
                    i.then_inc(stats1, 1)
                    dve.wait_ge(stats1, r.b + 1)
                    apart(dve, rstd1, r.b, dve_passed)
                    for c in range(C):
                        i = nc.vector.bn_aggr(mv1[r.par][:, c, :], st1[r.par][:, c, :])
                    i.then_inc(aggr1, 1)

                def ffn_inputs(r):
                    dve.wait_ge(rstd1, r.b + 1)
                    placing.wait_free(dve, r)
                    wait(dve, u1T_mm, 1, r.b - 1)
                    wait(dve, base, 1, r.b - 1)
                    for c in range(C):
                        i = nc.vector.tensor_scalar(U1[r.par][:, c, :], xs(r, c), mv1[r.par][:, c, 0:1],
                                                    tmp[r.par][:, 2, c:c + 1], ALU.subtract, ALU.mult)
                        nc.vector.tensor_scalar(placing.XS[r.par][:, c, 0:D],
                                                xs(r, c), mv1[r.par][:, c, 0:1],
                                                tmp[r.par][:, 7, c:c + 1], ALU.subtract, ALU.mult
                                                ).then_inc(u1, 1)

                def step(t):
                    f, m, z, y = t, t + -1, t + -2, t + -3
                    if z.within(B):
                        residual(z)
                    if y.within(B):
                        placing.choose(dve, y, (0, 1), affv)
                    if m.within(B):
                        dve.wait_ge(s_mm, m.b + 1)
                        wait(dve, r_mm, 1, m.b - 2)
                        nc.vector.tensor_tensor(SM_[m.par][:, :, :], quad[4],
                                                DEC[:, None, 0:128].broadcast_to([128, C, 128]),
                                                ALU.mult).then_inc(sm, 1)
                    if y.within(B):
                        placing.choose(dve, y, (2,))
                    if (t + 1).within(B):
                        input_stats(t + 1)
                    if y.within(B):
                        placing.choose(dve, y, (3,))
                    if m.within(B):
                        dve.wait_ge(U_mm, m.b + 1)
                        for c in range(C - 1):
                            if c == 0:
                                i = nc.vector.tensor_copy(MEM[m.par][:, 0, :], quad[6][:, 0, :])
                            else:
                                dve.wait_ge(mem, (C - 1) * m.b + c)
                                i = nc.vector.scalar_tensor_tensor(
                                    MEM[m.par][:, c, :], MEM[m.par][:, c - 1, :], DROW[:, 128:129],
                                    quad[6][:, c, :], ALU.mult, ALU.add)
                            i.then_inc(mem, 1)
                    if y.within(B):
                        placing.choose(dve, y, (4,))
                    if f.within(B):
                        dve.wait_ge(ke, f.b + 1)
                        dve.wait_ge(kr, f.b + 1)
                        wait(dve, kT_mm, 1, f.b - 2)
                        nc.vector.scalar_tensor_tensor(KT[f.par][:, :], KE[f.par][:, :], 1.0, KR[f.par][:, :],
                                                       ALU.min, ALU.add).then_inc(kt, 1)
                        dve.wait_ge(v_mm, f.b + 1)
                        nc.vector.tensor_tensor(V[f.par][:, :, :], quad[3],
                                                BVA[:, None, :].broadcast_to([128, C, D]), ALU.add).then_inc(vv, 1)
                    if y.within(B):
                        placing.place(dve, y, RANKS)
                    if z.within(B):
                        ffn_inputs(z)
                    if (t + 1).within(B):
                        normalise(t + 1)
                    if z.within(B):
                        dve.wait_ge(aff_mm, z.b + 1)
                        wait(dve, placing.kept, 1, z.b - 1)
                        nc.vector.tensor_copy(placing.AFFB[:, :, :],
                                              AFFP.rearrange("p (c e) -> p c e", c=C)).then_inc(affv, 1)
                input_stats(Round(0, 0, 0))
                normalise(Round(0, 0, 0))
                rounds(dve, 0, LO, HI, END, step)

            @block.gpsimd
            def _(pool):
                def input_rstd(r):
                    pool.wait_ge(aggr, r.b + 1)
                    wait(pool, u_done, 1, r.b - 2)
                    nc.gpsimd.tensor_tensor(tmp[r.par][:, 1, :], mv[r.par][:, :, 1], EPS1, ALU.add).then_inc(veps, 1)
                    pool.wait_ge(veps, r.b + 1)
                    nc.gpsimd.tensor_tensor(tmp[r.par][:, 0, :], tmp[r.par][:, 1, :], MHALF,
                                            ALU.pow).then_inc(rstd, 1)

                def ffn_rstd(r):
                    tt, n = tmp[r.par], [0]
                    pool.wait_ge(aggr1, r.b + 1)
                    wait(pool, u1, C, r.b - 1)

                    def op(o, a, b_, f):
                        nc.gpsimd.tensor_tensor(o, a, b_, f).then_inc(chain1, 1)
                        n[0] += 1
                        pool.wait_ge(chain1, 6 * r.b + n[0])
                    op(tt[:, 3, :], mv1[r.par][:, :, 1], EPS1, ALU.add)
                    op(tt[:, 2, :], tt[:, 3, :], MHALF, ALU.pow)
                    op(tt[:, 4, :], mv1[r.par][:, :, 1], tt[:, 2, :], ALU.mult)
                    op(tt[:, 5, :], tt[:, 4, :], tt[:, 2, :], ALU.mult)
                    op(tt[:, 6, :], tt[:, 5, :], EPS1, ALU.add)
                    op(tt[:, 3, :], tt[:, 6, :], MHALF, ALU.pow)
                    nc.gpsimd.tensor_tensor(tt[:, 7, :], tt[:, 3, :], tt[:, 2, :], ALU.mult).then_inc(rstd1, 1)

                def step(t):
                    f, z, y = t, t + -2, t + -3
                    if z.within(B):
                        ffn_rstd(z)
                    if (t + 1).within(B):
                        input_rstd(t + 1)
                    if f.within(B):
                        xb = X[:, ds(C * f.b, C), :]
                        pool.wait_ge(u_done, f.b + 1)
                        nc.gpsimd.tensor_tensor(xb, xb, BOA[:, None, :].broadcast_to([128, C, D]),
                                                ALU.add).then_inc(xbo, 1)
                        pool.wait_ge(qv, f.b + 1)
                        wait(pool, r_mm, 1, f.b - 2)
                        nc.gpsimd.tensor_tensor(QD[f.par][:, :, :],
                                                QT[f.par][:, :].rearrange("p (c t) -> p c t", c=C),
                                                DROW[:, None, 0:128].broadcast_to([128, C, 128]),
                                                ALU.mult).then_inc(qd, 1)
                    if y.within(B):
                        placing.send(pool, y)
                    if z.within(B):
                        xb = X[:, ds(C * z.b, C), :]
                        pool.wait_ge(u1, C * (z.b + 1))
                        nc.gpsimd.tensor_tensor(xb, xb, U1[z.par][:, :, :], ALU.add).then_inc(base, 1)
                    if y.within(B):
                        placing.release(pool, y)
                placing.start(pool)
                input_rstd(Round(0, 0, 0))
                rounds(pool, 0, LO, HI, END, step)

            @block.scalar
            def _(act):
                def step(t):
                    if (t + -3).within(B):
                        placing.keep(act, t + -3, affv)
                    if t.within(B):
                        r = t
                        act.wait_ge(uT, r.b + 1)
                        wait(act, v_mm, 1, r.b - 2)
                        nc.scalar.copy(UT[r.par][:, :], bank[0][:, :]).then_inc(uTv, 1)
                    if (t + -1).within(B):
                        r = t + -1
                        act.wait_ge(kT_mm, r.b + 1)
                        wait(act, U_mm, 1, r.b - 2)
                        nc.scalar.mul(KP[r.par][:, :, :], quad[3], DEC[:, 128:129]).then_inc(kp, 1)
                    if t.within(B):
                        r = t
                        act.wait_ge(q_mm, r.b + 1)
                        wait(act, s_mm, 1, r.b - 2)
                        wait(act, qd, 1, r.b - 2)
                        nc.scalar.activation(QT[r.par][:, :], bank[1][:, :], ACT.Identity, bias=BQA).then_inc(qv, 1)
                        act.wait_ge(k_mm, r.b + 1)
                        wait(act, kt, 1, r.b - 2)
                        nc.scalar.activation(KE[r.par][:, :], bank[2][:, :], ACT.Exp, bias=BKA).then_inc(ke, 1)
                        nc.scalar.activation(KR[r.par][:, :], bank[2][:, :], ACT.Relu, bias=BKA).then_inc(kr, 1)
                    if (t + -1).within(B):
                        r = t + -1
                        act.wait_ge(r_mm, r.b + 1)
                        wait(act, o_mm, 1, r.b - 2)
                        nc.scalar.copy(RT[r.par][:, :], bank[5][:, :]).then_inc(rtv, 1)
                    if (t + -2).within(B):
                        r = t + -2
                        act.wait_ge(u1T_mm, r.b + 1)
                        wait(act, aff_mm, 1, r.b - 1)
                        nc.scalar.copy(U1T[r.par][:, :], bank[0][:, :]).then_inc(u1Tv, 1)
                        placing.number(act, r)
                rounds(act, 0, LO, HI, END, step)

            @block.tensor
            def _(pe):
                def step(t):
                    f, m, z = t, t + -1, t + -2
                    if f.within(B):
                        pe.wait_ge(u_done, f.b + 1)
                        wait(pe, u1Tv, 1, f.b - 3)
                        if not isinstance(f.b, int) or f.b >= 1:
                            wait(pe, uTv, 1, f.b - 1)
                        for c in range(C):
                            i = nc.tensor.transpose(quad[0][:, c, :], U[f.par][:, c, :], ID)
                        i.then_inc(uT, 1)
                    if z.within(B):
                        pe.wait_ge(rtv, z.b + 1)
                        if not f.within(B):
                            at_least(pe, placing.link, LINKS * (t.b - 4) + 8)
                        for c in range(C):
                            i = nc.tensor.matmul(quad[7][:, c, :], RT[z.par][:, 128 * c:128 * c + 128],
                                                 WA[:, 3, :], start=True, stop=True)
                        i.then_inc(o_mm, 1)
                    if m.within(B):
                        pe.wait_ge(qv, m.b + 1)
                        pe.wait_ge(kt, m.b + 1)
                        wait(pe, sm, 1, m.b - 1)
                        for c in range(C):
                            sl = slice(128 * c, 128 * c + 128)
                            i = nc.tensor.matmul(quad[4][:, c, :], KT[m.par][:, sl], QT[m.par][:, sl],
                                                 start=True, stop=True)
                        i.then_inc(s_mm, 1)
                        pe.wait_ge(vv, m.b + 1)
                        for c in range(C):
                            i = nc.tensor.transpose(quad[3][:, c, :], KT[m.par][:, 128 * c:128 * c + 128], ID)
                        i.then_inc(kT_mm, 1)
                    if f.within(B):
                        pe.wait_ge(uTv, f.b + 1)
                        wait(pe, qv, 1, f.b - 1)
                        nc.tensor.matmul(bank[1][:, :], WA[:, 0, :], UT[f.par][:, :], start=True,
                                         stop=True).then_inc(q_mm, 1)
                        wait(pe, kr, 1, f.b - 1)
                        wait(pe, ke, 1, f.b - 1)
                        nc.tensor.matmul(bank[2][:, :], WA[:, 1, :], UT[f.par][:, :], start=True,
                                         stop=True).then_inc(k_mm, 1)
                    if m.within(B):
                        pe.wait_ge(kp, m.b + 1)
                        wait(pe, mem, C - 1, m.b - 1)
                        wait(pe, affv, 1, m.b - 2)
                        for c in range(C - 1):
                            i = nc.tensor.matmul(quad[6][:, c, :], KP[m.par][:, c, :], V[m.par][:, c, :],
                                                 start=True, stop=True)
                        i.then_inc(U_mm, 1)
                    if z.within(B):
                        pe.wait_ge(x1, z.b + 1)
                    if (t + -3).within(B):
                        placing.rank(pe, t + -3, RANKS)
                    if f.within(B):
                        wait(pe, kp, 1, f.b - 1)
                        for c in range(C):
                            i = nc.tensor.matmul(quad[3][:, c, :], UT[f.par][:, 128 * c:128 * c + 128],
                                                 WA[:, 2, :], start=True, stop=True)
                        i.then_inc(v_mm, 1)
                    if m.within(B):
                        pe.wait_ge(sm, m.b + 1)
                        pe.wait_ge(qd, m.b + 1)
                        wait(pe, rtv, 1, m.b - 1)
                        for c in range(C):
                            i = nc.tensor.matmul(quad[5][:, c, :], V[m.par][:, c, :], SM_[m.par][:, c, :],
                                                 start=True, stop=(c == 0))
                            if c:
                                pe.wait_ge(mem, (C - 1) * m.b + c)
                                i = nc.tensor.matmul(quad[5][:, c, :], MEM[m.par][:, c - 1, :],
                                                     QD[m.par][:, c, :], start=False, stop=True)
                        i.then_inc(r_mm, 1)
                    if z.within(B):
                        pe.wait_ge(u1, C * (z.b + 1))
                        if f.within(B):
                            pe.wait_ge(uTv, f.b + 1)
                        else:
                            wait(pe, u1Tv, 1, z.b - 1)
                        for c in range(C):
                            i = nc.tensor.transpose(quad[0][:, c, :], U1[z.par][:, c, :], ID)
                        i.then_inc(u1T_mm, 1)
                        pe.wait_ge(u1Tv, z.b + 1)
                        for c in range(C):
                            i = nc.tensor.matmul(AFFP[:, E * c:E * c + E], U1T[z.par][:, 128 * c:128 * c + 128],
                                                 CENT, start=True, stop=True)
                        i.then_inc(aff_mm, 1)
                rounds(pe, 0, LO, HI, END, step)

        if upto == 1:
            with ExitStack() as cd:
                dd = sem("dd")
                block = cd.enter_context(nc.Block())

                @block.sync
                def _(sp):
                    for k, t in enumerate((X[:, :, :], X[:, :, :])):
                        sp.dma_start(dbg[k].rearrange("(t p) d -> p t d", p=128), t).then_inc(dd, 16)
                    sp.dma_start(dbg[2, :, 0:8].rearrange("(t p) d -> p t d", p=128), AFF[:, :, :]).then_inc(dd, 16)
                    sp.dma_start(dbg[2, 0:128, 8:72], w1_kept[3, :, 0:64]).then_inc(dd, 16)
                    sp.dma_start(dbg[2, 128:256, 8:72], C2[:, 3, 0:64]).then_inc(dd, 16)
                    sp.dma_start(dbg[2, 256:384, 8:40], NB1[:, :, :].rearrange("p e c -> p (e c)")).then_inc(dd, 16)
                    sp.wait_ge(dd, 96)
            return
        def route(tag):
            with ExitStack() as c:
                AM = sb(f"AM{tag}", [128, NT], c=c)
                EX = sb(f"EX{tag}", [128, NT], c=c)
                EX1 = sb(f"EX1{tag}", [128, NT], c=c)
                CNT = sb(f"CNT{tag}", [128, E], c=c)
                GT = sb(f"GT{tag}", [128, E, NT], c=c)
                N_T = sb(f"N_T{tag}", [128, E], c=c)
                CUM = sb(f"CUM{tag}", [128, E], c=c)
                WG = sb(f"WG{tag}", [128, E], c=c)
                CMP = sb(f"CMP{tag}", [1, TILES, E], c=c)
                CMPW = sb(f"CMPW{tag}", [1, TILES, E], c=c)
                TEF = sb(f"TEF{tag}", [1, TILES], c=c)
                TR = sb(f"TR{tag}", [1, 2, TILES], c=c)
                PADF = sb(f"PADF{tag}", [128, E], c=c)
                PADI = sb(f"PADI{tag}", [128, E], I32, c=c)
                amax, exd, chain, pads = (sem(f"r{tag}_{n}") for n in ("amax", "exd", "chain", "pads"))
                padded = soft[f"r{tag}_padded"]
                block = c.enter_context(nc.Block())

                @block.vector
                def _(dve):
                    n = [0]

                    def link(i):
                        i.then_inc(chain, 1)
                        n[0] += 1
                        dve.wait_ge(chain, n[0])
                    wide = [1, TILES, E]
                    link(nc.vector.tensor_tensor(PADF[:, :], CARRY[:, :], PART, ALU.add))
                    nc.vector.tensor_copy(PADI[:, :], PADF[:, :]).then_inc(pads, 1)
                    nc.vector.tensor_reduce(AM[:, :], AFF[:, :, :], axis=AX.X, op=ALU.max).then_inc(amax, 1)
                    link(nc.vector.tensor_tensor(CNT[:, :], CARRY[:, :], REGION, ALU.subtract))
                    link(nc.vector.tensor_tensor(GT[:, :, :], CNT[:, :, None].broadcast_to([128, E, NT]),
                                                 STEPS[:, None, :].broadcast_to([128, E, NT]), ALU.is_gt))
                    link(nc.vector.tensor_reduce(N_T[:, :], GT[:, :, :], axis=AX.X, op=ALU.add))
                    link(nc.vector.tensor_tensor_scan(CUM[:, :], ONES[:, 0:E], N_T[:, :], 0.0, ALU.mult, ALU.add))
                    link(nc.vector.tensor_tensor(CMP[:, :, :], ROW39[0:1, :, None].broadcast_to(wide),
                                                 CUM[0:1, None, :].broadcast_to(wide), ALU.is_ge))
                    link(nc.vector.tensor_reduce(TEF[:, :], CMP[:, :, 0:E - 1], axis=AX.X, op=ALU.add))
                    nc.vector.tensor_copy(TE[:, :], TEF[:, :])
                    link(nc.vector.scalar_tensor_tensor(WG[:, :], N_T[:, :], -128.0, JUMP, ALU.mult, ALU.add))
                    link(nc.vector.tensor_tensor(CMPW[:, :, :], CMP[:, :, :], WG[0:1, None, :].broadcast_to(wide),
                                                 ALU.mult))
                    link(nc.vector.tensor_reduce(TR[:, 0, :], CMPW[:, :, :], axis=AX.X, op=ALU.add))
                    link(nc.vector.scalar_tensor_tensor(TR[:, 1, :], ROW39[0:1, :], 128.0, TR[:, 0, :],
                                                        ALU.mult, ALU.add))
                    nc.vector.tensor_copy(TROW[:, :], TR[:, 1, :])
                    dve.wait_ge(exd, 1)
                    link(nc.vector.tensor_scalar_add(EX1[:, :], EX[:, :], 1.0))
                    nc.vector.reciprocal(ALPHA[:, :], EX1[:, :])
                    nc.vector.tensor_copy(CARRY[:, :], REGION)

                @block.scalar
                def _(act):
                    act.wait_ge(amax, 1)
                    nc.scalar.activation(EX[:, :], AM[:, :], ACT.Exp, scale=-1.0).then_inc(exd, 1)

                @block.gpsimd
                def _(pool):
                    apart(pool, pads, 1, pool_passed)
                    for e in range(E):
                        nc.gpsimd.indirect_dma_start(
                            sorted_x, bass.IndirectOffsetOnAxis(ap=PADI[:, e:e + 1], axis=0),
                            PADROW[:, e, :], None).then_inc(padded, 16)
                    pool.wait_ge(padded, 16 * E)

        NB = 3

        def experts(tag):
            with ExitStack() as c:
                XT_IN = [sb(f"f{tag}_x{i}", [128, ROW], c=c) for i in range(NB)]
                W1B = [sb(f"f{tag}_w{i}", [128, F], c=c) for i in range(NB)]
                XT = [sb(f"f{tag}_xt{i}", [128, 128], c=c) for i in range(NB)]
                HM = [sb(f"f{tag}_h{i}", [128, FC, 128], c=c) for i in range(NB)]
                Y = [sb(f"f{tag}_y{i}", [128, D], c=c) for i in range(NB)]
                TO = [sb(f"f{tag}_to{i}", [128, 1], I32, c=c) for i in range(NB)]
                x_in_ = [sem(f"f{tag}_xin{i}") for i in range(NB)]
                w_in = [sem(f"f{tag}_win{i}") for i in range(NB)]
                y_out = [soft[f"f{tag}_yout{i}"] for i in range(NB)]
                xt_mm, xtv, h_mm, hv, y_mm, yv = (sem(f"f{tag}_" + n) for n in ("xt", "xtv", "h", "hv", "y", "yv"))
                XB, HB, YB = (0, 1, 0), (3, 4, 5), (2, 6, 7)
                block = c.enter_context(nc.Block())

                def tiles(eng, body, lag):
                    for t in range(2 * NB):
                        body(t, t // NB, t % NB)
                    with eng.Fori(2, TILES // NB) as i:
                        for k in range(NB):
                            body(NB * i + k, i, k)
                    for t in range(TILES, TILES + lag):
                        body(t, t // NB, t % NB)

                def back(t, use, k, lag):
                    if isinstance(t, int) and not 0 <= t - lag < TILES:
                        return None
                    return t - lag, use - (1 if k < lag else 0), (k - lag) % NB

                def first_row(eng, t):
                    return eng.value_load(TROW[0:1, ds(t, 1)], min_val=0, max_val=SPARE + 128 * (E - 2))

                def expert(eng, t):
                    return eng.value_load(TE[0:1, ds(t, 1)], min_val=0, max_val=E - 1)

                @block.sync
                def _(sp):
                    def load(t, use, k):
                        row = first_row(sp, t)
                        at_least(sp, xt_mm, t - 2)
                        at_least(sp, xtv, t - 2)
                        sp.dma_start(XT_IN[k][:, :], sorted_x[ds(row, 128), :]).then_inc(x_in_[k], 16)

                    def step(t, use, k):
                        if back(t, use, k, 0):
                            load(t, use, k)
                        z = back(t, use, k, 1)
                        if z:
                            e = expert(sp, z[0])
                            at_least(sp, h_mm, z[0] - 2)
                            sp.dma_start(W1B[z[2]][:, :], w1_kept[ds(e, 1), :, :].rearrange("e p f -> (e p) f")
                                         ).then_inc(w_in[z[2]], 16)
                    tiles(sp, step, 1)

                @block.gpsimd
                def _(pool):
                    def store(t, use, k):
                        apart(pool, yv, t + 1, pool_passed)
                        nc.gpsimd.indirect_dma_start(
                            y_tok, bass.IndirectOffsetOnAxis(ap=TO[k][:, 0:1], axis=0),
                            Y[k][:, :], None).then_inc(y_out[k], 16)
                    tiles(pool, store, 0)
                    for k in range(NB):
                        pool.wait_ge(y_out[k], 16 * TILES // NB)

                @block.scalar
                def _(act):
                    def step(t, use, k):
                        act.wait_ge(xt_mm, t + 1)
                        at_least(act, h_mm, t - 2)
                        nc.scalar.copy(IDS[:, ds(t, 1)], XT_IN[k][:, D:ROW])
                        nc.scalar.copy(XT[k][:, :], bank[XB[k]][:, 0:128]).then_inc(xtv, 1)
                    tiles(act, step, 0)

                @block.vector
                def _(dve):
                    def step(t, use, k):
                        z = back(t, use, k, 0)
                        if z:
                            e = expert(dve, z[0])
                            dve.wait_ge(h_mm, z[0] + 1)
                            at_least(dve, y_mm, z[0] - 2)
                            nc.vector.tensor_tensor(
                                HM[k][:, :, :], quad[HB[k]],
                                NB1[:, ds(e, 1), :].rearrange("p e c -> p (e c)")[:, :, None]
                                .broadcast_to([128, FC, 128]), ALU.max).then_inc(hv, 1)
                        z = back(t, use, k, 1)
                        if z:
                            e = expert(dve, z[0])
                            dve.wait_ge(y_mm, z[0] + 1)
                            at_least(dve, y_out[z[2]], 16 * z[1])
                            apart(dve, xtv, z[0] + 1, dve_passed)
                            nc.vector.tensor_copy(TO[z[2]][:, :], IDS[:, ds(z[0], 1)])
                            nc.vector.tensor_tensor(Y[z[2]][:, :], bank[YB[z[2]]][:, 0:D],
                                                    C2[:, ds(e, 1), :].rearrange("p e d -> p (e d)"),
                                                    ALU.add).then_inc(yv, 1)
                    tiles(dve, step, 1)

                @block.tensor
                def _(pe):
                    def step(t, use, k):
                        z = back(t, use, k, 0)
                        if z:
                            pe.wait_ge(x_in_[k], 16 * (use + 1))
                            at_least(pe, xtv, t - (0, 2, 1)[k])
                            nc.tensor.transpose(bank[XB[k]][:, 0:128], XT_IN[k][:, 0:D], ID).then_inc(xt_mm, 1)
                        z = back(t, use, k, 1)
                        if z:
                            j, u, kk = z
                            pe.wait_ge(w_in[kk], 16 * (u + 1))
                            pe.wait_ge(xtv, j + 1)
                            at_least(pe, hv, j - 2)
                            for f in range(FC):
                                m = nc.tensor.matmul(quad[HB[kk]][:, f, :], W1B[kk][:, 128 * f:128 * f + 128],
                                                     XT[kk][:, :], start=True, stop=True)
                            m.then_inc(h_mm, 1)
                        z = back(t, use, k, 2)
                        if z:
                            j, u, kk = z
                            e = expert(pe, j)
                            pe.wait_ge(hv, j + 1)
                            at_least(pe, yv, j - 2)
                            for f in range(FC):
                                m = nc.tensor.matmul(bank[YB[kk]][:, 0:D], HM[kk][:, f, :],
                                                     W2T[:, ds(e, 1), f, :].rearrange("p e d -> p (e d)"),
                                                     start=(f == 0), stop=(f == FC - 1))
                            m.then_inc(y_mm, 1)
                    tiles(pe, step, 2)

        def attention():
            with ExitStack() as c:
                def two(name, shape, dt=F32):
                    return [sb(f"b_{name}{i}", shape, dt, c=c) for i in range(2)]
                placing = Placing("b", c)
                GA = [sb("b_GA", [128, C, D], c=c)] * 2
                st, mv, st3, mv3 = two("st", [128, C, 6]), two("mv", [128, C, 2]), two("st3", [128, C, 6]), \
                    two("mv3", [128, C, 2])
                tmp = two("tmp", [128, 8, C])
                U2, U2T = [sb("b_U2", [128, C, D], c=c)] * 2, [sb("b_U2T", [128, S], c=c)] * 2
                QF, KF = sb("b_QF", [128, S], c=c), sb("b_KF", [128, S], c=c)
                QHI, QLO = sb("b_QHI", [128, S], F32R, c=c), sb("b_QLO", [128, S], F32R, c=c)
                KHI, KLO = sb("b_KHI", [128, S], F32R, c=c), sb("b_KLO", [128, S], F32R, c=c)
                QS, KS = two("QS", [128, SETS, S], F32R), two("KS", [128, SETS, G, S], F32R)
                VA = two("VA", [128, C, H, AUG])
                NM = two("NM", [128, SETS, C, G])
                PARTS, STACK = 3 * G * HD, 3 * G * HD + G
                P = two("P", [128, G, S])
                OSB = two("OSB", [128, S])
                RC = two("RC", [128, C, G])
                AT, ATB = [sb("b_AT", [128, C, D], c=c)] * 2, [sb("b_ATB", [128, C, D], c=c)] * 2
                ATT, U3 = [sb("b_ATT", [128, S], c=c)] * 2, [sb("b_U3", [128, C, D], c=c)] * 2
                U3T = [sb("b_U3T", [128, S], c=c)] * 2
                (x2, xbo, stats, aggr, veps, rstd, u2, u2T_mm, u2Tv, q_mm, qf, k_mm, kf, q_parts, k_parts,
                 q_stack, k_stack, v_mm, vv, mx_mm, mx, ones_in, s_mm, exps, av, o_v,
                 otr_mm, rc, otr_v, atb, att_mm, att_v, o_mm, x3, stats3, aggr3, chain3, rstd3, u3, base,
                 u3T_mm, u3Tv, aff_mm, affv) = (sem("b_" + n) for n in (
                     "x2 xbo stats aggr veps rstd u2 u2T u2Tv q qf k kf q_parts k_parts "
                     "q_stack k_stack v vv mx_mm mx ones_in s exps av o_v "
                     "otr rc otr_v atb att att_v o x3 stats3 aggr3 chain3 rstd3 u3 base "
                     "u3T u3Tv aff affv").split())
                mt_mm = sem("b_mt_mm")
                k_zero, k_zero1 = sem("b_k_zero"), sem("b_k_zero1")
                q_hi, k_hi, vones, va_zero = sem("b_q_hi"), sem("b_k_hi"), sem("b_vones"), sem("b_va_zero")
                mt_v = sem("b_mt_v")
                y_here = sem("b_y_here")
                O, MISC = bank[6], bank[7]
                MQ = quad[7]
                SLOTS = SETS * C
                misc = [(0, "u2T", 1, 0), (1, "otr", -1, 3), (2, "mt", 0, 1), (3, "q", 1, 0), (4, "k", 1, 0),
                        (5, "att", -1, 0), (6, "mt", 0, 2), (7, "wo", -1, 0), (8, "otr", 0, 0), (9, "otr", 0, 1),
                        (10, "mt", 0, 3), (11, "u3T", -1, 0), (12, "aff", -1, 0), (13, "otr", 0, 2),
                        (14, "mt", 1, 0), (15, "v", 1, 0), (15, "rank", -1, 0)]
                RANKS = MISC[:, 0:(C + 1) * E]
                taken = {"u2T": (u2Tv, 1, 0), "otr": (otr_v, SETS, 0), "mt": (mt_v, SETS, 0), "q": (qf, 1, 0),
                         "k": (kf, 1, 0), "att": (att_v, 1, 0), "wo": (x3, 1, 0), "v": (vv, 1, 0),
                         "u3T": (u3Tv, 1, 0), "aff": (affv, 1, 0), "rank": (placing.link, LINKS, 7)}

                def uses(t, k):
                    return [(what, t + ahead, s) for slot, what, ahead, s in misc
                            if slot == k and (t + ahead).within(B)]

                def misc_free(pe, t, use):
                    for back_ in range(1, 3 * len(misc)):
                        n = use - back_
                        _, what, ahead, s = misc[n % len(misc)]
                        r = t + n // len(misc) + ahead
                        if isinstance(r.b, int) and not 0 <= r.b < B:
                            continue
                        signal, per, more = taken[what]
                        at_least(pe, signal, per * r.b + s + 1 + more)
                        return

                def m_slot(t, k):
                    return (t, 2 + k // C) if k < SLOTS // 2 else (t + 1, k // C - 2)
                FIRST, LO, HI, END = -2, 2, 6, 9
                block = c.enter_context(nc.Block())

                @block.sync
                def _(sp):
                    sp.wait_ge(k_zero, 1)
                    sp.wait_ge(k_zero1, 1)

                    def stack(r, what, parts, src_ready, done, per):
                        apart(sp, src_ready, r.b + 1, sp_passed)
                        apart(sp, done, 16 * per * r.b, sp_passed)
                        apart(sp, s_mm, 2 * SLOTS * (r.b - 1), sp_passed)
                        for n, part in enumerate(parts):
                            if what == "q":
                                sp.dma_start(QS[r.par][32 * n:32 * n + 32, :, :].bitcast(F32),
                                             part[:, :].bitcast(F32)).then_inc(done, 16)
                                continue
                            for g in range(G):
                                z = 32 * n + HD * g
                                sp.dma_start(KS[r.par][z:z + HD, :, g, :].bitcast(F32),
                                             part[32 * g:32 * g + 32, :].bitcast(F32)).then_inc(done, 16)

                    def step(t):
                        if (t + 2).within(B):
                            r = t + 2
                            wait(sp, x2, 1, r.b - 1)
                            sp.dma_start(GA[r.par][:, :, :], y_tok[ds(S * r.b, S), :]
                                         .rearrange("(c p) d -> p c d", p=128)).then_inc(y_here, 16)
                        if (t + 1).within(B):
                            stack(t + 1, "q", (QHI, QHI, QLO), q_parts, q_stack, 3)
                            stack(t + 1, "k", (KHI, KLO, KHI), k_parts, k_stack, 3 * G)
                    rounds(sp, FIRST, LO, HI, END, step)

                @block.gpsimd
                def _(pool):
                    def rstd_in(r):
                        pool.wait_ge(aggr, r.b + 1)
                        wait(pool, u2, 1, r.b - 2)
                        nc.gpsimd.tensor_tensor(tmp[r.par][:, 1, :], mv[r.par][:, :, 1], EPS1, ALU.add).then_inc(veps, 1)
                        pool.wait_ge(veps, r.b + 1)
                        nc.gpsimd.tensor_tensor(tmp[r.par][:, 0, :], tmp[r.par][:, 1, :], MHALF,
                                                ALU.pow).then_inc(rstd, 1)

                    def rstd_out(r):
                        tt, n = tmp[r.par], [0]
                        pool.wait_ge(aggr3, r.b + 1)
                        wait(pool, u3, C, r.b - 1)

                        def op(o, a, b_, f):
                            nc.gpsimd.tensor_tensor(o, a, b_, f).then_inc(chain3, 1)
                            n[0] += 1
                            pool.wait_ge(chain3, 6 * r.b + n[0])
                        op(tt[:, 3, :], mv3[r.par][:, :, 1], EPS1, ALU.add)
                        op(tt[:, 2, :], tt[:, 3, :], MHALF, ALU.pow)
                        op(tt[:, 4, :], mv3[r.par][:, :, 1], tt[:, 2, :], ALU.mult)
                        op(tt[:, 5, :], tt[:, 4, :], tt[:, 2, :], ALU.mult)
                        op(tt[:, 6, :], tt[:, 5, :], EPS1, ALU.add)
                        op(tt[:, 3, :], tt[:, 6, :], MHALF, ALU.pow)
                        nc.gpsimd.tensor_tensor(tt[:, 7, :], tt[:, 3, :], tt[:, 2, :], ALU.mult).then_inc(rstd3, 1)

                    def parts(r, full, hi, lo, ready, stacked, per, first, done):
                        wait(pool, stacked, 16 * per, r.b - 1)
                        apart(pool, ready, r.b + 1, pool_passed)
                        nc.gpsimd.tensor_copy(hi[:, :], full[:, :]).then_inc(first, 1)
                        pool.wait_ge(first, r.b + 1)
                        nc.gpsimd.tensor_tensor(lo[:, :], full[:, :], hi[:, :].bitcast(F32),
                                                ALU.subtract).then_inc(done, 1)

                    def step(t):
                        for k in range(SLOTS):
                            if k == 2 and (t + -1).within(B):
                                r = t + -1
                                pool.wait_ge(otr_v, SETS * (r.b + 1))
                                wait(pool, att_mm, 1, r.b - 1)
                                nc.gpsimd.tensor_tensor(ATB[r.par][:, :, :], AT[r.par][:, :, :],
                                                        BVB[:, None, :].broadcast_to([128, C, D]),
                                                        ALU.add).then_inc(atb, 1)
                            if k == 3 and (t + 1).within(B):
                                parts(t + 1, QF, QHI, QLO, qf, q_stack, 3, q_hi, q_parts)
                            if k == 4 and (t + 1).within(B):
                                parts(t + 1, KF, KHI, KLO, kf, k_stack, 3 * G, k_hi, k_parts)
                            if k == 6 and (t + 2).within(B):
                                rstd_in(t + 2)
                            if k == 5 and (t + -2).within(B):
                                placing.send(pool, t + -2)
                            if k == 7 and (t + -2).within(B):
                                placing.release(pool, t + -2)
                            if k == 8 and (t + -1).within(B):
                                rstd_out(t + -1)
                            if k == 12 and (t + 2).within(B):
                                r = t + 2
                                xb = X[:, ds(C * r.b, C), :]
                                pool.wait_ge(u2, r.b + 1)
                                nc.gpsimd.tensor_tensor(xb, xb, BOB[:, None, :].broadcast_to([128, C, D]),
                                                        ALU.add).then_inc(xbo, 1)
                            if k == 13 and (t + -1).within(B):
                                r = t + -1
                                xb = X[:, ds(C * r.b, C), :]
                                pool.wait_ge(u3, C * (r.b + 1))
                                nc.gpsimd.tensor_tensor(xb, xb, U3[r.par][:, :, :], ALU.add).then_inc(base, 1)
                    placing.start(pool)
                    nc.gpsimd.memset(KS[1][0:PARTS, :, :, :].bitcast(F32), 0.0).then_inc(k_zero1, 1)
                    rounds(pool, FIRST, LO, HI, END, step)
    
                @block.vector
                def _(dve):
                    for p in range(2):
                        i = nc.vector.memset(VA[p][:, :, :, :], 0.0)
                    i.then_inc(va_zero, 1)
                    nc.vector.memset(KS[0][0:PARTS, :, :, :].bitcast(F32), 0.0).then_inc(k_zero, 1)

                    def xs(r, c_):
                        return X[:, ds(C * r.b + c_, 1), :].rearrange("p o d -> p (o d)")

                    def add_ffn(r):
                        dve.wait_ge(y_here, 16 * (r.b + 1))
                        for c_ in range(C):
                            i = nc.vector.scalar_tensor_tensor(xs(r, c_), GA[r.par][:, c_, :],
                                                               ALPHA[:, ds(C * r.b + c_, 1)], xs(r, c_),
                                                               ALU.mult, ALU.add)
                        i.then_inc(x2, 1)
                        apart(dve, x2, r.b + 1, dve_passed)
                        for c_ in range(C):
                            i = nc.vector.bn_stats(st[r.par][:, c_, :], xs(r, c_))
                        i.then_inc(stats, 1)
                        dve.wait_ge(stats, r.b + 1)
                        apart(dve, rstd, r.b - 1, dve_passed)
                        for c_ in range(C):
                            i = nc.vector.bn_aggr(mv[r.par][:, c_, :], st[r.par][:, c_, :])
                        i.then_inc(aggr, 1)

                    def step(t):
                        for k in range(SLOTS):
                            if k == 0 and (t + -2).within(B):
                                placing.place(dve, t + -2, RANKS)
                            r, s = m_slot(t, k)
                            if r.within(B):
                                for g in range(G):
                                    n = SLOTS * G * r.b + C * G * s + G * (k % C) + g
                                    dve.wait_ge(mx_mm, n + 1)
                                    nc.vector.tensor_reduce(NM[r.par][:, s, k % C, g:g + 1], bank[4 + g % 2],
                                                            axis=AX.X, op=ALU.max, negate=True).then_inc(mx, 1)
                            if k in (13, 14) and (t + -1).within(B):
                                placing.choose(dve, t + -1, (0, 1) if k == 13 else (2, 3, 4), affv)
                            if k == 9 and (t + -1).within(B):
                                r = t + -1
                                dve.wait_ge(rstd3, r.b + 1)
                                placing.wait_free(dve, r)
                                wait(dve, u3T_mm, 1, r.b - 1)
                                wait(dve, base, 1, r.b - 1)
                                for c_ in range(C):
                                    nc.vector.tensor_scalar(U3[r.par][:, c_, :], xs(r, c_), mv3[r.par][:, c_, 0:1],
                                                            tmp[r.par][:, 2, c_:c_ + 1], ALU.subtract, ALU.mult)
                                    nc.vector.tensor_scalar(placing.XS[r.par][:, c_, 0:D],
                                                            xs(r, c_), mv3[r.par][:, c_, 0:1],
                                                            tmp[r.par][:, 7, c_:c_ + 1], ALU.subtract, ALU.mult
                                                            ).then_inc(u3, 1)
                            for what, r, s in uses(t, k):
                                if what == "otr":
                                    n = SETS * r.b + s
                                    rows = MQ.rearrange("p c (g a) -> p c g a", g=G)
                                    dve.wait_ge(otr_mm, n + 1)
                                    nc.vector.reciprocal(RC[s % 2][:, :, :], rows[:, :, :, HD]).then_inc(rc, 1)
                                    dve.wait_ge(rc, n + 1)
                                    if s == 0:
                                        wait(dve, atb, 1, r.b - 1)
                                    nc.vector.tensor_tensor(
                                        AT[r.par][:, :, 32 * s:32 * s + 32].rearrange("p c (g d) -> p c g d", g=G),
                                        rows[:, :, :, 0:HD], RC[s % 2][:, :, :, None].broadcast_to([128, C, G, HD]),
                                        ALU.mult).then_inc(otr_v, 1)
                                if what == "wo":
                                    dve.wait_ge(o_mm, r.b + 1)
                                    dve.wait_ge(xbo, r.b + 1)
                                    nc.vector.tensor_tensor(X[:, ds(C * r.b, C), :], MQ, X[:, ds(C * r.b, C), :],
                                                            ALU.add).then_inc(x3, 1)
                                    apart(dve, x3, r.b + 1, dve_passed)
                                    for c_ in range(C):
                                        i = nc.vector.bn_stats(st3[r.par][:, c_, :], xs(r, c_))
                                    i.then_inc(stats3, 1)
                                    dve.wait_ge(stats3, r.b + 1)
                                    apart(dve, rstd3, r.b, dve_passed)
                                    for c_ in range(C):
                                        i = nc.vector.bn_aggr(mv3[r.par][:, c_, :], st3[r.par][:, c_, :])
                                    i.then_inc(aggr3, 1)
                                if what == "aff":
                                    dve.wait_ge(aff_mm, r.b + 1)
                                    wait(dve, placing.kept, 1, r.b - 1)
                                    nc.vector.tensor_copy(placing.AFFB[:, :, :],
                                                          MISC[:, 0:C * E].rearrange("p (c e) -> p c e", c=C)
                                                          ).then_inc(affv, 1)
                            if k == 4 and (t + 2).within(B):
                                add_ffn(t + 2)
                            if k == 8 and (t + 2).within(B):
                                r = t + 2
                                dve.wait_ge(rstd, r.b + 1)
                                wait(dve, u2T_mm, 1, r.b - 1)
                                for c_ in range(C):
                                    i = nc.vector.tensor_scalar(U2[r.par][:, c_, :], xs(r, c_),
                                                                mv[r.par][:, c_, 0:1], tmp[r.par][:, 0, c_:c_ + 1],
                                                                ALU.subtract, ALU.mult)
                                i.then_inc(u2, 1)

                    rounds(dve, FIRST, LO, HI, END, step)

                @block.scalar
                def _(act):
                    act.wait_ge(va_zero, 1)
                    for p in range(2):
                        i = nc.scalar.activation(VA[p][:, :, :, HD:HD + 1], VA[p][:, :, :, HD:HD + 1], ACT.Copy,
                                                 bias=1.0)
                    i.then_inc(vones, 1)
                    act.wait_ge(vones, 1)
                    for p in range(2):
                        nc.scalar.copy(KS[p][PARTS:STACK, :, :, :],
                                       ID[PARTS:STACK, None, PARTS:STACK, None].broadcast_to([G, SETS, G, S])
                                       ).then_inc(ones_in, 1)

                    def step(t):
                        for k in range(SLOTS):
                            if t.within(B):
                                r = t
                                for j in range(2):
                                    act.wait_ge(s_mm, 2 * SLOTS * r.b + 2 * k + j + 1)
                                    at_least(act, av, SLOTS * r.b + k - 1)
                                    nc.scalar.activation(P[k % 2][:, 2 * j:2 * j + 2, :], PS[:, 2 * j:2 * j + 2, :],
                                                         ACT.Exp, scale=SCALE).then_inc(exps, 1)
                            if k == 13 and (t + -1).within(B):
                                placing.number(act, t + -1)
                                placing.keep(act, t + -1, affv)
                            for what, r, s in uses(t, k):
                                if what == "u2T":
                                    act.wait_ge(u2T_mm, r.b + 1)
                                    wait(act, v_mm, 1, r.b - 1)
                                    nc.scalar.copy(U2T[r.par][:, :], MISC).then_inc(u2Tv, 1)
                                if what == "mt":
                                    act.wait_ge(mt_mm, SETS * r.b + s + 1)
                                    at_least(act, s_mm, 2 * (SLOTS * (r.b - 2) + C * (s + 1)))
                                    nc.scalar.copy(QS[r.par][PARTS:STACK, s, :],
                                                   MISC[PARTS:STACK, :]).then_inc(mt_v, 1)
                                if what == "q":
                                    act.wait_ge(q_mm, r.b + 1)
                                    wait(act, q_parts, 1, r.b - 1)
                                    nc.scalar.activation(QF[:, :], MISC, ACT.Identity, bias=BQB).then_inc(qf, 1)
                                if what == "k":
                                    act.wait_ge(k_mm, r.b + 1)
                                    wait(act, k_parts, 1, r.b - 1)
                                    nc.scalar.activation(KF[:, :], MISC, ACT.Identity, bias=BKB).then_inc(kf, 1)
                                if what == "v":
                                    act.wait_ge(v_mm, r.b + 1)
                                    at_least(act, av, SLOTS * (r.b - 1))
                                    nc.scalar.copy(VA[r.par][:, :, :, 0:HD],
                                                   MQ.rearrange("p c (h d) -> p c h d", h=H)).then_inc(vv, 1)
                                if what == "att":
                                    act.wait_ge(att_mm, r.b + 1)
                                    wait(act, o_mm, 1, r.b - 1)
                                    nc.scalar.copy(ATT[r.par][:, :], MISC).then_inc(att_v, 1)
                                if what == "u3T":
                                    act.wait_ge(u3T_mm, r.b + 1)
                                    wait(act, aff_mm, 1, r.b - 1)
                                    nc.scalar.copy(U3T[r.par][:, :], MISC).then_inc(u3Tv, 1)
                            if k % C == 0:
                                r, s = (t, k // C - 1) if k else (t + -1, SETS - 1)
                                if r.within(B):
                                    n = SETS * r.b + s
                                    act.wait_ge(av, SLOTS * r.b + C * (s + 1))
                                    at_least(act, otr_mm, n - 1)
                                    nc.scalar.copy(OSB[s % 2][:, :], O).then_inc(o_v, 1)
                    rounds(act, FIRST, LO, HI, END, step)

                @block.tensor
                def _(pe):
                    pe.wait_ge(ones_in, 2)
                    pe.wait_ge(vones, 1)

                    def products(r, k):
                        s, c_ = k // C, k % C
                        if c_ == 0:
                            at_least(pe, o_v, SETS * r.b + s)
                            if k == 0:
                                pe.wait_ge(vv, r.b + 1)
                        pe.wait_ge(exps, 2 * (SLOTS * r.b + k + 1))
                        for g in range(G):
                            i = nc.tensor.matmul(O[32 * g:32 * g + 32, :], VA[r.par][:, c_, G * s + g, :],
                                                 P[k % 2][:, g, :], start=(c_ == 0), stop=(c_ == C - 1))
                        i.then_inc(av, 1)

                    def scores(t, k, j):
                        if not t.within(B):
                            return
                        s, c_ = k // C, k % C
                        if c_ == 0 and j == 0:
                            pe.wait_ge(mt_v, SETS * t.b + s + 1)
                        at_least(pe, exps, 2 * (SLOTS * t.b + k) + j - 1)
                        for g in (2 * j, 2 * j + 1):
                            i = nc.tensor.matmul(bank[g], KS[t.par][0:STACK, s, g, 128 * c_:128 * c_ + 128],
                                                 QS[t.par][0:STACK, s, :], start=True, stop=True)
                        i.then_inc(s_mm, 1)

                    def rowwise(t, k, g):
                        r, s = m_slot(t, k)
                        if not r.within(B):
                            return
                        if k == SLOTS // 2 and g == 0:
                            pe.wait_ge(q_stack, 16 * 3 * (r.b + 1))
                            pe.wait_ge(k_stack, 16 * 3 * G * (r.b + 1))
                        at_least(pe, mx, SLOTS * G * r.b + C * G * s + G * (k % C) + g - 1)
                        qt = 128 * (k % C)
                        nc.tensor.matmul(bank[4 + g % 2], QS[r.par][0:PARTS, s, qt:qt + 128],
                                         KS[r.par][0:PARTS, s, g, :], start=True, stop=True).then_inc(mx_mm, 1)

                    def spare(t, k):
                        for use, (slot, what, ahead, s) in enumerate(misc):
                            r = t + ahead
                            if slot != k or not r.within(B):
                                continue
                            misc_free(pe, t, use)
                            if what == "rank":
                                placing.rank(pe, r, RANKS)
                            if what == "u2T":
                                pe.wait_ge(u2, r.b + 1)
                                for c_ in range(C):
                                    i = nc.tensor.transpose(MQ[:, c_, :], U2[r.par][:, c_, :], ID)
                                i.then_inc(u2T_mm, 1)
                            if what == "otr":
                                n = SETS * r.b + s
                                pe.wait_ge(o_v, n + 1)
                                for c_ in range(C):
                                    i = nc.tensor.transpose(MQ[:, c_, :], OSB[s % 2][:, 128 * c_:128 * c_ + 128], ID)
                                i.then_inc(otr_mm, 1)
                            if what == "mt":
                                pe.wait_ge(mx, SLOTS * G * r.b + C * G * (s + 1))
                                for c_ in range(C):
                                    i = nc.tensor.matmul(MQ[PARTS:STACK, c_, :], NM[r.par][:, s, c_, :], ID,
                                                         start=True, stop=True)
                                i.then_inc(mt_mm, 1)
                            if what in ("q", "k"):
                                pe.wait_ge(u2Tv, r.b + 1)
                                nc.tensor.matmul(MISC, WB[:, 0 if what == "q" else 1, :], U2T[r.par][:, :],
                                                 start=True, stop=True).then_inc(q_mm if what == "q" else k_mm, 1)
                            if what == "v":
                                for c_ in range(C):
                                    i = nc.tensor.matmul(MQ[:, c_, :], U2T[r.par][:, 128 * c_:128 * c_ + 128],
                                                         WB[:, 2, :], start=True, stop=True)
                                i.then_inc(v_mm, 1)
                            if what == "att":
                                pe.wait_ge(atb, r.b + 1)
                                for c_ in range(C):
                                    i = nc.tensor.transpose(MQ[:, c_, :], ATB[r.par][:, c_, :], ID)
                                i.then_inc(att_mm, 1)
                            if what == "wo":
                                pe.wait_ge(att_v, r.b + 1)
                                for c_ in range(C):
                                    i = nc.tensor.matmul(MQ[:, c_, :], ATT[r.par][:, 128 * c_:128 * c_ + 128],
                                                         WB[:, 3, :], start=True, stop=True)
                                i.then_inc(o_mm, 1)
                            if what == "u3T":
                                pe.wait_ge(u3, C * (r.b + 1))
                                for c_ in range(C):
                                    i = nc.tensor.transpose(MQ[:, c_, :], U3[r.par][:, c_, :], ID)
                                i.then_inc(u3T_mm, 1)
                            if what == "aff":
                                pe.wait_ge(u3Tv, r.b + 1)
                                for c_ in range(C):
                                    i = nc.tensor.matmul(MISC[:, E * c_:E * c_ + E],
                                                         U3T[r.par][:, 128 * c_:128 * c_ + 128], CENT,
                                                         start=True, stop=True)
                                i.then_inc(aff_mm, 1)

                    def step(t):
                        for k in range(SLOTS):
                            scores(t, k, 0)
                            rowwise(t, k, 0)
                            scores(t, k, 1)
                            rowwise(t, k, 1)
                            r, kk = (t, k - 1) if k else (t + -1, SLOTS - 1)
                            if r.within(B):
                                products(r, kk)
                            rowwise(t, k, 2)
                            spare(t, k)
                            rowwise(t, k, 3)
                    rounds(pe, FIRST, LO, HI, END, step)

        def finish():
            with ExitStack() as c:
                GA = [sb(f"z_GA{i}", [128, C, D], c=c) for i in range(2)]
                done, stored = sem("z_done"), sem("z_stored")
                y_here = [sem(f"z_y{i}") for i in range(2)]
                block = c.enter_context(nc.Block())

                @block.scalar
                def _(act):
                    def load(r):
                        wait(act, done, 1, r.b - 2)
                        act.dma_start(GA[r.par][:, :, :], y_tok[ds(S * r.b, S), :]
                                      .rearrange("(c p) d -> p c d", p=128)).then_inc(y_here[r.par], 16)
                    rounds(act, 0, 2, 8, 7, load)

                @block.vector
                def _(dve):
                    def add(r):
                        dve.wait_ge(y_here[r.par], 16 * (r.half + 1))
                        for c_ in range(C):
                            xs = X[:, ds(C * r.b + c_, 1), :].rearrange("p o d -> p (o d)")
                            i = nc.vector.scalar_tensor_tensor(xs, GA[r.par][:, c_, :],
                                                               ALPHA[:, ds(C * r.b + c_, 1)], xs,
                                                               ALU.mult, ALU.add)
                        i.then_inc(done, 1)
                    rounds(dve, 0, 2, 8, 7, add)

                @block.sync
                def _(sp):
                    def store(r):
                        sp.wait_ge(done, r.b + 1)
                        sp.dma_start(out[ds(r.b, 1), :, :].rearrange("o (c p) d -> p (o c) d", p=128),
                                     X[:, ds(C * r.b, C), :]).then_inc(stored, 16)
                    rounds(sp, 0, 2, 8, 7, store)
                    sp.wait_ge(stored, 16 * B)

        def dump(n, parts):
            with ExitStack() as cd:
                dd = sem("dd")
                cd.enter_context(nc.allow_non_contiguous_dma(reason="debug"))
                block = cd.enter_context(nc.Block())

                @block.sync
                def _(sp):
                    for o, i in parts:
                        sp.dma_start(o, i).then_inc(dd, 16)
                    sp.wait_ge(dd, 16 * len(parts))
        with nc.Block() as block:
            @block.gpsimd
            def _(pool):
                for s in held:
                    pool.sem_clear(s)
        held = None
        early.close()
        route(1)
        experts(1)
        if upto == 3:
            return dump(3, [(dbg[0], y_tok[0:4096, :]), (dbg[1, :, 0:1].rearrange("(t p) o -> p (t o)", p=128), ALPHA[:, :]),
                            (dbg[2, :, 0:8].rearrange("(t p) d -> p t d", p=128), AFF[:, :, :]),
                            (dbg[1, 0:1, 64:103], TE[:, :].bitcast(F32)), (dbg[1, 1:2, 64:103], TROW[:, :].bitcast(F32))])
        attention()
        if upto == 4:
            return dump(4, [(dbg[0].rearrange("(t p) d -> p t d", p=128), X[:, :, :])] +
                        [(dbg[2, :, 0:8].rearrange("(t p) d -> p t d", p=128), AFF[:, :, :])])
        route(2)
        experts(2)
        finish()


_INS = ['L0_attn_a_x', 'L0_attn_a_Wq', 'L0_attn_a_bq', 'L0_attn_a_Wk', 'L0_attn_a_bk', 'L0_attn_a_Wv',
        'L0_attn_a_bv', 'L0_attn_a_Wo', 'L0_attn_a_bo', 'L0_attn_a_decay_param', 'L0_attn_b_Wq', 'L0_attn_b_bq',
        'L0_attn_b_Wk', 'L0_attn_b_bk', 'L0_attn_b_Wv', 'L0_attn_b_bv', 'L0_attn_b_Wo', 'L0_attn_b_bo',
        'L0_attn_b_head_mask', 'L0_ffn_centroids', 'L0_ffn_ln_g', 'L0_ffn_ln_b', 'L0_ffn_w1', 'L0_ffn_b1',
        'L0_ffn_w2', 'L0_ffn_b2']


def shape_constants(np):
    con = np.zeros((128, 672), np.float32)
    con[:, 0:128] = np.eye(128)
    i = np.arange(128)
    con[:, 128:256] = i[:, None] < i[None, :]
    con[:, 256:385] = np.arange(129)[None, :] == i[:, None] + 1
    con[:, 385] = 1
    con[:, 514:522] = E - np.arange(E)
    con[:, 522:554] = 128 * np.arange(NT)
    con[:, 554:586] = 128 * np.arange(NT) + i[:, None]
    con[:, 586:625] = np.arange(TILES)
    con[:, 625:629] = EPS
    con[:, 629:633] = -0.5
    con[:, 633:641] = CAP * np.arange(E)
    con[:, 641:649] = CAP
    con[:, 649:657] = i[:, None]
    con[:, 657:657 + PADS] = TOKENS + 128 * np.arange(PADS) + i[:, None]
    ids = np.tile(np.arange(TILES, dtype=np.float32), (1, 1))
    return con, ids


def kernel(**inputs):
    import numpy as _np
    import concourse.bacc as _bacc
    from concourse import mybir as _mybir
    from concourse.bass_utils import run_bass_kernel_spmd as _run

    nc = _bacc.Bacc("TRN2", target_bir_lowering=False, num_devices=1)
    arrays, args = {}, []
    con, ids = shape_constants(_np)
    named = [(n, _np.ascontiguousarray(inputs[n]).reshape(_np.shape(inputs[n]) or (1,))) for n in _INS] + [("consts", con), ("tile_ids", ids)]
    for name, a in named:
        arrays[f"in_{name}"] = a
        args.append(nc.dram_tensor(f"in_{name}", a.shape, _mybir.dt.from_np(a.dtype), kind="ExternalInput").ap())
    out = nc.dram_tensor("out", (B, S, D), F32, kind="ExternalOutput").ap()
    hybrid(nc, *args, out)
    r = _run(nc, [arrays], core_ids=[0])
    return r.results[0]["out"]
```

```python
import concourse.bass as bass
from concourse import mybir
from contextlib import ExitStack

F32 = mybir.dt.float32
F32R = mybir.dt.float32r
I32 = mybir.dt.int32
BF16 = mybir.dt.bfloat16
ALU = mybir.AluOpType
ACT = mybir.ActivationFunctionType
AX = mybir.AxisListType

D = 128
B, S = 8, 512
C = S // 128
NT = B * C
E, F = 8, 512
FC = F // 128
TILES = NT + E - 1
TOKENS = B * S
CAP = TOKENS + 128
SPARE = E * CAP
PADS = 2 * E - 1
ROW = D + 1
LINKS = 10
H, HD = 16, 8
G = 4
SETS = H // G
PARTS = 3 * G * HD
STACK = PARTS + G
AUG = 32
EPS = 1e-5
SCALE = 1.0 / float(HD) ** 0.5


def ds(i, n):
    return bass.ds(i, n)


def wait(eng, sem, per, b):
    if isinstance(b, int) and b < 0:
        return
    eng.wait_ge(sem, per * (b + 1))


def at_least(eng, sem, value):
    if isinstance(value, int) and value <= 0:
        return
    eng.wait_ge(sem, value)


def apart(eng, sem, value, passed):
    if isinstance(value, int) and value <= 0:
        return
    eng.wait_ge(sem, value)
    eng.sem_inc(passed, 1)


class Round:

    def __init__(self, b, half, par):
        self.b, self.half, self.par = b, half, par

    def __add__(self, k):
        b = self.b + k
        return Round(b, self.half + (self.par + k) // 2, (self.par + k) % 2)

    def within(self, n):
        return not isinstance(self.b, int) or 0 <= self.b < n


def rounds(eng, first, loop_from, loop_to, last, body):
    def at(t):
        return Round(t, t // 2, t % 2)
    for t in range(first, loop_from):
        body(at(t))
    if loop_to > loop_from:
        turns = (loop_to - loop_from) // 2
        lo = loop_from // 2
        assert loop_from + 2 * turns == loop_to
        with eng.Fori(lo, lo + turns) as i:
            for h in range(2):
                k = loop_from % 2 + h
                body(Round(2 * i + k, i + k // 2, k % 2))
    for t in range(loop_to, last + 1):
        body(at(t))


def hybrid(nc, x_in, Wq_a, bq_a, Wk_a, bk_a, Wv_a, bv_a, Wo_a, bo_a, decay,
           Wq_b, bq_b, Wk_b, bk_b, Wv_b, bv_b, Wo_b, bo_b, head_mask,
           cent, ln_g, ln_b, w1, b1, w2, b2, consts, out):
    ctx = ExitStack()
    with ctx:
        def sb(name, shape, dt=F32, c=ctx):
            return c.enter_context(nc.sbuf_tensor(name, shape, dt))

        early = ExitStack()
        held = []

        def sem(name):
            if held is None:
                return ctx.enter_context(nc.semaphore(name))
            held.append(early.enter_context(nc.semaphore(name)))
            return held[-1]

        soft = {n: ctx.enter_context(nc.semaphore(n)) for n in
                ("u_kept0 u_kept1 pa_sent0 pa_sent1 pb_sent0 pb_sent1 r1_padded r2_padded "
                 "f1_yout0 f1_yout1 f1_yout2 f2_yout0 f2_yout1 f2_yout2").split()}
        PS = ctx.enter_context(nc.psum_tensor("PS", [128, 8, 512], F32))
        bank = [PS[:, i, :] for i in range(8)]
        quad = [b_.rearrange("p (c d) -> p c d", c=C) for b_ in bank]

        sorted_x = nc.dram_tensor("sorted_x", [SPARE + 128 * (E - 1), ROW], F32, kind="Internal").ap()
        y_tok = nc.dram_tensor("y_tok", [TOKENS + 128 * PADS, D], F32, kind="Internal").ap()

        dve_passed, pool_passed, sp_passed = (ctx.enter_context(nc.semaphore(n))
                                              for n in ("dve_passed", "pool_passed", "sp_passed"))
        X = sb("X", [128, NT, D])
        AFF = sb("AFF", [128, NT, E])
        ALPHA = sb("ALPHA", [128, NT])
        TE = sb("TE", [1, TILES], I32)
        TROW = sb("TROW", [1, TILES], I32)
        IDS = sb("IDS", [128, TILES], I32)
        CARRY = sb("CARRY", [128, E])
        PADROW = sb("PADROW", [128, PADS, ROW])
        NB1 = sb("NB1", [128, E, FC])
        C2 = sb("C2", [128, E, D])
        CON = sb("CON", [128, 672])
        ID = CON[:, 0:128]
        LOW = CON[:, 128:256]
        IMP = CON[:, 256:385]
        IMP0 = CON[:, 385:514]
        CODE = CON[:, 514:522]
        STEPS = CON[:, 522:554]
        TOK = CON[:, 554:586]
        ROW39 = CON[:, 586:625]
        EPS1 = CON[:, 625:629]
        MHALF = CON[:, 629:633]
        REGION = CON[:, 633:641]
        JUMP = CON[:, 641:649]
        PART = CON[:, 649:657]
        PADID = CON[:, 657:657 + PADS]
        ONES = sb("ONES", [128, 128])
        LOW16, ONES16 = sb("LOW16", [128, 128], BF16), sb("ONES16", [128, 128], BF16)
        COL = sb("COL", [128, 61])
        LNG, LNB, B1T, CENT = COL[:, 1:9], COL[:, 9:17], COL[:, 17:49], COL[:, 49:57]
        MASKH, BQA, BKA, BQB, BKB = (COL[:, k:k + 1] for k in (0, 57, 58, 59, 60))
        WA = sb("WA", [128, 4, D])
        WB = sb("WB", [128, 4, D])
        REP = sb("REP", [128, 4, D])
        DEC = sb("DEC", [128, 129])
        DROW = sb("DROW", [128, 129])
        BVA, BOA, BVB, BOB = (REP[:, k, :] for k in range(4))

        W2T = sb("W2T", [128, E, FC, D])
        w1_kept = nc.dram_tensor("w1_kept", [E, 128, F], F32, kind="Internal").ap()

        class Placing:

            def __init__(self, tag, c):
                t = "p" + tag + "_"
                self.AFFB = sb(t + "AFFB", [128, C, E], c=c)
                self.AM, self.KM, self.POSF = (sb(t + n, [128, C], c=c) for n in ("AM", "KM", "POSF"))
                self.EQ, self.KEY, self.W, self.SEL = (sb(t + n, [128, C, E], c=c)
                                                       for n in ("EQ", "KEY", "W", "SEL"))
                self.OH = sb(t + "OH", [128, C, E], BF16, c=c)
                self.IDX = [sb(f"{t}IDX{i}", [128, C], I32, c=c) for i in range(2)]
                self.XS = [sb(f"{t}XS{i}", [128, C, ROW], c=c) for i in range(2)]
                self.kept, self.link, self.ranked, self.ids = (sem(t + n) for n in ("kept", "link", "ranked", "ids"))
                self.sent = [soft[f"{t}sent{i}"] for i in range(2)]
                self.free = [sem(f"{t}free{i}") for i in range(2)]

            def start(self, pool):
                for f in self.free:
                    pool.sem_inc(f, 1)

            def wait_free(self, eng, r):
                eng.wait_ge(self.free[r.par], r.half + 1)

            def keep(self, act, r, affv):
                act.wait_ge(affv, r.b + 1)
                nc.scalar.copy(AFF[:, ds(C * r.b, C), :], self.AFFB[:, :, :]).then_inc(self.kept, 1)

            def number(self, act, r):
                self.wait_free(act, r)
                nc.scalar.copy(self.XS[r.par][:, :, D:ROW], TOK[:, ds(C * r.b, C)][:, :, None]).then_inc(self.ids, 1)

            def choose(self, dve, r, steps, affv=None):
                wide = [128, C, E]
                code = CODE[:, None, :].broadcast_to(wide)
                for n in steps:
                    if n == 0:
                        dve.wait_ge(affv, r.b + 1)
                        i = nc.vector.tensor_reduce(self.AM[:, :], self.AFFB[:, :, :], axis=AX.X, op=ALU.max)
                    else:
                        dve.wait_ge(self.link, LINKS * r.b + n)
                    if n == 1:
                        i = nc.vector.tensor_tensor(self.EQ[:, :, :], self.AFFB[:, :, :],
                                                    self.AM[:, :, None].broadcast_to(wide), ALU.is_equal)
                    if n == 2:
                        i = nc.vector.tensor_tensor(self.KEY[:, :, :], self.EQ[:, :, :], code, ALU.mult)
                    if n == 3:
                        i = nc.vector.tensor_reduce(self.KM[:, :], self.KEY[:, :, :], axis=AX.X, op=ALU.max)
                    if n == 4:
                        i = nc.vector.tensor_tensor(self.OH[:, :, :], code, self.KM[:, :, None].broadcast_to(wide),
                                                    ALU.is_equal)
                    i.then_inc(self.link, 1)

            def rank(self, pe, r, ranks):
                pe.wait_ge(self.link, LINKS * r.b + 5)
                oh = self.OH[:, :, :].rearrange("p c e -> p (c e)")
                for n in range(1, C + 1):
                    nc.tensor.matmul(ranks[:, E * n:(C + 1) * E], ONES16[:, :], oh[:, 0:E * (C + 1 - n)],
                                     start=(n == 1), stop=False)
                nc.tensor.matmul(ranks[:, E:C * E], LOW16[:, :], oh[:, E:C * E], start=False, stop=False)
                i = nc.tensor.matmul(ranks[:, 0:E], LOW16[:, :], oh[:, 0:E], start=False, stop=True)
                i.then_inc(self.ranked, 1)

            def place(self, dve, r, ranks):
                dve.wait_ge(self.ranked, r.b + 1)
                dve.wait_ge(self.link, LINKS * r.b + 5)
                nc.vector.tensor_tensor(self.W[:, :, :], ranks[:, 0:C * E].rearrange("p (c e) -> p c e", c=C),
                                        CARRY[:, None, :].broadcast_to([128, C, E]), ALU.add).then_inc(self.link, 1)
                dve.wait_ge(self.link, LINKS * r.b + 6)
                nc.vector.tensor_tensor(self.SEL[:, :, :], self.W[:, :, :], self.OH[:, :, :],
                                        ALU.mult).then_inc(self.link, 1)
                nc.vector.tensor_tensor(CARRY[:, :], ranks[:, C * E:(C + 1) * E], CARRY[:, :],
                                        ALU.add).then_inc(self.link, 1)
                dve.wait_ge(self.link, LINKS * r.b + 7)
                nc.vector.tensor_reduce(self.POSF[:, :], self.SEL[:, :, :], axis=AX.X,
                                        op=ALU.add).then_inc(self.link, 1)
                dve.wait_ge(self.link, LINKS * r.b + 9)
                self.wait_free(dve, r)
                nc.vector.tensor_copy(self.IDX[r.par][:, :], self.POSF[:, :]).then_inc(self.link, 1)

            def send(self, pool, r):
                pool.wait_ge(self.link, LINKS * (r.b + 1))
                apart(pool, self.ids, r.b + 1, pool_passed)
                for c_ in range(C):
                    nc.gpsimd.indirect_dma_start(
                        sorted_x, bass.IndirectOffsetOnAxis(ap=self.IDX[r.par][:, c_:c_ + 1], axis=0),
                        self.XS[r.par][:, c_, :], None).then_inc(self.sent[r.par], 16)

            def release(self, pool, r):
                pool.wait_ge(self.sent[r.par], 16 * C * (r.half + 1))
                pool.sem_inc(self.free[r.par], 1)

        with ExitStack() as c0:
            W1N = sb("W1N", [128, 2, FC, D], c=c0)
            W2N = sb("W2N", [128, 2, F], c=c0)
            W1U = sb("W1U", [128, 2, F], c=c0)
            W1G = sb("W1G", [128, 2, F], c=c0)
            B1E = sb("B1E", [128, E, FC], c=c0)
            B1R = sb("B1R", [128, 2, FC, D], c=c0)
            B2R = sb("B2R", [128, E, D], c=c0)
            SM = sb("SMALL", [61, D], c=c0)
            HM = sb("HM", [1, H], c=c0)
            u_mask, u_maskv = sem("u_mask"), sem("u_maskv")
            WBN = sb("WBN", [128, 4, D], c=c0)
            DT = sb("DT", [128, 4], c=c0)
            u_con, u_small, u_w, u_rep, u_b2 = (sem("u_" + n) for n in ("con", "small", "w", "rep", "b2"))
            u_w1n = [sem(f"u_w1n{i}") for i in range(2)]
            u_w2n = [sem(f"u_w2n{i}") for i in range(2)]
            u_col, u_colv, u_wbt, u_wbv = sem("u_col"), sem("u_colv"), sem("u_wbt"), sem("u_wbv")
            u_w1t, u_w1u, u_w1g, u_w2t, u_w2v = (sem("u_" + n) for n in ("w1t", "w1u", "w1g", "w2t", "w2v"))
            u_b1, u_b1e, u_b1r, u_c2, u_c2v = (sem("u_" + n) for n in ("b1", "b1e", "b1r", "c2", "c2v"))
            u_dec, u_e, u_ones, u_zero, u_xz, u_x = (sem("u_" + n) for n in ("dec", "e", "ones", "zero", "xz", "x"))
            u_kept, u_carry, u_pad = [soft[f"u_kept{i}"] for i in range(2)], sem("u_carry"), sem("u_pad")
            block = c0.enter_context(nc.Block())

            @block.sync
            def _(sp):
                sp.dma_start(CON[:, :], consts).then_inc(u_con, 16)
                sp.dma_start(HM[:, :], head_mask[None, :]).then_inc(u_mask, 16)
                rows = [(ln_g, 1, 9), (ln_b, 9, 17), (b1.rearrange("e (c f) -> (e c) f", c=FC), 17, 49),
                        (cent, 49, 57), (bq_a[None, :], 57, 58), (bk_a[None, :], 58, 59),
                        ]
                for src, a, z in rows:
                    sp.dma_start(SM[a:z, :], src).then_inc(u_small, 16)
                with nc.allow_non_contiguous_dma(reason="256 numbers"):
                    for src, a in ((bq_b, 59), (bk_b, 60)):
                        sp.dma_start(SM[a:a + 1, :].rearrange("o (x s) -> o x s", s=SETS),
                                     src[None, :].rearrange("o (s x) -> o x s", s=SETS)).then_inc(u_small, 16)
                for k, w in enumerate((Wq_b, Wk_b, Wv_b, Wo_b)):
                    sp.dma_start(WBN[:, k, :], w).then_inc(u_w, 16)

                def load(r):
                    wait(sp, u_w1t, 1, r.b - 2)
                    sp.dma_start(W1N[:, r.par, :, :],
                                 w1[ds(r.b, 1), :, :].rearrange("e (c p) d -> p (e c) d", p=128)
                                 ).then_inc(u_w1n[r.par], 16)
                    wait(sp, u_w2t, 1, r.b - 2)
                    sp.dma_start(W2N[:, r.par, :],
                                 w2[ds(r.b, 1), :, :].rearrange("e d f -> (e d) f")).then_inc(u_w2n[r.par], 16)
                rounds(sp, 0, 2, 8, 7, load)
                sp.dma_start(X[:, :, :], x_in.rearrange("b (c p) d -> p (b c) d", p=128)).then_inc(u_x, 16)
                sp.wait_ge(u_pad, 1)
                sp.dma_start(sorted_x[SPARE:SPARE + 128 * (E - 1), :].rearrange("(n p) d -> p n d", p=128),
                             PADROW[:, E:PADS, :]).then_inc(u_xz, 16)
                sp.wait_ge(u_xz, 16)
                sp.wait_ge(u_x, 16)

            @block.scalar
            def _(act):
                for k, w in enumerate((Wq_a, Wk_a, Wv_a, Wo_a)):
                    act.dma_start(WA[:, k, :], w).then_inc(u_w, 16)
                for k, v in enumerate((bv_a, bo_a, bv_b, bo_b)):
                    act.dma_start(REP[:, k, :], v[None, :].broadcast_to([128, D])).then_inc(u_rep, 16)
                act.dma_start(B2R[:, :, :], b2[None, :, :].broadcast_to([128, E, D])).then_inc(u_b2, 16)
                act.dma_start(DT[:, 0:1], decay[None, :].broadcast_to([128, 1])).then_inc(u_rep, 16)
                act.wait_ge(u_rep, 80)
                nc.scalar.activation(DT[:, 1:2], DT[:, 0:1], ACT.Exp, scale=-1.0).then_inc(u_e, 1)
                act.wait_ge(u_wbt, 1)
                for k in range(2):
                    nc.scalar.copy(WB[:, k, :].rearrange("p (g d s) -> p g s d", g=G, s=SETS),
                                   quad[1][:, k, :].rearrange("p (s g d) -> p g s d", g=G, s=SETS))
                nc.scalar.copy(WB[:, 2, :], quad[1][:, 2, :]).then_inc(u_wbv, 1)
                act.wait_ge(u_colv, 1)
                nc.scalar.mul(WB[:, 3, :], quad[1][:, 3, :], MASKH).then_inc(u_wbv, 1)

                def take(r):
                    act.wait_ge(u_w1t, r.b + 1)
                    wait(act, u_b1, 1, r.b - 2)
                    wait(act, u_w1g, 1, r.b - 2)
                    nc.scalar.copy(W1U[:, r.par, :], bank[r.par][:, :]).then_inc(u_w1u, 1)
                    act.wait_ge(u_w2t, r.b + 1)
                    nc.scalar.copy(W2T[:, ds(r.b, 1), :, :].rearrange("p e c d -> p (e c) d"),
                                   quad[2 + r.par]).then_inc(u_w2v, 1)
                rounds(act, 0, 2, 8, 7, take)

            @block.gpsimd
            def _(pool):
                nc.gpsimd.memset(ONES[:, :], 1.0).then_inc(u_ones, 1)
                pool.wait_ge(u_mask, 16)
                nc.gpsimd.tensor_copy(SM[0:1, :].rearrange("o (h d) -> o h d", h=H),
                                      HM[:, :, None].broadcast_to([1, H, HD])).then_inc(u_maskv, 1)
                nc.gpsimd.memset(PADROW[:, :, 0:D], 0.0).then_inc(u_zero, 1)
                pool.wait_ge(u_con, 16)
                nc.gpsimd.tensor_copy(LOW16[:, :], LOW)
                nc.gpsimd.memset(ONES16[:, :], 1.0)
                nc.gpsimd.tensor_copy(PADROW[:, :, D:ROW], PADID[:, :, None]).then_inc(u_pad, 1)
                nc.gpsimd.tensor_copy(CARRY[:, :], REGION).then_inc(u_carry, 1)

                def keep(r):
                    apart(pool, u_w1g, r.b + 1, pool_passed)
                    nc.gpsimd.dma_start(w1_kept[ds(r.b, 1), :, :].rearrange("e p f -> (e p) f"),
                                        W1G[:, r.par, :]).then_inc(u_kept[r.par], 16)
                rounds(pool, 0, 2, 8, 7, keep)
                for i in range(2):
                    pool.wait_ge(u_kept[i], 16 * E // 2)

            @block.vector
            def _(dve):
                dve.wait_ge(u_col, 1)
                nc.vector.tensor_copy(COL[:, :], bank[0][:, 0:61]).then_inc(u_colv, 1)
                dve.wait_ge(u_e, 1)
                nc.vector.tensor_scalar_add(DT[:, 2:3], DT[:, 1:2], 1.0).then_inc(u_dec, 1)
                dve.wait_ge(u_dec, 1)
                nc.vector.reciprocal(DT[:, 3:4], DT[:, 2:3]).then_inc(u_dec, 1)
                dve.wait_ge(u_dec, 2)
                dve.wait_ge(u_con, 16)
                decays = DT[:, 3:4].broadcast_to([128, 129])
                nc.vector.tensor_tensor_scan(DEC[:, :], decays, IMP, 0.0, ALU.mult, ALU.add)
                nc.vector.tensor_tensor_scan(DROW[:, :], decays, IMP0, 0.0, ALU.mult, ALU.add).then_inc(u_dec, 1)
                dve.wait_ge(u_b2, 16)

                def gains(r):
                    dve.wait_ge(u_w1u, r.b + 1)
                    dve.wait_ge(u_colv, 1)
                    at_least(dve, u_kept[r.par], 16 * r.half)
                    nc.vector.tensor_scalar(W1G[:, r.par, :],
                                            W1U[:, r.par, :], LNG[:, ds(r.b, 1)], None,
                                            ALU.mult).then_inc(u_w1g, 1)

                def biases(r):
                    dve.wait_ge(u_b1, r.b + 1)
                    b1e = B1E[:, ds(r.b, 1), :].rearrange("p e c -> p (e c)")
                    nc.vector.tensor_tensor(b1e, bank[4 + r.par][:, 0:FC], B1T[:, ds(FC * r.b, FC)],
                                            ALU.add).then_inc(u_b1e, 1)
                    dve.wait_ge(u_b1e, r.b + 1)
                    apart(dve, u_c2, r.b - 1, dve_passed)
                    nc.vector.tensor_copy(B1R[:, r.par, :, :],
                                          b1e[:, :, None].broadcast_to([128, FC, D])).then_inc(u_b1r, 1)
                    nc.vector.tensor_scalar(NB1[:, ds(r.b, 1), :].rearrange("p e c -> p (e c)"), b1e, -1.0, None,
                                            ALU.mult)

                def step(t):
                    if (t + -1).within(E):
                        biases(t + -1)
                    if t.within(E):
                        gains(t)
                    if (t + -1).within(E):
                        r = t + -1
                        dve.wait_ge(u_c2, r.b + 1)
                        nc.vector.tensor_tensor(C2[:, ds(r.b, 1), :].rearrange("p e d -> p (e d)"),
                                                bank[6 + r.par][:, 0:D],
                                                B2R[:, ds(r.b, 1), :].rearrange("p e d -> p (e d)"),
                                                ALU.add).then_inc(u_c2v, 1)
                rounds(dve, 0, 3, 7, 8, step)

            @block.tensor
            def _(pe):
                pe.wait_ge(u_con, 16)
                pe.wait_ge(u_small, 128)
                pe.wait_ge(u_maskv, 1)
                nc.tensor.transpose(bank[0][:, 0:61], SM[:, :], ID[0:61, 0:61]).then_inc(u_col, 1)
                pe.wait_ge(u_w, 128)
                for k in range(4):
                    m = nc.tensor.transpose(quad[1][:, k, :], WBN[:, k, :], ID)
                m.then_inc(u_wbt, 1)
                pe.wait_ge(u_colv, 1)
                pe.wait_ge(u_wbv, 2)
                pe.wait_ge(u_ones, 1)

                def step(t):
                    r, z = t, t + -1
                    if r.within(E):
                        pe.wait_ge(u_w1n[r.par], 16 * (r.half + 1))
                        wait(pe, u_w1u, 1, r.b - 2)
                        for k in range(FC):
                            m = nc.tensor.transpose(bank[r.par][:, 128 * k:128 * k + 128], W1N[:, r.par, k, :], ID)
                        m.then_inc(u_w1t, 1)
                    if z.within(E):
                        pe.wait_ge(u_w1u, z.b + 1)
                        wait(pe, u_b1e, 1, z.b - 2)
                        for k in range(FC):
                            m = nc.tensor.matmul(bank[4 + z.par][:, k:k + 1], W1U[:, z.par, 128 * k:128 * k + 128],
                                                 LNB[:, ds(z.b, 1)], start=True, stop=True)
                        m.then_inc(u_b1, 1)
                    if r.within(E):
                        pe.wait_ge(u_w2n[r.par], 16 * (r.half + 1))
                        wait(pe, u_w2v, 1, r.b - 2)
                        for k in range(FC):
                            m = nc.tensor.transpose(quad[2 + r.par][:, k, :],
                                                    W2N[:, r.par, 128 * k:128 * k + 128], ID)
                        m.then_inc(u_w2t, 1)
                    if z.within(E):
                        pe.wait_ge(u_b1r, z.b + 1)
                        pe.wait_ge(u_w2v, z.b + 1)
                        wait(pe, u_c2v, 1, z.b - 2)
                        for k in range(FC):
                            m = nc.tensor.matmul(bank[6 + z.par][:, 0:D], B1R[:, z.par, k, :],
                                                 W2T[:, ds(z.b, 1), k, :].rearrange("p e d -> p (e d)"),
                                                 start=(k == 0), stop=(k == FC - 1))
                        m.then_inc(u_c2, 1)
                rounds(pe, 0, 3, 7, 8, step)

        with ExitStack() as c1:
            st = [sb(f"a_st{i}", [128, C, 6], c=c1) for i in range(2)]
            mv = [sb(f"a_mv{i}", [128, C, 2], c=c1) for i in range(2)]
            st1 = [sb(f"a_st1{i}", [128, C, 6], c=c1) for i in range(2)]
            mv1 = [sb(f"a_mv1{i}", [128, C, 2], c=c1) for i in range(2)]
            tmp = [sb(f"a_tmp{i}", [128, 8, C], c=c1) for i in range(2)]
            U = [sb(f"a_U{i}", [128, C, D], c=c1) for i in range(2)]
            UT = [sb(f"a_UT{i}", [128, S], c=c1) for i in range(2)]
            QT = [sb(f"a_QT{i}", [128, S], c=c1) for i in range(2)]
            QD = [sb(f"a_QD{i}", [128, C, 128], c=c1) for i in range(2)]
            KE = [sb(f"a_KE{i}", [128, S], c=c1) for i in range(2)]
            KR = [sb(f"a_KR{i}", [128, S], c=c1) for i in range(2)]
            KT = [sb(f"a_KT{i}", [128, S], c=c1) for i in range(2)]
            V = [sb(f"a_V{i}", [128, C, D], c=c1) for i in range(2)]
            KP = [sb(f"a_KP{i}", [128, C, D], c=c1) for i in range(2)]
            SM_ = [sb(f"a_SM{i}", [128, C, 128], c=c1) for i in range(2)]
            MEM = [sb(f"a_MEM{i}", [128, C - 1, D], c=c1) for i in range(2)]
            RT = [sb(f"a_RT{i}", [128, S], c=c1) for i in range(2)]
            U1 = [sb(f"a_U1{i}", [128, C, D], c=c1) for i in range(2)]
            U1T = [sb(f"a_U1T{i}", [128, S], c=c1) for i in range(2)]
            (stats, aggr, veps, rstd, u_done, xbo, uT, uTv, q_mm, qv, qd, k_mm, ke, kr, kt, v_mm, vv,
             s_mm, sm, kT_mm, kp, U_mm, mem, r_mm, rtv, o_mm, x1, stats1, aggr1, chain1, rstd1, u1, base,
             u1T_mm, u1Tv, aff_mm, affv) = (sem("a_" + n) for n in (
                 "stats aggr veps rstd u xbo uT uTv q qv qd k ke kr kt v vv s sm kT kp U mem r rtv o x1 "
                 "stats1 aggr1 chain1 rstd1 u1 base u1T u1Tv aff affv").split())
            block = c1.enter_context(nc.Block())
            LO, HI, END = 3, 7, 10
            placing = Placing("a", c1)
            xs_done = sem("a_xs")
            RANKS = bank[7][:, 0:(C + 1) * E]
            AFFP = bank[6][:, (C - 1) * D:(C - 1) * D + C * E]

            @block.vector
            def _(dve):
                def xs(r, c):
                    return X[:, ds(C * r.b + c, 1), :].rearrange("p o d -> p (o d)")

                def input_stats(r):
                    for c in range(C):
                        i = nc.vector.bn_stats(st[r.par][:, c, :], xs(r, c))
                    i.then_inc(stats, 1)
                    dve.wait_ge(stats, r.b + 1)
                    apart(dve, rstd, r.b - 1, dve_passed)
                    for c in range(C):
                        i = nc.vector.bn_aggr(mv[r.par][:, c, :], st[r.par][:, c, :])
                    i.then_inc(aggr, 1)

                def normalise(r):
                    dve.wait_ge(rstd, r.b + 1)
                    wait(dve, uT, 1, r.b - 2)
                    for c in range(C):
                        i = nc.vector.tensor_scalar(U[r.par][:, c, :], xs(r, c), mv[r.par][:, c, 0:1],
                                                    tmp[r.par][:, 0, c:c + 1], ALU.subtract, ALU.mult)
                    i.then_inc(u_done, 1)

                def residual(r):
                    dve.wait_ge(o_mm, r.b + 1)
                    dve.wait_ge(xbo, r.b + 1)
                    nc.vector.tensor_tensor(X[:, ds(C * r.b, C), :], quad[7], X[:, ds(C * r.b, C), :],
                                            ALU.add).then_inc(x1, 1)
                    apart(dve, x1, r.b + 1, dve_passed)
                    for c in range(C):
                        i = nc.vector.bn_stats(st1[r.par][:, c, :], xs(r, c))
                    i.then_inc(stats1, 1)
                    dve.wait_ge(stats1, r.b + 1)
                    apart(dve, rstd1, r.b, dve_passed)
                    for c in range(C):
                        i = nc.vector.bn_aggr(mv1[r.par][:, c, :], st1[r.par][:, c, :])
                    i.then_inc(aggr1, 1)

                def ffn_inputs(r):
                    dve.wait_ge(rstd1, r.b + 1)
                    placing.wait_free(dve, r)
                    wait(dve, u1T_mm, 1, r.b - 1)
                    wait(dve, base, 1, r.b - 1)
                    for c in range(C):
                        i = nc.vector.tensor_scalar(U1[r.par][:, c, :], xs(r, c), mv1[r.par][:, c, 0:1],
                                                    tmp[r.par][:, 2, c:c + 1], ALU.subtract, ALU.mult)
                    i.then_inc(u1, 1)

                def rows(r):
                    for c in range(C):
                        nc.vector.tensor_scalar(placing.XS[r.par][:, c, 0:D],
                                                xs(r, c), mv1[r.par][:, c, 0:1],
                                                tmp[r.par][:, 7, c:c + 1], ALU.subtract, ALU.mult
                                                ).then_inc(xs_done, 1)

                def step(t):
                    f, m, z, y = t, t + -1, t + -2, t + -3
                    if z.within(B):
                        residual(z)
                    if y.within(B):
                        placing.choose(dve, y, (0, 1, 2, 3, 4), affv)
                    if m.within(B):
                        dve.wait_ge(s_mm, m.b + 1)
                        wait(dve, r_mm, 1, m.b - 2)
                        nc.vector.tensor_tensor(SM_[m.par][:, :, :], quad[4],
                                                DEC[:, None, 0:128].broadcast_to([128, C, 128]),
                                                ALU.mult).then_inc(sm, 1)
                    if (t + 1).within(B):
                        input_stats(t + 1)
                    if m.within(B):
                        dve.wait_ge(U_mm, m.b + 1)
                        for c in range(C - 1):
                            if c == 0:
                                i = nc.vector.tensor_copy(MEM[m.par][:, 0, :], quad[6][:, 0, :])
                            else:
                                dve.wait_ge(mem, (C - 1) * m.b + c)
                                i = nc.vector.scalar_tensor_tensor(
                                    MEM[m.par][:, c, :], MEM[m.par][:, c - 1, :], DROW[:, 128:129],
                                    quad[6][:, c, :], ALU.mult, ALU.add)
                            i.then_inc(mem, 1)
                    if f.within(B):
                        dve.wait_ge(ke, f.b + 1)
                        dve.wait_ge(kr, f.b + 1)
                        wait(dve, kT_mm, 1, f.b - 2)
                        nc.vector.scalar_tensor_tensor(KT[f.par][:, :], KE[f.par][:, :], 1.0, KR[f.par][:, :],
                                                       ALU.min, ALU.add).then_inc(kt, 1)
                    if z.within(B):
                        ffn_inputs(z)
                    if f.within(B):
                        dve.wait_ge(v_mm, f.b + 1)
                        nc.vector.tensor_tensor(V[f.par][:, :, :], quad[3],
                                                BVA[:, None, :].broadcast_to([128, C, D]), ALU.add).then_inc(vv, 1)
                    if y.within(B):
                        placing.place(dve, y, RANKS)
                    if (t + 1).within(B):
                        normalise(t + 1)
                    if z.within(B):
                        rows(z)
                    if z.within(B):
                        dve.wait_ge(aff_mm, z.b + 1)
                        wait(dve, placing.kept, 1, z.b - 1)
                        nc.vector.tensor_copy(placing.AFFB[:, :, :],
                                              AFFP.rearrange("p (c e) -> p c e", c=C)).then_inc(affv, 1)
                input_stats(Round(0, 0, 0))
                normalise(Round(0, 0, 0))
                rounds(dve, 0, LO, HI, END, step)

            @block.gpsimd
            def _(pool):
                def input_rstd(r):
                    pool.wait_ge(aggr, r.b + 1)
                    wait(pool, u_done, 1, r.b - 2)
                    nc.gpsimd.tensor_tensor(tmp[r.par][:, 1, :], mv[r.par][:, :, 1], EPS1, ALU.add).then_inc(veps, 1)
                    pool.wait_ge(veps, r.b + 1)
                    nc.gpsimd.tensor_tensor(tmp[r.par][:, 0, :], tmp[r.par][:, 1, :], MHALF,
                                            ALU.pow).then_inc(rstd, 1)

                def ffn_rstd(r):
                    tt, n = tmp[r.par], [0]
                    pool.wait_ge(aggr1, r.b + 1)
                    wait(pool, xs_done, C, r.b - 1)

                    def op(o, a, b_, f):
                        nc.gpsimd.tensor_tensor(o, a, b_, f).then_inc(chain1, 1)
                        n[0] += 1
                        pool.wait_ge(chain1, 6 * r.b + n[0])
                    op(tt[:, 3, :], mv1[r.par][:, :, 1], EPS1, ALU.add)
                    op(tt[:, 2, :], tt[:, 3, :], MHALF, ALU.pow)
                    op(tt[:, 4, :], mv1[r.par][:, :, 1], tt[:, 2, :], ALU.mult)
                    op(tt[:, 5, :], tt[:, 4, :], tt[:, 2, :], ALU.mult)
                    op(tt[:, 6, :], tt[:, 5, :], EPS1, ALU.add)
                    op(tt[:, 3, :], tt[:, 6, :], MHALF, ALU.pow)
                    nc.gpsimd.tensor_tensor(tt[:, 7, :], tt[:, 3, :], tt[:, 2, :], ALU.mult).then_inc(rstd1, 1)

                def step(t):
                    f, z, y = t, t + -2, t + -3
                    if z.within(B):
                        ffn_rstd(z)
                    if (t + 1).within(B):
                        input_rstd(t + 1)
                    if f.within(B):
                        xb = X[:, ds(C * f.b, C), :]
                        pool.wait_ge(u_done, f.b + 1)
                        nc.gpsimd.tensor_tensor(xb, xb, BOA[:, None, :].broadcast_to([128, C, D]),
                                                ALU.add).then_inc(xbo, 1)
                        pool.wait_ge(qv, f.b + 1)
                        wait(pool, r_mm, 1, f.b - 2)
                        nc.gpsimd.tensor_tensor(QD[f.par][:, :, :],
                                                QT[f.par][:, :].rearrange("p (c t) -> p c t", c=C),
                                                DROW[:, None, 0:128].broadcast_to([128, C, 128]),
                                                ALU.mult).then_inc(qd, 1)
                    if y.within(B):
                        placing.send(pool, y)
                    if z.within(B):
                        xb = X[:, ds(C * z.b, C), :]
                        pool.wait_ge(xs_done, C * (z.b + 1))
                        nc.gpsimd.tensor_tensor(xb, xb, U1[z.par][:, :, :], ALU.add).then_inc(base, 1)
                    if y.within(B):
                        placing.release(pool, y)
                placing.start(pool)
                input_rstd(Round(0, 0, 0))
                rounds(pool, 0, LO, HI, END, step)

            @block.scalar
            def _(act):
                def step(t):
                    if (t + -3).within(B):
                        placing.keep(act, t + -3, affv)
                    if t.within(B):
                        r = t
                        act.wait_ge(uT, r.b + 1)
                        wait(act, v_mm, 1, r.b - 2)
                        nc.scalar.copy(UT[r.par][:, :], bank[0][:, :]).then_inc(uTv, 1)
                    if (t + -1).within(B):
                        r = t + -1
                        act.wait_ge(kT_mm, r.b + 1)
                        wait(act, U_mm, 1, r.b - 2)
                        nc.scalar.mul(KP[r.par][:, :, :], quad[3], DEC[:, 128:129]).then_inc(kp, 1)
                    if t.within(B):
                        r = t
                        act.wait_ge(q_mm, r.b + 1)
                        wait(act, s_mm, 1, r.b - 2)
                        wait(act, qd, 1, r.b - 2)
                        nc.scalar.activation(QT[r.par][:, :], bank[1][:, :], ACT.Identity, bias=BQA).then_inc(qv, 1)
                        act.wait_ge(k_mm, r.b + 1)
                        wait(act, kt, 1, r.b - 2)
                        nc.scalar.activation(KE[r.par][:, :], bank[2][:, :], ACT.Exp, bias=BKA).then_inc(ke, 1)
                        nc.scalar.activation(KR[r.par][:, :], bank[2][:, :], ACT.Relu, bias=BKA).then_inc(kr, 1)
                    if (t + -1).within(B):
                        r = t + -1
                        act.wait_ge(r_mm, r.b + 1)
                        wait(act, o_mm, 1, r.b - 2)
                        nc.scalar.copy(RT[r.par][:, :], bank[5][:, :]).then_inc(rtv, 1)
                    if (t + -2).within(B):
                        r = t + -2
                        act.wait_ge(u1T_mm, r.b + 1)
                        wait(act, aff_mm, 1, r.b - 1)
                        nc.scalar.copy(U1T[r.par][:, :], bank[0][:, :]).then_inc(u1Tv, 1)
                        placing.number(act, r)
                rounds(act, 0, LO, HI, END, step)

            @block.tensor
            def _(pe):
                def step(t):
                    f, m, z = t, t + -1, t + -2
                    if f.within(B):
                        pe.wait_ge(u_done, f.b + 1)
                        wait(pe, u1Tv, 1, f.b - 3)
                        if not isinstance(f.b, int) or f.b >= 1:
                            wait(pe, uTv, 1, f.b - 1)
                        for c in range(C):
                            i = nc.tensor.transpose(quad[0][:, c, :], U[f.par][:, c, :], ID)
                        i.then_inc(uT, 1)
                    if z.within(B):
                        pe.wait_ge(rtv, z.b + 1)
                        if not f.within(B):
                            at_least(pe, placing.link, LINKS * (t.b - 4) + 8)
                        for c in range(C):
                            i = nc.tensor.matmul(quad[7][:, c, :], RT[z.par][:, 128 * c:128 * c + 128],
                                                 WA[:, 3, :], start=True, stop=True)
                        i.then_inc(o_mm, 1)
                    if m.within(B):
                        pe.wait_ge(qv, m.b + 1)
                        pe.wait_ge(kt, m.b + 1)
                        wait(pe, sm, 1, m.b - 1)
                        for c in range(C):
                            sl = slice(128 * c, 128 * c + 128)
                            i = nc.tensor.matmul(quad[4][:, c, :], KT[m.par][:, sl], QT[m.par][:, sl],
                                                 start=True, stop=True)
                        i.then_inc(s_mm, 1)
                        pe.wait_ge(vv, m.b + 1)
                        for c in range(C):
                            i = nc.tensor.transpose(quad[3][:, c, :], KT[m.par][:, 128 * c:128 * c + 128], ID)
                        i.then_inc(kT_mm, 1)
                    if f.within(B):
                        pe.wait_ge(uTv, f.b + 1)
                        wait(pe, qv, 1, f.b - 1)
                        nc.tensor.matmul(bank[1][:, :], WA[:, 0, :], UT[f.par][:, :], start=True,
                                         stop=True).then_inc(q_mm, 1)
                        wait(pe, kr, 1, f.b - 1)
                        wait(pe, ke, 1, f.b - 1)
                        nc.tensor.matmul(bank[2][:, :], WA[:, 1, :], UT[f.par][:, :], start=True,
                                         stop=True).then_inc(k_mm, 1)
                    if m.within(B):
                        pe.wait_ge(kp, m.b + 1)
                        wait(pe, mem, C - 1, m.b - 1)
                        wait(pe, affv, 1, m.b - 2)
                        for c in range(C - 1):
                            i = nc.tensor.matmul(quad[6][:, c, :], KP[m.par][:, c, :], V[m.par][:, c, :],
                                                 start=True, stop=True)
                        i.then_inc(U_mm, 1)
                    if z.within(B):
                        pe.wait_ge(x1, z.b + 1)
                    if (t + -3).within(B):
                        placing.rank(pe, t + -3, RANKS)
                    if f.within(B):
                        wait(pe, kp, 1, f.b - 1)
                        for c in range(C):
                            i = nc.tensor.matmul(quad[3][:, c, :], UT[f.par][:, 128 * c:128 * c + 128],
                                                 WA[:, 2, :], start=True, stop=True)
                        i.then_inc(v_mm, 1)
                    if m.within(B):
                        pe.wait_ge(sm, m.b + 1)
                        pe.wait_ge(qd, m.b + 1)
                        wait(pe, rtv, 1, m.b - 1)
                        for c in range(C):
                            i = nc.tensor.matmul(quad[5][:, c, :], V[m.par][:, c, :], SM_[m.par][:, c, :],
                                                 start=True, stop=(c == 0))
                            if c:
                                pe.wait_ge(mem, (C - 1) * m.b + c)
                                i = nc.tensor.matmul(quad[5][:, c, :], MEM[m.par][:, c - 1, :],
                                                     QD[m.par][:, c, :], start=False, stop=True)
                        i.then_inc(r_mm, 1)
                    if z.within(B):
                        pe.wait_ge(u1, z.b + 1)
                        if f.within(B):
                            pe.wait_ge(uTv, f.b + 1)
                        else:
                            wait(pe, u1Tv, 1, z.b - 1)
                        for c in range(C):
                            i = nc.tensor.transpose(quad[0][:, c, :], U1[z.par][:, c, :], ID)
                        i.then_inc(u1T_mm, 1)
                        pe.wait_ge(u1Tv, z.b + 1)
                        for c in range(C):
                            i = nc.tensor.matmul(AFFP[:, E * c:E * c + E], U1T[z.par][:, 128 * c:128 * c + 128],
                                                 CENT, start=True, stop=True)
                        i.then_inc(aff_mm, 1)
                rounds(pe, 0, LO, HI, END, step)

        def route(tag, used=()):
            with ExitStack() as c:
                AM = sb(f"AM{tag}", [128, NT], c=c)
                EX = sb(f"EX{tag}", [128, NT], c=c)
                EX1 = sb(f"EX1{tag}", [128, NT], c=c)
                CNT = sb(f"CNT{tag}", [128, E], c=c)
                GT = sb(f"GT{tag}", [128, E, NT], c=c)
                N_T = sb(f"N_T{tag}", [128, E], c=c)
                CUM = sb(f"CUM{tag}", [128, E], c=c)
                WG = sb(f"WG{tag}", [128, E], c=c)
                CMP = sb(f"CMP{tag}", [1, TILES, E], c=c)
                CMPW = sb(f"CMPW{tag}", [1, TILES, E], c=c)
                TEF = sb(f"TEF{tag}", [1, TILES], c=c)
                TR = sb(f"TR{tag}", [1, 2, TILES], c=c)
                PADF = sb(f"PADF{tag}", [128, E], c=c)
                PADI = sb(f"PADI{tag}", [128, E], I32, c=c)
                amax, exd, chain, pads = (sem(f"r{tag}_{n}") for n in ("amax", "exd", "chain", "pads"))
                padded = soft[f"r{tag}_padded"]
                block = c.enter_context(nc.Block())

                @block.vector
                def _(dve):
                    n = [0]

                    def link(i):
                        i.then_inc(chain, 1)
                        n[0] += 1
                        dve.wait_ge(chain, n[0])
                    wide = [1, TILES, E]
                    link(nc.vector.tensor_tensor(PADF[:, :], CARRY[:, :], PART, ALU.add))
                    nc.vector.tensor_copy(PADI[:, :], PADF[:, :]).then_inc(pads, 1)
                    nc.vector.tensor_reduce(AM[:, :], AFF[:, :, :], axis=AX.X, op=ALU.max).then_inc(amax, 1)
                    link(nc.vector.tensor_tensor(CNT[:, :], CARRY[:, :], REGION, ALU.subtract))
                    link(nc.vector.tensor_tensor(GT[:, :, :], CNT[:, :, None].broadcast_to([128, E, NT]),
                                                 STEPS[:, None, :].broadcast_to([128, E, NT]), ALU.is_gt))
                    link(nc.vector.tensor_reduce(N_T[:, :], GT[:, :, :], axis=AX.X, op=ALU.add))
                    link(nc.vector.tensor_tensor_scan(CUM[:, :], ONES[:, 0:E], N_T[:, :], 0.0, ALU.mult, ALU.add))
                    link(nc.vector.tensor_tensor(CMP[:, :, :], ROW39[0:1, :, None].broadcast_to(wide),
                                                 CUM[0:1, None, :].broadcast_to(wide), ALU.is_ge))
                    link(nc.vector.tensor_reduce(TEF[:, :], CMP[:, :, 0:E - 1], axis=AX.X, op=ALU.add))
                    nc.vector.tensor_copy(TE[:, :], TEF[:, :])
                    link(nc.vector.scalar_tensor_tensor(WG[:, :], N_T[:, :], -128.0, JUMP, ALU.mult, ALU.add))
                    link(nc.vector.tensor_tensor(CMPW[:, :, :], CMP[:, :, :], WG[0:1, None, :].broadcast_to(wide),
                                                 ALU.mult))
                    link(nc.vector.tensor_reduce(TR[:, 0, :], CMPW[:, :, :], axis=AX.X, op=ALU.add))
                    link(nc.vector.scalar_tensor_tensor(TR[:, 1, :], ROW39[0:1, :], 128.0, TR[:, 0, :],
                                                        ALU.mult, ALU.add))
                    nc.vector.tensor_copy(TROW[:, :], TR[:, 1, :])
                    dve.wait_ge(exd, 1)
                    link(nc.vector.tensor_scalar_add(EX1[:, :], EX[:, :], 1.0))
                    nc.vector.reciprocal(ALPHA[:, :], EX1[:, :])
                    nc.vector.tensor_copy(CARRY[:, :], REGION)
                    if tag == 1:
                        nc.vector.tensor_copy(KS[1][0:STACK, :, :, :],
                                              ID[0:STACK, None, PARTS:STACK, None].broadcast_to([STACK, SETS, G, S]))

                @block.scalar
                def _(act):
                    act.wait_ge(amax, 1)
                    nc.scalar.activation(EX[:, :], AM[:, :], ACT.Exp, scale=-1.0).then_inc(exd, 1)
                    if tag == 1:
                        nc.scalar.copy(KS[0][0:STACK, :, :, :],
                                       ID[0:STACK, None, PARTS:STACK, None].broadcast_to([STACK, SETS, G, S]))
                        for p in range(2):
                            nc.scalar.copy(VA[p][:, :, :, HD:AUG],
                                           IMP0[:, None, None, 0:AUG - HD].broadcast_to([128, C, H, AUG - HD]))

                @block.sync
                def _(sp):
                    for s_ in used:
                        sp.sem_clear(s_)

                @block.gpsimd
                def _(pool):
                    apart(pool, pads, 1, pool_passed)
                    for e in range(E):
                        nc.gpsimd.indirect_dma_start(
                            sorted_x, bass.IndirectOffsetOnAxis(ap=PADI[:, e:e + 1], axis=0),
                            PADROW[:, e, :], None).then_inc(padded, 16)
                    pool.wait_ge(padded, 16 * E)

        NB = 3

        def experts(tag):
            with ExitStack() as c:
                XT_IN = [sb(f"f{tag}_x{i}", [128, ROW], c=c) for i in range(NB)]
                W1B = [sb(f"f{tag}_w{i}", [128, F], c=c) for i in range(NB)]
                XT = [sb(f"f{tag}_xt{i}", [128, 128], c=c) for i in range(NB)]
                HM = [sb(f"f{tag}_h{i}", [128, FC, 128], c=c) for i in range(NB)]
                Y = [sb(f"f{tag}_y{i}", [128, D], c=c) for i in range(NB)]
                TO = [sb(f"f{tag}_to{i}", [128, 1], I32, c=c) for i in range(NB)]
                x_in_ = [sem(f"f{tag}_xin{i}") for i in range(NB)]
                w_in = [sem(f"f{tag}_win{i}") for i in range(NB)]
                y_out = [soft[f"f{tag}_yout{i}"] for i in range(NB)]
                xt_mm, xtv, h_mm, hv, y_mm, yv = (sem(f"f{tag}_" + n) for n in ("xt", "xtv", "h", "hv", "y", "yv"))
                XB, HB, YB = (0, 1, 0), (3, 4, 5), (2, 6, 7)
                block = c.enter_context(nc.Block())

                def tiles(eng, body, lag):
                    for t in range(2 * NB):
                        body(t, t // NB, t % NB)
                    with eng.Fori(2, TILES // NB) as i:
                        for k in range(NB):
                            body(NB * i + k, i, k)
                    for t in range(TILES, TILES + lag):
                        body(t, t // NB, t % NB)

                def back(t, use, k, lag):
                    if isinstance(t, int) and not 0 <= t - lag < TILES:
                        return None
                    return t - lag, use - (1 if k < lag else 0), (k - lag) % NB

                def first_row(eng, t):
                    return eng.value_load(TROW[0:1, ds(t, 1)], min_val=0, max_val=SPARE + 128 * (E - 2))

                def expert(eng, t):
                    return eng.value_load(TE[0:1, ds(t, 1)], min_val=0, max_val=E - 1)

                @block.sync
                def _(sp):
                    def load(t, use, k):
                        row = first_row(sp, t)
                        at_least(sp, xt_mm, t - 2)
                        at_least(sp, xtv, t - 2)
                        sp.dma_start(XT_IN[k][:, :], sorted_x[ds(row, 128), :]).then_inc(x_in_[k], 16)
                    tiles(sp, load, 0)

                @block.gpsimd
                def _(pool):
                    def store(t, use, k):
                        apart(pool, yv, t + 1, pool_passed)
                        nc.gpsimd.indirect_dma_start(
                            y_tok, bass.IndirectOffsetOnAxis(ap=TO[k][:, 0:1], axis=0),
                            Y[k][:, :], None).then_inc(y_out[k], 16)
                    tiles(pool, store, 0)
                    for k in range(NB):
                        pool.wait_ge(y_out[k], 16 * TILES // NB)

                @block.scalar
                def _(act):
                    def step(t, use, k):
                        z = back(t, use, k, 0)
                        if z:
                            e = expert(act, t)
                            at_least(act, h_mm, t - 2)
                            act.dma_start(W1B[k][:, :], w1_kept[ds(e, 1), :, :].rearrange("e p f -> (e p) f")
                                          ).then_inc(w_in[k], 16)
                        z = back(t, use, k, 1)
                        if z:
                            j, _, kk = z
                            act.wait_ge(xt_mm, j + 1)
                            at_least(act, h_mm, j - 2)
                            nc.scalar.copy(IDS[:, ds(j, 1)], XT_IN[kk][:, D:ROW])
                            nc.scalar.copy(XT[kk][:, :], bank[XB[kk]][:, 0:128]).then_inc(xtv, 1)
                    tiles(act, step, 1)

                @block.vector
                def _(dve):
                    def step(t, use, k):
                        z = back(t, use, k, 0)
                        if z:
                            e = expert(dve, z[0])
                            dve.wait_ge(h_mm, z[0] + 1)
                            at_least(dve, y_mm, z[0] - 2)
                            nc.vector.tensor_tensor(
                                HM[k][:, :, :], quad[HB[k]],
                                NB1[:, ds(e, 1), :].rearrange("p e c -> p (e c)")[:, :, None]
                                .broadcast_to([128, FC, 128]), ALU.max).then_inc(hv, 1)
                        z = back(t, use, k, 1)
                        if z:
                            e = expert(dve, z[0])
                            dve.wait_ge(y_mm, z[0] + 1)
                            at_least(dve, y_out[z[2]], 16 * z[1])
                            apart(dve, xtv, z[0] + 1, dve_passed)
                            nc.vector.tensor_copy(TO[z[2]][:, :], IDS[:, ds(z[0], 1)])
                            nc.vector.tensor_tensor(Y[z[2]][:, :], bank[YB[z[2]]][:, 0:D],
                                                    C2[:, ds(e, 1), :].rearrange("p e d -> p (e d)"),
                                                    ALU.add).then_inc(yv, 1)
                    tiles(dve, step, 1)

                @block.tensor
                def _(pe):
                    def step(t, use, k):
                        z = back(t, use, k, 0)
                        if z:
                            pe.wait_ge(x_in_[k], 16 * (use + 1))
                            at_least(pe, xtv, t - (0, 2, 1)[k])
                            nc.tensor.transpose(bank[XB[k]][:, 0:128], XT_IN[k][:, 0:D], ID).then_inc(xt_mm, 1)
                        z = back(t, use, k, 1)
                        if z:
                            j, u, kk = z
                            pe.wait_ge(w_in[kk], 16 * (u + 1))
                            pe.wait_ge(xtv, j + 1)
                            at_least(pe, hv, j - 2)
                            for f in range(FC):
                                m = nc.tensor.matmul(quad[HB[kk]][:, f, :], W1B[kk][:, 128 * f:128 * f + 128],
                                                     XT[kk][:, :], start=True, stop=True)
                            m.then_inc(h_mm, 1)
                        z = back(t, use, k, 2)
                        if z:
                            j, u, kk = z
                            e = expert(pe, j)
                            pe.wait_ge(hv, j + 1)
                            at_least(pe, yv, j - 2)
                            for f in range(FC):
                                m = nc.tensor.matmul(bank[YB[kk]][:, 0:D], HM[kk][:, f, :],
                                                     W2T[:, ds(e, 1), f, :].rearrange("p e d -> p (e d)"),
                                                     start=(f == 0), stop=(f == FC - 1))
                            m.then_inc(y_mm, 1)
                    tiles(pe, step, 2)

        def attention():
            with ExitStack() as c:
                def two(name, shape, dt=F32):
                    return [sb(f"b_{name}{i}", shape, dt, c=c) for i in range(2)]
                placing = Placing("b", c)
                GA = [sb("b_GA", [128, C, D], c=c)] * 2
                st, mv, st3, mv3 = two("st", [128, C, 6]), two("mv", [128, C, 2]), two("st3", [128, C, 6]), \
                    two("mv3", [128, C, 2])
                tmp = two("tmp", [128, 8, C])
                U2, U2T = [sb("b_U2", [128, C, D], c=c)] * 2, [sb("b_U2T", [128, S], c=c)] * 2
                QF, KF = sb("b_QF", [128, S], c=c), sb("b_KF", [128, S], c=c)
                QHI, QLO = sb("b_QHI", [128, S], F32R, c=c), sb("b_QLO", [128, S], F32R, c=c)
                KHI, KLO = sb("b_KHI", [128, S], F32R, c=c), sb("b_KLO", [128, S], F32R, c=c)
                QS = two("QS", [128, SETS, S], F32R)
                NM = two("NM", [128, SETS, C, G])
                P = two("P", [128, G, S])
                OSB = two("OSB", [128, S])
                RC = two("RC", [128, C, G])
                AT, ATB = [sb("b_AT", [128, C, D], c=c)] * 2, [sb("b_ATB", [128, C, D], c=c)] * 2
                ATT, U3 = [sb("b_ATT", [128, S], c=c)] * 2, [sb("b_U3", [128, C, D], c=c)] * 2
                U3T = [sb("b_U3T", [128, S], c=c)] * 2
                (x2, xbo, stats, aggr, veps, rstd, u2, u2T_mm, u2Tv, q_mm, qf, k_mm, kf, q_parts, k_parts,
                 q_stack, k_stack, v_mm, vv, mx_mm, mx, s_mm, exps, av, o_v,
                 otr_mm, rc, otr_v, atb, att_mm, att_v, o_mm, x3, stats3, aggr3, chain3, rstd3, u3, base,
                 u3T_mm, u3Tv, aff_mm, affv) = (sem("b_" + n) for n in (
                     "x2 xbo stats aggr veps rstd u2 u2T u2Tv q qf k kf q_parts k_parts "
                     "q_stack k_stack v vv mx_mm mx s exps av o_v "
                     "otr rc otr_v atb att att_v o x3 stats3 aggr3 chain3 rstd3 u3 base "
                     "u3T u3Tv aff affv").split())
                mt_mm = sem("b_mt_mm")
                q_hi, k_hi = sem("b_q_hi"), sem("b_k_hi")
                mt_v = sem("b_mt_v")
                y_here, diff, diff3 = sem("b_y_here"), sem("b_diff"), sem("b_diff3")
                O, MISC = bank[6], bank[7]
                MQ = quad[7]
                SLOTS = SETS * C
                misc = [(0, "q", 1, 0), (1, "otr", -1, 3), (2, "mt", 0, 1), (3, "k", 1, 0),
                        (5, "att", -1, 0), (6, "wo", -1, 0), (7, "mt", 0, 2), (8, "otr", 0, 0), (9, "otr", 0, 1),
                        (10, "mt", 0, 3), (11, "u3T", -1, 0), (12, "aff", -1, 0), (13, "otr", 0, 2),
                        (14, "mt", 1, 0), (14, "v", 1, 0), (15, "u2T", 2, 0), (15, "rank", -1, 0)]
                RANKS = MISC[:, 0:(C + 1) * E]
                taken = {"u2T": (u2Tv, 1, 0), "otr": (otr_v, SETS, 0), "mt": (mt_v, SETS, 0), "q": (qf, 1, 0),
                         "k": (kf, 1, 0), "att": (att_v, 1, 0), "wo": (x3, 1, 0), "v": (vv, 1, 0),
                         "u3T": (u3Tv, 1, 0), "aff": (affv, 1, 0), "rank": (placing.link, LINKS, 7)}

                def uses(t, k):
                    return [(what, t + ahead, s) for slot, what, ahead, s in misc
                            if slot == k and (t + ahead).within(B)]

                def misc_free(pe, t, use):
                    for back_ in range(1, 3 * len(misc)):
                        n = use - back_
                        _, what, ahead, s = misc[n % len(misc)]
                        r = t + n // len(misc) + ahead
                        if isinstance(r.b, int) and not 0 <= r.b < B:
                            continue
                        signal, per, more = taken[what]
                        at_least(pe, signal, per * r.b + s + 1 + more)
                        return

                def m_slot(t, k):
                    return (t, 2 + k // C) if k < SLOTS // 2 else (t + 1, k // C - 2)
                FIRST, LO, HI, END = -2, 2, 6, 9
                block = c.enter_context(nc.Block())

                @block.sync
                def _(sp):

                    def stack(r, what, parts, src_ready, done, per):
                        apart(sp, src_ready, r.b + 1, sp_passed)
                        apart(sp, done, 16 * per * r.b, sp_passed)
                        apart(sp, s_mm, 2 * SLOTS * (r.b - 1), sp_passed)
                        for n, part in enumerate(parts):
                            if what == "q":
                                sp.dma_start(QS[r.par][32 * n:32 * n + 32, :, :].bitcast(F32),
                                             part[:, :].bitcast(F32)).then_inc(done, 16)
                                continue
                            for g in range(G):
                                z = 32 * n + HD * g
                                sp.dma_start(KS[r.par][z:z + HD, :, g, :].bitcast(F32),
                                             part[32 * g:32 * g + 32, :].bitcast(F32)).then_inc(done, 16)

                    def step(t):
                        if (t + 2).within(B):
                            r = t + 2
                            wait(sp, x2, C, r.b - 1)
                            sp.dma_start(GA[r.par][:, :, :], y_tok[ds(S * r.b, S), :]
                                         .rearrange("(c p) d -> p c d", p=128)).then_inc(y_here, 16)
                        if (t + 1).within(B):
                            stack(t + 1, "q", (QHI, QHI, QLO), q_parts, q_stack, 3)
                            stack(t + 1, "k", (KHI, KLO, KHI), k_parts, k_stack, 3 * G)
                    rounds(sp, FIRST, LO, HI, END, step)

                @block.gpsimd
                def _(pool):
                    def rstd_in(r):
                        pool.wait_ge(aggr, C * (r.b + 1))
                        wait(pool, u2, 1, r.b - 2)
                        nc.gpsimd.tensor_tensor(tmp[r.par][:, 1, :], mv[r.par][:, :, 1], EPS1, ALU.add).then_inc(veps, 1)
                        pool.wait_ge(veps, r.b + 1)
                        nc.gpsimd.tensor_tensor(tmp[r.par][:, 0, :], tmp[r.par][:, 1, :], MHALF,
                                                ALU.pow).then_inc(rstd, 1)

                    def rstd_out(r):
                        tt, n = tmp[r.par], [0]
                        pool.wait_ge(aggr3, C * (r.b + 1))
                        wait(pool, u3, 1, r.b - 1)

                        def op(o, a, b_, f):
                            nc.gpsimd.tensor_tensor(o, a, b_, f).then_inc(chain3, 1)
                            n[0] += 1
                            pool.wait_ge(chain3, 6 * r.b + n[0])
                        op(tt[:, 3, :], mv3[r.par][:, :, 1], EPS1, ALU.add)
                        op(tt[:, 2, :], tt[:, 3, :], MHALF, ALU.pow)
                        op(tt[:, 4, :], mv3[r.par][:, :, 1], tt[:, 2, :], ALU.mult)
                        op(tt[:, 5, :], tt[:, 4, :], tt[:, 2, :], ALU.mult)
                        op(tt[:, 6, :], tt[:, 5, :], EPS1, ALU.add)
                        op(tt[:, 3, :], tt[:, 6, :], MHALF, ALU.pow)
                        nc.gpsimd.tensor_tensor(tt[:, 7, :], tt[:, 3, :], tt[:, 2, :], ALU.mult).then_inc(rstd3, 1)

                    wide = [128, C, D]

                    def normalise(r):
                        wait(pool, u2T_mm, 1, r.b - 1)
                        apart(pool, rstd, r.b + 1, pool_passed)
                        nc.gpsimd.tensor_tensor(U2[r.par][:, :, :], X[:, ds(C * r.b, C), :],
                                                mv[r.par][:, :, 0:1].broadcast_to(wide), ALU.subtract).then_inc(diff, 1)
                        pool.wait_ge(diff, r.b + 1)
                        nc.gpsimd.tensor_tensor(U2[r.par][:, :, :], U2[r.par][:, :, :],
                                                tmp[r.par][:, 0, :][:, :, None].broadcast_to(wide),
                                                ALU.mult).then_inc(u2, 1)

                    def ffn_inputs(r):
                        placing.wait_free(pool, r)
                        wait(pool, u3T_mm, 1, r.b - 1)
                        wait(pool, base, 1, r.b - 1)
                        apart(pool, rstd3, r.b + 1, pool_passed)
                        nc.gpsimd.tensor_tensor(U3[r.par][:, :, :], X[:, ds(C * r.b, C), :],
                                                mv3[r.par][:, :, 0:1].broadcast_to(wide), ALU.subtract).then_inc(diff3, 1)
                        pool.wait_ge(diff3, 2 * r.b + 1)
                        nc.gpsimd.tensor_tensor(placing.XS[r.par][:, :, 0:D], U3[r.par][:, :, :],
                                                tmp[r.par][:, 7, :][:, :, None].broadcast_to(wide),
                                                ALU.mult).then_inc(diff3, 1)
                        pool.wait_ge(diff3, 2 * r.b + 2)
                        nc.gpsimd.tensor_tensor(U3[r.par][:, :, :], U3[r.par][:, :, :],
                                                tmp[r.par][:, 2, :][:, :, None].broadcast_to(wide),
                                                ALU.mult).then_inc(u3, 1)

                    def parts(r, full, hi, lo, ready, stacked, per, first, done):
                        wait(pool, stacked, 16 * per, r.b - 1)
                        apart(pool, ready, r.b + 1, pool_passed)
                        nc.gpsimd.tensor_copy(hi[:, :], full[:, :]).then_inc(first, 1)
                        pool.wait_ge(first, r.b + 1)
                        nc.gpsimd.tensor_tensor(lo[:, :], full[:, :], hi[:, :].bitcast(F32),
                                                ALU.subtract).then_inc(done, 1)

                    def step(t):
                        for k in range(SLOTS):
                            if k == 2 and (t + -1).within(B):
                                r = t + -1
                                pool.wait_ge(otr_v, SETS * (r.b + 1))
                                wait(pool, att_mm, 1, r.b - 1)
                                nc.gpsimd.tensor_tensor(ATB[r.par][:, :, :], AT[r.par][:, :, :],
                                                        BVB[:, None, :].broadcast_to([128, C, D]),
                                                        ALU.add).then_inc(atb, 1)
                            if k == 1 and (t + 1).within(B):
                                parts(t + 1, QF, QHI, QLO, qf, q_stack, 3, q_hi, q_parts)
                            if k == 3 and (t + 1).within(B):
                                parts(t + 1, KF, KHI, KLO, kf, k_stack, 3 * G, k_hi, k_parts)
                            if k == 7 and (t + 2).within(B):
                                rstd_in(t + 2)
                            if k == 10 and (t + 2).within(B):
                                normalise(t + 2)
                            if k == 5 and (t + -2).within(B):
                                placing.send(pool, t + -2)
                            if k == 7 and (t + -2).within(B):
                                placing.release(pool, t + -2)
                            if k == 8 and (t + -1).within(B):
                                rstd_out(t + -1)
                                ffn_inputs(t + -1)
                            if k == 12 and (t + 2).within(B):
                                r = t + 2
                                xb = X[:, ds(C * r.b, C), :]
                                apart(pool, u2, r.b + 1, pool_passed)
                                nc.gpsimd.tensor_tensor(xb, xb, BOB[:, None, :].broadcast_to([128, C, D]),
                                                        ALU.add).then_inc(xbo, 1)
                            if k == 13 and (t + -1).within(B):
                                r = t + -1
                                xb = X[:, ds(C * r.b, C), :]
                                apart(pool, u3, r.b + 1, pool_passed)
                                nc.gpsimd.tensor_tensor(xb, xb, U3[r.par][:, :, :], ALU.add).then_inc(base, 1)
                    placing.start(pool)
                    rounds(pool, FIRST, LO, HI, END, step)
    
                @block.vector
                def _(dve):
                    def xs(r, c_):
                        return X[:, ds(C * r.b + c_, 1), :].rearrange("p o d -> p (o d)")

                    def between(t, k, c_):
                        r = t + 2
                        if k == 4 and r.within(B):
                            dve.wait_ge(y_here, 16 * (r.b + 1))
                            nc.vector.scalar_tensor_tensor(xs(r, c_), GA[r.par][:, c_, :],
                                                           ALPHA[:, ds(C * r.b + c_, 1)], xs(r, c_),
                                                           ALU.mult, ALU.add).then_inc(x2, 1)
                        if k == 5 and r.within(B):
                            apart(dve, x2, C * r.b + c_ + 1, dve_passed)
                            nc.vector.bn_stats(st[r.par][:, c_, :], xs(r, c_)).then_inc(stats, 1)
                        if k == 6 and r.within(B):
                            if c_ == 0:
                                at_least(dve, u2, r.b - 1)
                            apart(dve, stats, C * r.b + c_ + 1, dve_passed)
                            nc.vector.bn_aggr(mv[r.par][:, c_, :], st[r.par][:, c_, :]).then_inc(aggr, 1)
                        r = t + -1
                        if k == 7 and r.within(B):
                            apart(dve, x3, r.b + 1, dve_passed)
                            nc.vector.bn_stats(st3[r.par][:, c_, :], xs(r, c_)).then_inc(stats3, 1)
                        if k == 8 and r.within(B):
                            if c_ == 0:
                                at_least(dve, rstd3, r.b)
                            apart(dve, stats3, C * r.b + c_ + 1, dve_passed)
                            nc.vector.bn_aggr(mv3[r.par][:, c_, :], st3[r.par][:, c_, :]).then_inc(aggr3, 1)

                    def step(t):
                        for k in range(SLOTS):
                            if k == 0 and (t + -2).within(B):
                                placing.place(dve, t + -2, RANKS)
                            r, s = m_slot(t, k)
                            for g in range(G):
                                if r.within(B):
                                    n = SLOTS * G * r.b + C * G * s + G * (k % C) + g
                                    dve.wait_ge(mx_mm, n + 1)
                                    nc.vector.tensor_reduce(NM[r.par][:, s, k % C, g:g + 1], bank[4 + g % 2],
                                                            axis=AX.X, op=ALU.max, negate=True).then_inc(mx, 1)
                                between(t, k, g)
                            if k in (13, 14) and (t + -1).within(B):
                                placing.choose(dve, t + -1, (0, 1) if k == 13 else (2, 3, 4), affv)
                            for what, r, s in uses(t, k):
                                if what == "otr":
                                    n = SETS * r.b + s
                                    rows = MQ.rearrange("p c (g a) -> p c g a", g=G)
                                    dve.wait_ge(otr_mm, n + 1)
                                    nc.vector.reciprocal(RC[s % 2][:, :, :], rows[:, :, :, HD]).then_inc(rc, 1)
                                    dve.wait_ge(rc, n + 1)
                                    if s == 0:
                                        wait(dve, atb, 1, r.b - 1)
                                    nc.vector.tensor_tensor(
                                        AT[r.par][:, :, 32 * s:32 * s + 32].rearrange("p c (g d) -> p c g d", g=G),
                                        rows[:, :, :, 0:HD], RC[s % 2][:, :, :, None].broadcast_to([128, C, G, HD]),
                                        ALU.mult).then_inc(otr_v, 1)
                                if what == "wo":
                                    dve.wait_ge(o_mm, r.b + 1)
                                    dve.wait_ge(xbo, r.b + 1)
                                    nc.vector.tensor_tensor(X[:, ds(C * r.b, C), :], MQ, X[:, ds(C * r.b, C), :],
                                                            ALU.add).then_inc(x3, 1)
                                if what == "aff":
                                    dve.wait_ge(aff_mm, r.b + 1)
                                    wait(dve, placing.kept, 1, r.b - 1)
                                    nc.vector.tensor_copy(placing.AFFB[:, :, :],
                                                          MISC[:, 0:C * E].rearrange("p (c e) -> p c e", c=C)
                                                          ).then_inc(affv, 1)

                    rounds(dve, FIRST, LO, HI, END, step)

                @block.scalar
                def _(act):
                    def step(t):
                        for k in range(SLOTS):
                            if t.within(B):
                                r = t
                                for j in range(2):
                                    act.wait_ge(s_mm, 2 * SLOTS * r.b + 2 * k + j + 1)
                                    at_least(act, av, SLOTS * r.b + k - 1)
                                    nc.scalar.activation(P[k % 2][:, 2 * j:2 * j + 2, :], PS[:, 2 * j:2 * j + 2, :],
                                                         ACT.Exp, scale=SCALE).then_inc(exps, 1)
                            if k == 13 and (t + -1).within(B):
                                placing.number(act, t + -1)
                                placing.keep(act, t + -1, affv)
                            for what, r, s in uses(t, k):
                                if what == "u2T":
                                    act.wait_ge(u2T_mm, r.b + 1)
                                    wait(act, v_mm, 1, r.b - 1)
                                    nc.scalar.copy(U2T[r.par][:, :], MISC).then_inc(u2Tv, 1)
                                if what == "mt":
                                    act.wait_ge(mt_mm, SETS * r.b + s + 1)
                                    at_least(act, s_mm, 2 * (SLOTS * (r.b - 2) + C * (s + 1)))
                                    nc.scalar.copy(QS[r.par][PARTS:STACK, s, :],
                                                   MISC[PARTS:STACK, :]).then_inc(mt_v, 1)
                                if what == "q":
                                    act.wait_ge(q_mm, r.b + 1)
                                    wait(act, q_parts, 1, r.b - 1)
                                    nc.scalar.activation(QF[:, :], MISC, ACT.Identity, bias=BQB).then_inc(qf, 1)
                                if what == "k":
                                    act.wait_ge(k_mm, r.b + 1)
                                    wait(act, k_parts, 1, r.b - 1)
                                    nc.scalar.activation(KF[:, :], MISC, ACT.Identity, bias=BKB).then_inc(kf, 1)
                                if what == "v":
                                    act.wait_ge(v_mm, r.b + 1)
                                    at_least(act, av, SLOTS * (r.b - 1))
                                    nc.scalar.copy(VA[r.par][:, :, :, 0:HD],
                                                   MQ.rearrange("p c (h d) -> p c h d", h=H)).then_inc(vv, 1)
                                if what == "att":
                                    act.wait_ge(att_mm, r.b + 1)
                                    wait(act, o_mm, 1, r.b - 1)
                                    nc.scalar.copy(ATT[r.par][:, :], MISC).then_inc(att_v, 1)
                                if what == "u3T":
                                    act.wait_ge(u3T_mm, r.b + 1)
                                    wait(act, aff_mm, 1, r.b - 1)
                                    nc.scalar.copy(U3T[r.par][:, :], MISC).then_inc(u3Tv, 1)
                            if k % C == 0:
                                r, s = (t, k // C - 1) if k else (t + -1, SETS - 1)
                                if r.within(B):
                                    n = SETS * r.b + s
                                    act.wait_ge(av, SLOTS * r.b + C * (s + 1))
                                    at_least(act, otr_mm, n - 1)
                                    nc.scalar.copy(OSB[s % 2][:, :], O).then_inc(o_v, 1)
                    rounds(act, FIRST, LO, HI, END, step)

                @block.tensor
                def _(pe):

                    def products(r, k):
                        s, c_ = k // C, k % C
                        if c_ == 0:
                            at_least(pe, o_v, SETS * r.b + s)
                            if k == 0:
                                pe.wait_ge(vv, r.b + 1)
                        pe.wait_ge(exps, 2 * (SLOTS * r.b + k + 1))
                        for g in range(G):
                            i = nc.tensor.matmul(O[32 * g:32 * g + 32, :], VA[r.par][:, c_, G * s + g, :],
                                                 P[k % 2][:, g, :], start=(c_ == 0), stop=(c_ == C - 1))
                        i.then_inc(av, 1)

                    def scores(t, k, j):
                        if not t.within(B):
                            return
                        s, c_ = k // C, k % C
                        if c_ == 0 and j == 0:
                            pe.wait_ge(mt_v, SETS * t.b + s + 1)
                        at_least(pe, exps, 2 * (SLOTS * t.b + k) + j - 1)
                        for g in (2 * j, 2 * j + 1):
                            i = nc.tensor.matmul(bank[g], KS[t.par][0:STACK, s, g, 128 * c_:128 * c_ + 128],
                                                 QS[t.par][0:STACK, s, :], start=True, stop=True)
                        i.then_inc(s_mm, 1)

                    def rowwise(t, k, g):
                        r, s = m_slot(t, k)
                        if not r.within(B):
                            return
                        if k == SLOTS // 2 and g == 0:
                            pe.wait_ge(q_stack, 16 * 3 * (r.b + 1))
                            pe.wait_ge(k_stack, 16 * 3 * G * (r.b + 1))
                        at_least(pe, mx, SLOTS * G * r.b + C * G * s + G * (k % C) + g - 1)
                        qt = 128 * (k % C)
                        nc.tensor.matmul(bank[4 + g % 2], QS[r.par][0:PARTS, s, qt:qt + 128],
                                         KS[r.par][0:PARTS, s, g, :], start=True, stop=True).then_inc(mx_mm, 1)

                    def spare(t, k):
                        for use, (slot, what, ahead, s) in enumerate(misc):
                            r = t + ahead
                            if slot != k or not r.within(B):
                                continue
                            misc_free(pe, t, use)
                            if what == "rank":
                                placing.rank(pe, r, RANKS)
                            if what == "u2T":
                                pe.wait_ge(u2, r.b + 1)
                                for c_ in range(C):
                                    i = nc.tensor.transpose(MQ[:, c_, :], U2[r.par][:, c_, :], ID)
                                i.then_inc(u2T_mm, 1)
                            if what == "otr":
                                n = SETS * r.b + s
                                pe.wait_ge(o_v, n + 1)
                                for c_ in range(C):
                                    i = nc.tensor.transpose(MQ[:, c_, :], OSB[s % 2][:, 128 * c_:128 * c_ + 128], ID)
                                i.then_inc(otr_mm, 1)
                            if what == "mt":
                                pe.wait_ge(mx, SLOTS * G * r.b + C * G * (s + 1))
                                for c_ in range(C):
                                    i = nc.tensor.matmul(MQ[PARTS:STACK, c_, :], NM[r.par][:, s, c_, :], ID,
                                                         start=True, stop=True)
                                i.then_inc(mt_mm, 1)
                            if what in ("q", "k"):
                                pe.wait_ge(u2Tv, r.b + 1)
                                nc.tensor.matmul(MISC, WB[:, 0 if what == "q" else 1, :], U2T[r.par][:, :],
                                                 start=True, stop=True).then_inc(q_mm if what == "q" else k_mm, 1)
                            if what == "v":
                                for c_ in range(C):
                                    i = nc.tensor.matmul(MQ[:, c_, :], U2T[r.par][:, 128 * c_:128 * c_ + 128],
                                                         WB[:, 2, :], start=True, stop=True)
                                i.then_inc(v_mm, 1)
                            if what == "att":
                                pe.wait_ge(atb, r.b + 1)
                                for c_ in range(C):
                                    i = nc.tensor.transpose(MQ[:, c_, :], ATB[r.par][:, c_, :], ID)
                                i.then_inc(att_mm, 1)
                            if what == "wo":
                                pe.wait_ge(att_v, r.b + 1)
                                for c_ in range(C):
                                    i = nc.tensor.matmul(MQ[:, c_, :], ATT[r.par][:, 128 * c_:128 * c_ + 128],
                                                         WB[:, 3, :], start=True, stop=True)
                                i.then_inc(o_mm, 1)
                            if what == "u3T":
                                pe.wait_ge(u3, r.b + 1)
                                for c_ in range(C):
                                    i = nc.tensor.transpose(MQ[:, c_, :], U3[r.par][:, c_, :], ID)
                                i.then_inc(u3T_mm, 1)
                            if what == "aff":
                                pe.wait_ge(u3Tv, r.b + 1)
                                for c_ in range(C):
                                    i = nc.tensor.matmul(MISC[:, E * c_:E * c_ + E],
                                                         U3T[r.par][:, 128 * c_:128 * c_ + 128], CENT,
                                                         start=True, stop=True)
                                i.then_inc(aff_mm, 1)

                    def step(t):
                        for k in range(SLOTS):
                            scores(t, k, 0)
                            rowwise(t, k, 0)
                            scores(t, k, 1)
                            rowwise(t, k, 1)
                            r, kk = (t, k - 1) if k else (t + -1, SLOTS - 1)
                            if r.within(B):
                                products(r, kk)
                            rowwise(t, k, 2)
                            spare(t, k)
                            rowwise(t, k, 3)
                    rounds(pe, FIRST, LO, HI, END, step)

        def finish():
            with ExitStack() as c:
                Y = sb("z_Y", [128, NT, D], c=c)
                done, stored = sem("z_done"), sem("z_stored")
                y_here = [sem(f"z_y{b}") for b in range(B)]
                block = c.enter_context(nc.Block())

                @block.scalar
                def _(act):
                    for b in range(B):
                        act.dma_start(Y[:, C * b:C * b + C, :], y_tok[S * b:S * b + S, :]
                                      .rearrange("(c p) d -> p c d", p=128)).then_inc(y_here[b], 16)

                @block.vector
                def _(dve):
                    for b in range(B):
                        dve.wait_ge(y_here[b], 16)
                        for j in range(C * b, C * b + C):
                            i = nc.vector.scalar_tensor_tensor(X[:, j, :], Y[:, j, :], ALPHA[:, j:j + 1], X[:, j, :],
                                                               ALU.mult, ALU.add)
                        i.then_inc(done, 1)

                @block.sync
                def _(sp):
                    for b in range(B):
                        sp.wait_ge(done, b + 1)
                        sp.dma_start(out[b].rearrange("(c p) d -> p c d", p=128),
                                     X[:, C * b:C * b + C, :]).then_inc(stored, 16)
                    sp.wait_ge(stored, 16 * B)

        used, held = held, None
        KS = [sb(f"KS{i}", [128, SETS, G, S], F32R) for i in range(2)]
        VA = [sb(f"VA{i}", [128, C, H, AUG]) for i in range(2)]
        route(1, used)
        early.close()
        experts(1)
        attention()
        route(2)
        experts(2)
        finish()


_INS = ['L0_attn_a_x', 'L0_attn_a_Wq', 'L0_attn_a_bq', 'L0_attn_a_Wk', 'L0_attn_a_bk', 'L0_attn_a_Wv',
        'L0_attn_a_bv', 'L0_attn_a_Wo', 'L0_attn_a_bo', 'L0_attn_a_decay_param', 'L0_attn_b_Wq', 'L0_attn_b_bq',
        'L0_attn_b_Wk', 'L0_attn_b_bk', 'L0_attn_b_Wv', 'L0_attn_b_bv', 'L0_attn_b_Wo', 'L0_attn_b_bo',
        'L0_attn_b_head_mask', 'L0_ffn_centroids', 'L0_ffn_ln_g', 'L0_ffn_ln_b', 'L0_ffn_w1', 'L0_ffn_b1',
        'L0_ffn_w2', 'L0_ffn_b2']


def shape_constants(np):
    con = np.zeros((128, 672), np.float32)
    con[:, 0:128] = np.eye(128)
    i = np.arange(128)
    con[:, 128:256] = i[:, None] < i[None, :]
    con[:, 256:385] = np.arange(129)[None, :] == i[:, None] + 1
    con[:, 385] = 1
    con[:, 514:522] = E - np.arange(E)
    con[:, 522:554] = 128 * np.arange(NT)
    con[:, 554:586] = 128 * np.arange(NT) + i[:, None]
    con[:, 586:625] = np.arange(TILES)
    con[:, 625:629] = EPS
    con[:, 629:633] = -0.5
    con[:, 633:641] = CAP * np.arange(E)
    con[:, 641:649] = CAP
    con[:, 649:657] = i[:, None]
    con[:, 657:657 + PADS] = TOKENS + 128 * np.arange(PADS) + i[:, None]
    return con


def kernel(**inputs):
    import numpy as _np
    import concourse.bacc as _bacc
    from concourse import mybir as _mybir
    from concourse.bass_utils import run_bass_kernel_spmd as _run

    nc = _bacc.Bacc("TRN2", target_bir_lowering=False, num_devices=1)
    arrays, args = {}, []
    con = shape_constants(_np)
    named = [(n, _np.ascontiguousarray(inputs[n]).reshape(_np.shape(inputs[n]) or (1,))) for n in _INS]
    named.append(("consts", con))
    for name, a in named:
        arrays[f"in_{name}"] = a
        args.append(nc.dram_tensor(f"in_{name}", a.shape, _mybir.dt.from_np(a.dtype), kind="ExternalInput").ap())
    out = nc.dram_tensor("out", (B, S, D), F32, kind="ExternalOutput").ap()
    hybrid(nc, *args, out)
    r = _run(nc, [arrays], core_ids=[0])
    return r.results[0]["out"]
```
